# Optimizing a Trainium2 kernel written in Bass

```python
import numpy as np
import jax
import jax.numpy as jnp

def _softmax(x, axis=-1):
    return jax.nn.softmax(x, axis=axis)

def _gelu(x):
    return jax.nn.gelu(x, approximate=True)

def _silu(x):
    return jax.nn.silu(x)

def _sigmoid(x):
    return jax.nn.sigmoid(x)

def _layernorm(x, axis=-1, eps=1e-05):
    m = jnp.mean(x, axis=axis, keepdims=True)
    v = jnp.var(x, axis=axis, keepdims=True)
    return (x - m) / jnp.sqrt(v + eps)

def _scatter_add(tgt, idx, src, axis=0):
    return tgt.at[idx].add(src)

def _segment_sum(src, seg, n):
    return jax.ops.segment_sum(src, seg, n)
kernel_name = 'mk_seq_preln_d1_jaxref_r4_ef8656'

def setup_inputs(seed: int=0):
    np.random.seed(seed)
    _w = jnp.asarray

    def _L0_attn_setup():
        import jax, jax.numpy as jnp
        import numpy as np
        D_MODEL = 512
        D_INNER = 1024
        D_XB = 256
        D_STATE = 64
        HEADDIM = 64
        NHEADS = D_INNER // HEADDIM
        NXB = D_XB // HEADDIM
        D_CONV = 4
        CHUNK = 128
        EPS = 1e-05
        D_FF = 2048
        CONV_DIM = D_XB + D_XB + D_INNER
        D_IN_PROJ = D_INNER + D_XB + D_XB + D_INNER + NHEADS

        def rmsnorm(x, w, eps=EPS):
            return x * jax.lax.rsqrt(jnp.mean(x * x, axis=-1, keepdims=True) + eps) * w

        def causal_depthwise_conv(x, w, b):
            k = w.shape[1]
            xp = jnp.pad(x, ((0, 0), (k - 1, 0), (0, 0)))
            out = jax.lax.conv_general_dilated(xp.transpose(0, 2, 1), w[:, None, :], (1,), 'VALID', feature_group_count=x.shape[-1])
            return out.transpose(0, 2, 1) + b

        def ssd_chunked(xdt, dA, Bm, Cm):
            b, l, h, p = xdt.shape
            n = Bm.shape[-1]
            c, q = (l // CHUNK, CHUNK)
            xdt = xdt.reshape(b, c, q, h, p)
            Bm = Bm.reshape(b, c, q, h, n)
            Cm = Cm.reshape(b, c, q, h, n)
            dA = dA.reshape(b, c, q, h).transpose(0, 3, 1, 2)
            dAc = jnp.cumsum(dA, axis=-1)
            seg = dAc[..., :, None] - dAc[..., None, :]
            mask = jnp.tril(jnp.ones((q, q), bool))
            Lm = jnp.where(mask, jnp.exp(seg), 0.0)
            Y_diag = jnp.einsum('bcqhn,bcshn,bhcqs,bcshp->bcqhp', Cm, Bm, Lm, xdt)
            decay_states = jnp.exp(dAc[..., -1:] - dAc)
            states = jnp.einsum('bcqhn,bhcq,bcqhp->bchpn', Bm, decay_states, xdt)
            chunk_decay = jnp.exp(dAc[..., -1])

            def step(carry, inp):
                s, d = inp
                new = s + d[:, :, None, None] * carry
                return (new, carry)
            init = jnp.zeros((b, h, p, n), xdt.dtype)
            _, prevs = jax.lax.scan(step, init, (states.transpose(1, 0, 2, 3, 4), chunk_decay.transpose(2, 0, 1)))
            Y_off = jnp.einsum('bcqhn,cbhpn,bhcq->bcqhp', Cm, prevs, jnp.exp(dAc))
            return (Y_diag + Y_off).reshape(b, l, h, p)

        def mamba2(x, in_proj_w, conv_w, conv_b, dt_bias, A_log, Dp, norm_w, out_proj_w):
            b, l, _ = x.shape
            zxbcdt = x @ in_proj_w
            z, xb, Bc, Cc, dt = jnp.split(zxbcdt, [D_INNER, D_INNER + D_XB, D_INNER + 2 * D_XB, 2 * D_INNER + 2 * D_XB], axis=-1)
            xBC = jax.nn.silu(causal_depthwise_conv(jnp.concatenate([xb, Bc, Cc], -1), conv_w, conv_b))
            xb, Bc, Cc = jnp.split(xBC, [D_XB, 2 * D_XB], axis=-1)
            dt = jax.nn.softplus(dt + dt_bias)
            A = -jnp.exp(A_log)
            rep = NHEADS // NXB
            x_h = jnp.repeat(xb.reshape(b, l, NXB, HEADDIM), rep, axis=2)
            B_h = jnp.repeat(Bc.reshape(b, l, NXB, D_STATE), rep, axis=2)
            C_h = Cc.reshape(b, l, NHEADS, D_STATE)
            y = ssd_chunked(x_h * dt[..., None], dt * A, B_h, C_h)
            y = y + Dp[None, None, :, None] * x_h
            y = y.reshape(b, l, D_INNER)
            y = rmsnorm(y * jax.nn.silu(z), norm_w)
            return y @ out_proj_w
        key = jax.random.key(seed)
        ks = jax.random.split(key, 8)
        s = 0.02
        return {'hidden_states': jax.random.normal(ks[0], (2, 512, D_MODEL), jnp.float32), 'in_proj_w': jax.random.normal(ks[1], (D_MODEL, D_IN_PROJ), jnp.float32) * s, 'conv_w': jax.random.normal(ks[2], (CONV_DIM, D_CONV), jnp.float32) * 0.1, 'conv_b': jnp.zeros((CONV_DIM,), jnp.float32), 'dt_bias': jnp.log(jnp.expm1(jnp.linspace(0.001, 0.1, NHEADS, dtype=jnp.float32))), 'A_log': jnp.log(jnp.linspace(1.0, 16.0, NHEADS, dtype=jnp.float32)), 'D': jnp.ones((NHEADS,), jnp.float32), 'norm_w': jnp.ones((D_INNER,), jnp.float32), 'out_proj_w': jax.random.normal(ks[3], (D_INNER, D_MODEL), jnp.float32) * s, 'ln1_w': jnp.ones((D_MODEL,), jnp.float32), 'ln2_w': jnp.ones((D_MODEL,), jnp.float32), 'gate_w': jax.random.normal(ks[4], (D_MODEL, D_FF), jnp.float32) * s, 'up_w': jax.random.normal(ks[5], (D_MODEL, D_FF), jnp.float32) * s, 'down_w': jax.random.normal(ks[6], (D_FF, D_MODEL), jnp.float32) * s}
    _L0_attn_in = _L0_attn_setup()

    def _L0_ffn_setup():
        import jax, jax.numpy as jnp
        import numpy as np
        H = 512
        I = 352
        E = 8
        K = 2
        B, S = (2, 512)
        key = jax.random.key(seed)
        k0, k1, k2, k3, k4 = jax.random.split(key, 5)
        scale = 1.0 / np.sqrt(H)
        x = jax.random.normal(k0, (B, S, H), dtype=jnp.float32)
        Wr = jax.random.normal(k1, (H, E), dtype=jnp.float32) * scale
        Wg = jax.random.normal(k2, (E, H, I), dtype=jnp.float32) * scale
        Wu = jax.random.normal(k3, (E, H, I), dtype=jnp.float32) * scale
        Wd = jax.random.normal(k4, (E, I, H), dtype=jnp.float32) * (1.0 / np.sqrt(I))
        return {'x': x, 'Wr': Wr, 'Wg': Wg, 'Wu': Wu, 'Wd': Wd}
    _L0_ffn_in = _L0_ffn_setup()
    _d = {'L0_attn_hidden_states': _L0_attn_in['hidden_states'], 'L0_attn_in_proj_w': _L0_attn_in['in_proj_w'], 'L0_attn_conv_w': _L0_attn_in['conv_w'], 'L0_attn_conv_b': _L0_attn_in['conv_b'], 'L0_attn_dt_bias': _L0_attn_in['dt_bias'], 'L0_attn_A_log': _L0_attn_in['A_log'], 'L0_attn_D': _L0_attn_in['D'], 'L0_attn_norm_w': _L0_attn_in['norm_w'], 'L0_attn_out_proj_w': _L0_attn_in['out_proj_w'], 'L0_attn_ln1_w': _L0_attn_in['ln1_w'], 'L0_attn_ln2_w': _L0_attn_in['ln2_w'], 'L0_attn_gate_w': _L0_attn_in['gate_w'], 'L0_attn_up_w': _L0_attn_in['up_w'], 'L0_attn_down_w': _L0_attn_in['down_w'], 'L0_ffn_Wr': _L0_ffn_in['Wr'], 'L0_ffn_Wg': _L0_ffn_in['Wg'], 'L0_ffn_Wu': _L0_ffn_in['Wu'], 'L0_ffn_Wd': _L0_ffn_in['Wd']}
    _x0 = _d['L0_attn_hidden_states']
    _d['L0_attn_hidden_states'] = jax.random.normal(jax.random.fold_in(jax.random.key(seed), 1), (1, 2048, 512), dtype=_x0.dtype)
    del _x0
    return _d

def reference(L0_attn_hidden_states, L0_attn_in_proj_w, L0_attn_conv_w, L0_attn_conv_b, L0_attn_dt_bias, L0_attn_A_log, L0_attn_D, L0_attn_norm_w, L0_attn_out_proj_w, L0_attn_ln1_w, L0_attn_ln2_w, L0_attn_gate_w, L0_attn_up_w, L0_attn_down_w, L0_ffn_Wr, L0_ffn_Wg, L0_ffn_Wu, L0_ffn_Wd):

    def _L0_attn_ref(hidden_states, in_proj_w, conv_w, conv_b, dt_bias, A_log, D, norm_w, out_proj_w, ln1_w, ln2_w, gate_w, up_w, down_w):
        import jax, jax.numpy as jnp
        import numpy as np
        D_MODEL = 512
        D_INNER = 1024
        D_XB = 256
        D_STATE = 64
        HEADDIM = 64
        NHEADS = D_INNER // HEADDIM
        NXB = D_XB // HEADDIM
        D_CONV = 4
        CHUNK = 128
        EPS = 1e-05
        D_FF = 2048
        CONV_DIM = D_XB + D_XB + D_INNER
        D_IN_PROJ = D_INNER + D_XB + D_XB + D_INNER + NHEADS

        def rmsnorm(x, w, eps=EPS):
            return x * jax.lax.rsqrt(jnp.mean(x * x, axis=-1, keepdims=True) + eps) * w

        def causal_depthwise_conv(x, w, b):
            k = w.shape[1]
            xp = jnp.pad(x, ((0, 0), (k - 1, 0), (0, 0)))
            out = jax.lax.conv_general_dilated(xp.transpose(0, 2, 1), w[:, None, :], (1,), 'VALID', feature_group_count=x.shape[-1])
            return out.transpose(0, 2, 1) + b

        def ssd_chunked(xdt, dA, Bm, Cm):
            b, l, h, p = xdt.shape
            n = Bm.shape[-1]
            c, q = (l // CHUNK, CHUNK)
            xdt = xdt.reshape(b, c, q, h, p)
            Bm = Bm.reshape(b, c, q, h, n)
            Cm = Cm.reshape(b, c, q, h, n)
            dA = dA.reshape(b, c, q, h).transpose(0, 3, 1, 2)
            dAc = jnp.cumsum(dA, axis=-1)
            seg = dAc[..., :, None] - dAc[..., None, :]
            mask = jnp.tril(jnp.ones((q, q), bool))
            Lm = jnp.where(mask, jnp.exp(seg), 0.0)
            Y_diag = jnp.einsum('bcqhn,bcshn,bhcqs,bcshp->bcqhp', Cm, Bm, Lm, xdt)
            decay_states = jnp.exp(dAc[..., -1:] - dAc)
            states = jnp.einsum('bcqhn,bhcq,bcqhp->bchpn', Bm, decay_states, xdt)
            chunk_decay = jnp.exp(dAc[..., -1])

            def step(carry, inp):
                s, d = inp
                new = s + d[:, :, None, None] * carry
                return (new, carry)
            init = jnp.zeros((b, h, p, n), xdt.dtype)
            _, prevs = jax.lax.scan(step, init, (states.transpose(1, 0, 2, 3, 4), chunk_decay.transpose(2, 0, 1)))
            Y_off = jnp.einsum('bcqhn,cbhpn,bhcq->bcqhp', Cm, prevs, jnp.exp(dAc))
            return (Y_diag + Y_off).reshape(b, l, h, p)

        def mamba2(x, in_proj_w, conv_w, conv_b, dt_bias, A_log, Dp, norm_w, out_proj_w):
            b, l, _ = x.shape
            zxbcdt = x @ in_proj_w
            z, xb, Bc, Cc, dt = jnp.split(zxbcdt, [D_INNER, D_INNER + D_XB, D_INNER + 2 * D_XB, 2 * D_INNER + 2 * D_XB], axis=-1)
            xBC = jax.nn.silu(causal_depthwise_conv(jnp.concatenate([xb, Bc, Cc], -1), conv_w, conv_b))
            xb, Bc, Cc = jnp.split(xBC, [D_XB, 2 * D_XB], axis=-1)
            dt = jax.nn.softplus(dt + dt_bias)
            A = -jnp.exp(A_log)
            rep = NHEADS // NXB
            x_h = jnp.repeat(xb.reshape(b, l, NXB, HEADDIM), rep, axis=2)
            B_h = jnp.repeat(Bc.reshape(b, l, NXB, D_STATE), rep, axis=2)
            C_h = Cc.reshape(b, l, NHEADS, D_STATE)
            y = ssd_chunked(x_h * dt[..., None], dt * A, B_h, C_h)
            y = y + Dp[None, None, :, None] * x_h
            y = y.reshape(b, l, D_INNER)
            y = rmsnorm(y * jax.nn.silu(z), norm_w)
            return y @ out_proj_w
        residual = hidden_states
        h = rmsnorm(hidden_states, ln1_w)
        h = residual + mamba2(h, in_proj_w, conv_w, conv_b, dt_bias, A_log, D, norm_w, out_proj_w)
        residual = h
        h2 = rmsnorm(h, ln2_w)
        mlp = jax.nn.silu(h2 @ gate_w) * (h2 @ up_w) @ down_w
        return residual + mlp

    def _L0_ffn_ref(x, Wr, Wg, Wu, Wd):
        import jax, jax.numpy as jnp
        import numpy as np
        H = 512
        I = 352
        E = 8
        K = 2
        B, S = (2, 512)
        router_logits = jnp.einsum('bsh,he->bse', x, Wr)
        probs = jax.nn.softmax(router_logits.astype(jnp.float32), axis=-1)
        topk_w, topk_idx = jax.lax.top_k(probs, K)
        topk_w = topk_w / jnp.sum(topk_w, axis=-1, keepdims=True)
        onehot = jax.nn.one_hot(topk_idx, E, dtype=topk_w.dtype)
        combine = jnp.einsum('bsk,bske->bse', topk_w, onehot)
        g = jnp.einsum('bsh,ehi->besi', x, Wg)
        u = jnp.einsum('bsh,ehi->besi', x, Wu)
        h = jax.nn.silu(g) * u
        y = jnp.einsum('besi,eih->besh', h, Wd)
        out = jnp.einsum('bse,besh->bsh', combine.astype(x.dtype), y)
        return out
    x = L0_attn_hidden_states
    x = x + _L0_attn_ref(_layernorm(x, axis=-1), L0_attn_in_proj_w, L0_attn_conv_w, L0_attn_conv_b, L0_attn_dt_bias, L0_attn_A_log, L0_attn_D, L0_attn_norm_w, L0_attn_out_proj_w, L0_attn_ln1_w, L0_attn_ln2_w, L0_attn_gate_w, L0_attn_up_w, L0_attn_down_w)
    x = x + _L0_ffn_ref(_layernorm(x, axis=-1), L0_ffn_Wr, L0_ffn_Wg, L0_ffn_Wu, L0_ffn_Wd)
    return x

_drawn_inputs = setup_inputs


def setup_inputs(seed=0):
    import zlib

    import numpy as np

    out = dict(_drawn_inputs(seed))
    spreads = {'L0_attn_conv_b': (0.0, 0.1),
     'L0_attn_D': (1.0, 0.2),
     'L0_attn_norm_w': (1.0, 0.2),
     'L0_attn_ln1_w': (1.0, 0.2),
     'L0_attn_ln2_w': (1.0, 0.6)}
    factors = {'L0_attn_dt_bias': 8.0, 'L0_attn_A_log': 8.0}
    for name, (base, spread) in spreads.items():
        noise = np.random.default_rng([zlib.crc32(name.encode()), seed]).standard_normal(out[name].shape)
        drawn = base * np.exp(spread * noise) if base else spread * noise
        out[name] = jnp.asarray(drawn.astype(out[name].dtype))
    for name, factor in factors.items():
        out[name] = (out[name] * factor).astype(out[name].dtype)
    return out
```

```python
from contextlib import ExitStack

import concourse.bass as bass
from concourse import mybir

F32 = mybir.dt.float32
F32R = mybir.dt.float32r
U32 = mybir.dt.uint32
ALU = mybir.AluOpType
ACT = mybir.ActivationFunctionType
AX_X = mybir.AxisListType.X

P = 128
EPS = 1e-5
ROWS = 2048
D = 512
KD = D // P
DI = 1024
HEADS, HD, DST, NG = 16, 64, 64, 4
HPG = HEADS // NG
DXB = NG * HD
NCH = (2 * DXB + DI) // P
TAPS = 4
DIN = DI + 2 * DXB + DI + HEADS
CH0 = DI
DT0 = DIN - HEADS
TILES = ROWS // P
GR = 256
NGRP = ROWS // GR
FF, FB = 2048, 256
E, EI = 8, 352
MASKED = -1.0e30
SORT_TILES = 2 * ROWS // P + E - 1
IC = [(i, min(P, EI - i)) for i in range(0, EI, P)]


def softplus_dt_steps():
    return [1.0 / n for n in (13, 11, 9, 7, 5, 3)]


def mixer(nc, ins, dr, ident, ones):
    x_d = ins["L0_attn_hidden_states"].rearrange("b s d -> (b s) d")
    with ExitStack() as ctx:
        def sb(name, shape, dt=F32):
            return ctx.enter_context(nc.sbuf_tensor(name, shape, dt))

        def sem(name):
            return ctx.enter_context(nc.semaphore(name))

        w_in = sb("w_in", [P, KD, DIN])
        w_out = sb("w_out", [P, DI // P, D])
        ln1 = sb("ln1", [P, KD])
        ln2_row = sb("ln2_row", [P, D])
        normw = sb("normw", [P, DI // P])
        conv_w = sb("conv_w", [P, NCH, TAPS])
        conv_b = sb("conv_b", [P, NCH])
        a_neg = sb("a_neg", [P, HEADS])
        dt_bias = sb("dt_bias", [P, HEADS])
        d_skip = sb("d_skip", [P, HEADS])
        tri = sb("tri", [P, P])
        suffix = sb("suffix", [P, P])
        mask = sb("mask", [P, P])
        tri_r = sb("tri_r", [P, P], F32R)
        ident_r = sb("ident_r", [P, P], F32R)
        mask_r = sb("mask_r", [P, P], F32R)
        half_neg = sb("half_neg", [P, 1])
        xin = sb("xin", [P, 2, D])
        bn = sb("bn", [P, 2, 6])
        mv = sb("mv", [P, 2, 2, 2])
        lnq = sb("lnq", [P, 2, 2, 4])
        hT = [sb(f"hT{i}", [P, KD, GR]) for i in range(2)]
        raw = sb("raw", [P, NCH, TAPS - 1 + GR])
        acc = [sb(f"acc{i}", [P, GR]) for i in range(3)]
        tnh = [sb(f"tnh{i}", [P, GR]) for i in range(2)]
        cv = [sb(f"cv{i}", [P, NCH, GR]) for i in range(2)]
        sp = sb("sp", [P, 8, 2 * HEADS])
        dt = [sb(f"dt{i}", [P, 2, HEADS]) for i in range(2)]
        da = sb("da", [P, 2, HEADS])
        da_hi = [sb(f"da_hi{i}", [P, 2, HEADS], F32R) for i in range(2)]
        da_lo = [sb(f"da_lo{i}", [P, 2, HEADS], F32R) for i in range(2)]
        neg_cum = [sb(f"neg_cum{i}", [P, 2, HEADS]) for i in range(2)]
        exp_cum = [sb(f"exp_cum{i}", [P, 2, HEADS]) for i in range(2)]
        exp_suf = [sb(f"exp_suf{i}", [P, 2, HEADS]) for i in range(2)]
        chunk_decay = [sb(f"chunk_decay{i}", [P, 2, 2, HPG]) for i in range(2)]
        zs = sb("zs", [P, DI])
        xb_row = sb("xb_row", [P, 2, DXB])
        xdt = sb("xdt", [P, DI])
        dx = sb("dx", [P, DI])
        xdd = sb("xdd", [P, DI])
        decay = [sb(f"decay{i}", [P, HPG, P]) for i in range(2)]
        score = [sb(f"score{i}", [P, HPG, P]) for i in range(2)]
        ydiag = sb("ydiag", [P, DI])
        yoff = sb("yoff", [P, HPG * HD])
        yg = sb("yg", [P, DI])
        junk = sb("junk", [P, 2, D])
        sumsq = sb("sumsq", [P, 8])
        carry = sb("carry", [P, 2, HPG, HD])
        yT = sb("yT", [P, DI // P, P])
        xres = sb("xres", [P, D])
        yres = sb("yres", [P, D])
        hres = sb("hres", [P, D])
        xh = sb("xh", [P, D])
        h2 = sb("h2", [P, D])

        bank = [ctx.enter_context(nc.psum_tensor(f"mix_bank{i}", [P, 512], F32)) for i in range(8)]
        proj_ps, seg_ps, y_ps, cb_ps, misc = bank[0:2], bank[2:4], bank[4:6], bank[6], bank[7]

        s = {n: sem(n) for n in (
            "w_dma", "xin_dma", "xres_dma", "stored", "consts", "cast", "a_exp", "folded",
            "bn", "stat", "lnq_step", "normed", "rowT", "hT_done",
            "dt_ps", "dt_v", "dt_neg", "dt_exp", "dt_step", "dt_done", "cum_ps", "cum_done",
            "ch_ps", "halo", "ch_copied", "tap", "ch_tanh", "ch_done",
            "z_ps", "z_tanh", "z_gate", "xb_ps", "xb_row", "xdt", "dx", "xdd",
            "seg0", "seg1", "cb", "exp0", "exp1", "sc0", "sc1", "yd0", "yd1", "yo0", "yo1", "yread0", "yread1",
            "yread_a", "ysum", "ygate", "state_ps", "carry_decayed", "carry_done", "sq", "r_step",
            "yT_ps", "yT_done", "out_ps", "yres", "h_done", "xh_done", "hsq", "h2_step", "passed")}
        seg_s, exp_s, sc_s, yd_s, yread_s = (
            [s[n + "0"], s[n + "1"]] for n in ("seg", "exp", "sc", "yd", "yread"))
        NV = 17
        NW = NV + KD + 1 + 4 * KD
        NLN, NDT, NR, NH2 = 6, 14, 4, 4

        def wait_apart(eng, which, value):
            eng.wait_ge(which, value)
            eng.sem_inc(s["passed"], 1)

        def head_cols(t, g):
            return t[:, g * HPG * HD:(g + 1) * HPG * HD]

        block = ctx.enter_context(nc.Block())


        def slots(run, eng):
            with eng.Fori(0, 3) as it:
                for k in range(4):
                    run(it * 4 + k, k, it * 2 + k // 2 + 1, True, True)
            for k in range(4):
                run(12 + k, k, 7 + k // 2, k < 2, False)

        @block.sync
        def _(eng):
            def load_pre(g, guard):
                if guard:
                    eng.wait_ge(s["rowT"], g * 2)
                for u in range(2):
                    eng.dma_start(xin[:, u, :], x_d[bass.ds((g * 2 + u) * P, P), :]).then_inc(s["xin_dma"], 16)

            load_pre(0, False)
            w = ins["L0_attn_in_proj_w"]
            loads = [(ln1[:, :], ins["L0_attn_ln1_w"].rearrange("(k p) -> p k", p=P)),
                     (normw[:, :], ins["L0_attn_norm_w"].rearrange("(k p) -> p k", p=P)),
                     (a_neg[:, :], ins["L0_attn_A_log"].partition_broadcast(P)),
                     (dt_bias[:, :], ins["L0_attn_dt_bias"].partition_broadcast(P)),
                     (d_skip[:, :], ins["L0_attn_D"].partition_broadcast(P)),
                     (ln2_row[:, :], ins["L0_attn_ln2_w"].partition_broadcast(P))]
            cw = ins["L0_attn_conv_w"]
            cb = ins["L0_attn_conv_b"]
            nb = 2 * DXB // P
            loads += [(conv_w[:, 0:nb, :], cw[0:2 * DXB, :].rearrange("(k p) t -> p k t", p=P)),
                      (conv_b[:, 0:nb], cb[0:2 * DXB].rearrange("(k p) -> p k", p=P))]
            for a in range(2):
                for b in range(2):
                    half, at, src = slice(b * HD, (b + 1) * HD), nb + HPG * a, 2 * DXB + (2 * a + b) * HPG * DST
                    loads += [(conv_w[half, at:at + HPG, :],
                               cw[src:src + HPG * DST, :].rearrange("(j n) t -> n j t", j=HPG)),
                              (conv_b[half, at:at + HPG],
                               cb[src:src + HPG * DST].rearrange("(j n) -> n j", j=HPG))]
            loads += [(w_out[:, :, :], ins["L0_attn_out_proj_w"].rearrange("(k p) n -> p k n", p=P))]
            assert len(loads) == NV
            for dst, src in loads[:-1]:
                with nc.allow_non_contiguous_dma("small vectors"):
                    eng.dma_start(dst, src).then_inc(s["w_dma"], 16)
            wr = w.rearrange("(k p) n -> p k n", p=P)
            c0 = CH0 + 2 * DXB
            for k in range(KD):
                eng.dma_start(w_in[:, k, 0:c0], wr[:, k, 0:c0]).then_inc(s["w_dma"], 16)
            eng.dma_start(w_in[:, :, DT0:DIN], wr[:, :, DT0:DIN]).then_inc(s["w_dma"], 16)
            eng.dma_start(*loads[-1]).then_inc(s["w_dma"], 16)
            for k in range(KD):
                for a in range(2):
                    for b in range(2):
                        lo, src = c0 + a * DI // 2, c0 + (2 * a + b) * HPG * DST
                        eng.dma_start(
                            w_in[:, k, lo:lo + DI // 2].rearrange("p (j b n) -> p j b n", j=HPG, b=2)[:, :, b, :],
                            wr[:, k, src:src + HPG * DST].rearrange("p (j n) -> p j n", j=HPG)
                        ).then_inc(s["w_dma"], 16)
            load_pre(1, True)

            def slot(c, k, gf, front, pre):
                eng.wait_ge(s["xh_done"], c + 1)
                eng.dma_start(xres[:, :], x_d[bass.ds(c * P, P), :]).then_inc(s["xres_dma"], 16)
                if pre and k % 2 == 0:
                    load_pre(gf + 1, True)
                eng.wait_ge(s["xh_done"], c + 2)
                eng.dma_start(dr["xh"][bass.ds(c * P, P), :], xh[:, :]).then_inc(s["stored"], 16)
                eng.wait_ge(s["h2_step"], c * NH2 + NH2 + 1)
                eng.dma_start(dr["h2"][bass.ds(c * P, P), :], h2[:, :]).then_inc(s["stored"], 16)

            slots(slot, eng)
            eng.wait_ge(s["stored"], 16 + 32 * TILES)

        @block.gpsimd
        def _(eng):
            for name, n in (("xh_done", 1), ("stored", 16), ("ch_done", 3), ("h_done", 1), ("sc0", 1), ("sc1", 1),
                            ("exp0", 1), ("exp1", 1), ("yread0", 1), ("yread1", 1), ("yd0", 1), ("yd1", 1),
                            ("xdd", 1),
                            ("ygate", 2), ("yT_ps", 2), ("out_ps", 1), ("state_ps", 1), ("carry_done", 1),
                            ("ysum", 4), ("xdt", 1), ("h2_step", 1)):
                eng.sem_inc(s[name], n)
            eng.memset(tri[:, :], 1.0).then_inc(s["consts"], 1)
            eng.memset(suffix[:, :], 1.0).then_inc(s["consts"], 1)
            eng.memset(mask[:, :], 0.0).then_inc(s["consts"], 1)
            eng.memset(half_neg[:, :], -0.5).then_inc(s["consts"], 1)
            eng.memset(raw[:, :, GR:GR + TAPS - 1], 0.0).then_inc(s["consts"], 1)
            eng.memset(carry[:, :, :, :], 0.0).then_inc(s["consts"], 1)
            eng.wait_ge(s["consts"], 6)
            eng.affine_select(out=tri[:, :], in_=tri[:, :], compare_op=ALU.is_ge, fill=0.0, base=0,
                              pattern=[[1, P]], channel_multiplier=-1).then_inc(s["consts"], 1)
            eng.affine_select(out=suffix[:, :], in_=suffix[:, :], compare_op=ALU.is_gt, fill=0.0, base=0,
                              pattern=[[-1, P]], channel_multiplier=1).then_inc(s["consts"], 1)
            eng.affine_select(out=mask[:, :], in_=mask[:, :], compare_op=ALU.is_ge, fill=MASKED, base=0,
                              pattern=[[1, P]], channel_multiplier=-1).then_inc(s["consts"], 1)

            def pre(g, par, guard):
                for u in range(2):
                    n = (g * 2 + u) * NLN
                    v, q = mv[:, par, u, 1:2], lnq[:, par, u, :]
                    wait_apart(eng, s["stat"], g * 2 + u + 1)
                    steps = [lambda: eng.tensor_scalar(q[:, 0:1], v, EPS, None, ALU.add),
                             lambda: eng.tensor_tensor(q[:, 1:2], q[:, 0:1], half_neg[:, :], ALU.pow),
                             lambda: eng.tensor_tensor(q[:, 0:1], q[:, 1:2], q[:, 1:2], ALU.mult),
                             lambda: eng.tensor_scalar(q[:, 0:1], q[:, 0:1], v, EPS, ALU.mult, ALU.add),
                             lambda: eng.tensor_tensor(q[:, 2:3], q[:, 0:1], half_neg[:, :], ALU.pow),
                             lambda: eng.tensor_tensor(q[:, 3:4], q[:, 1:2], q[:, 2:3], ALU.mult)]
                    for i, step in enumerate(steps):
                        if i:
                            wait_apart(eng, s["lnq_step"], n + i)
                        step().then_inc(s["lnq_step"], 1)

            pre(0, 0, False)
            eng.wait_ge(s["w_dma"], 16 * NW)
            pre(1, 1, False)

            def slot(c, k, gf, front, prev):
                u, par = k % 2, (k // 2) % 2
                hb = lambda t: t.unsqueeze(2).broadcast_to([P, HEADS, HD])
                xr = xb_row[:, 0, :].rearrange("p (g d) -> p g d", g=NG).unsqueeze(2).broadcast_to([P, NG, HPG, HD])
                eng.wait_ge(s["xb_row"], c + 1)
                eng.wait_ge(s["ysum"], c * 4 + 4)
                eng.tensor_tensor(dx[:, :].rearrange("p (g r d) -> p g r d", g=NG, r=HPG), xr,
                                  d_skip[:, :].rearrange("p (g r) -> p g r", g=NG).unsqueeze(3)
                                  .broadcast_to([P, NG, HPG, HD]), ALU.mult).then_inc(s["dx"], 1)
                eng.wait_ge(s["xdt"], c + 2)
                eng.wait_ge(s["cum_done"], gf)
                eng.wait_ge(s["state_ps"], c + 1)
                eng.tensor_tensor(xdd[:, :].rearrange("p (h d) -> p h d", h=HEADS),
                                  xdt[:, :].rearrange("p (h d) -> p h d", h=HEADS),
                                  hb(exp_suf[par][:, u, :]), ALU.mult).then_inc(s["xdd"], 1)
                if prev and k % 2 == 1:
                    pre(gf + 1, par, True)
                eng.wait_ge(s["yd1"], c * 2 + 3)
                eng.wait_ge(s["carry_done"], c + 1)
                eng.tensor_tensor(carry[:, :, :, :].rearrange("p a j d -> p (a j) d"),
                                  carry[:, :, :, :].rearrange("p a j d -> p (a j) d"),
                                  chunk_decay[par][:, u, :, :].rearrange("p a j -> p (a j)").unsqueeze(2)
                                  .broadcast_to([P, 2 * HPG, HD]), ALU.mult).then_inc(s["carry_decayed"], 1)
                n = c * NR
                eng.wait_ge(s["sq"], c * 2 + 2)
                a = sumsq[:, 2:3]
                steps = [lambda: eng.tensor_tensor(a, sumsq[:, 0:1], sumsq[:, 1:2], ALU.add),
                         lambda: eng.tensor_scalar(a, a, 0.25 / DI, EPS, ALU.mult, ALU.add),
                         lambda: eng.tensor_tensor(a, a, half_neg[:, :], ALU.pow),
                         lambda: eng.tensor_scalar(sumsq[:, 3:4], a, 0.5, None, ALU.mult)]
                for i, step in enumerate(steps):
                    if i:
                        wait_apart(eng, s["r_step"], n + i)
                    step().then_inc(s["r_step"], 1)
                eng.wait_ge(s["h_done"], c + 2)
                eng.wait_ge(s["stored"], c * 32 + 16)
                eng.tensor_tensor(xh[:, :], hres[:, :], xres[:, :], ALU.add).then_inc(s["xh_done"], 1)
                n = c * NH2
                wait_apart(eng, s["hsq"], c + 1)
                b = sumsq[:, 5:6]
                steps = [lambda: eng.tensor_scalar(b, sumsq[:, 4:5], 1.0 / D, EPS, ALU.mult, ALU.add),
                         lambda: eng.tensor_tensor(b, b, half_neg[:, :], ALU.pow),
                         lambda: eng.tensor_scalar(h2[:, :], hres[:, :], b, None, ALU.mult),
                         lambda: eng.tensor_tensor(h2[:, :], h2[:, :], ln2_row[:, :], ALU.mult)]
                for i, step in enumerate(steps):
                    if i:
                        wait_apart(eng, s["h2_step"], n + i + 1)
                    step().then_inc(s["h2_step"], 1)

            slots(slot, eng)

        @block.scalar
        def _(eng):
            eng.wait_ge(s["w_dma"], 16 * NW)
            eng.activation(a_neg[:, :], a_neg[:, :], ACT.Exp).then_inc(s["a_exp"], 1)

            def copy_hT(g, par, u):
                eng.wait_ge(s["rowT"], g * 2 + u + 1)
                eng.activation(hT[par][:, :, u * P:(u + 1) * P], misc[:, :].rearrange("p (k n) -> p k n", k=KD),
                               ACT.Copy).then_inc(s["hT_done"], 1)

            def dt_exp(g):
                eng.wait_ge(s["dt_neg"], g + 1)
                eng.activation(sp[:, 2, :], sp[:, 1, :], ACT.Exp).then_inc(s["dt_exp"], 1)

            def cum_exps(g, par):
                eng.wait_ge(s["cum_ps"], g + 1)
                f = lambda t: t[:, :, :].rearrange("p u h -> p (u h)")
                eng.activation(f(neg_cum[par]), misc[:, 0:32], ACT.Copy, scale=-1.0)
                eng.activation(f(exp_cum[par]), misc[:, 0:32], ACT.Exp)
                eng.activation(f(exp_suf[par]), misc[:, 32:64], ACT.Exp)
                for b in range(2):
                    h = slice(b * HD, (b + 1) * HD)
                    tot = misc[h, 64:96].rearrange("p (u a b j) -> p (u a) b j", u=2, a=2, b=2)[:, :, b, :]
                    last = eng.activation(chunk_decay[par][h, :, :, :].rearrange("p u a j -> p (u a) j"), tot, ACT.Exp)
                last.then_inc(s["cum_done"], 1)

            def copy_ch(g, ch, i):
                n = g * NCH + ch
                eng.wait_ge(s["ch_ps"], n + 1)
                eng.wait_ge(s["ch_done"], n + 1)
                ps = proj_ps[ch % 2][:, 0:GR]
                eng.activation(raw[:, ch, 0:TAPS - 1], raw[:, ch, GR:GR + TAPS - 1], ACT.Copy)\
                   .then_inc(s["halo"], 1)
                eng.activation(acc[ch % 3][:, :], ps, ACT.Identity, bias=conv_b[:, ch:ch + 1],
                               scale=conv_w[:, ch, TAPS - 1:TAPS])
                eng.wait_ge(s["halo"], n + 1)
                eng.activation(raw[:, ch, TAPS - 1:TAPS - 1 + GR], ps, ACT.Copy).then_inc(s["ch_copied"], 1)

            def tanh_ch(g, ch):
                n = g * NCH + ch
                eng.wait_ge(s["tap"], n * 3 + 3)
                eng.wait_ge(s["ch_done"], n + 2)
                eng.activation(tnh[ch % 2][:, :], acc[ch % 3][:, :], ACT.Tanh).then_inc(s["ch_tanh"], 1)

            eng.wait_ge(s["consts"], 9)
            for u in range(2):
                copy_hT(0, 0, u)
            eng.wait_ge(s["folded"], 1)
            dt_exp(0)
            cum_exps(0, 0)
            for ch in range(NCH):
                copy_ch(0, ch, ch)
                if ch:
                    tanh_ch(0, ch - 1)
            tanh_ch(0, NCH - 1)
            for u in range(2):
                copy_hT(1, 1, u)

            def slot(c, k, gf, front, pre):
                u, par = k % 2, (k // 2) % 2
                half = u * (NCH // 2)
                for j in range(2):
                    eng.wait_ge(s["z_ps"], c * 2 + j + 1)
                    eng.wait_ge(s["ygate"], c * 2 + j + 1)
                    eng.activation(zs[:, j * 512:(j + 1) * 512], proj_ps[j][:, :], ACT.Tanh, scale=0.5)\
                       .then_inc(s["z_tanh"], 1)
                eng.wait_ge(s["xb_ps"], c + 1)
                eng.wait_ge(s["xdd"], c + 1)
                eng.activation(xb_row[:, :, :].rearrange("p a d -> p (a d)"), misc[:, :], ACT.Copy)\
                   .then_inc(s["xb_row"], 1)

                def exps(hg):
                    eng.wait_ge(seg_s[hg % 2], c * 2 + hg // 2 + 1)
                    eng.wait_ge(sc_s[hg % 2], c * 2 + hg // 2 + 1)
                    for j in range(HPG):
                        last = eng.activation(decay[hg % 2][:, j, :], seg_ps[hg % 2][:, j * P:(j + 1) * P], ACT.Exp,
                                              bias=neg_cum[par][:, u, hg * HPG + j:hg * HPG + j + 1])
                    last.then_inc(exp_s[hg % 2], 1)

                for hg in range(NG):
                    exps(hg)
                    if front:
                        copy_ch(gf, half + hg, hg)
                        if u == 0 and hg == 0:
                            dt_exp(gf)
                        if hg:
                            tanh_ch(gf, half + hg - 1)
                        if u == 0 and hg == 2:
                            cum_exps(gf, 1 - par)
                if front:
                    for i in (4, 5):
                        copy_ch(gf, half + i, i)
                        tanh_ch(gf, half + i - 1)
                if pre and u == 1:
                    copy_hT(gf + 1, par, 0)
                if front:
                    tanh_ch(gf, half + 5)
                if pre and u == 1:
                    copy_hT(gf + 1, par, 1)
                for j in range(2):
                    eng.wait_ge(s["ygate"], c * 2 + j + 3)
                    eng.activation(junk[:, j, :], yg[:, j * 512:(j + 1) * 512], ACT.Square,
                                   accum_out=sumsq[:, j:j + 1]).then_inc(s["sq"], 1)
                for j in range(2):
                    eng.wait_ge(s["yT_ps"], c * 2 + j + 3)
                    eng.wait_ge(s["out_ps"], c + 1)
                    eng.activation(yT[:, j * 4:j * 4 + 4, :].rearrange("p k n -> p (k n)"), misc[:, :], ACT.Copy)\
                       .then_inc(s["yT_done"], 1)
                eng.wait_ge(s["h_done"], c + 2)
                eng.activation(junk[:, 0, :], hres[:, :], ACT.Square, accum_out=sumsq[:, 4:5]).then_inc(s["hsq"], 1)

            slots(slot, eng)

        @block.vector
        def _(eng):
            def norm_rows(g, par):
                for u in range(2):
                    eng.wait_ge(s["lnq_step"], (g * 2 + u + 1) * NLN)
                    eng.tensor_scalar(xin[:, u, :], xin[:, u, :], mv[:, par, u, 0:1], lnq[:, par, u, 3:4],
                                      ALU.subtract, ALU.mult).then_inc(s["normed"], 1)

            def rows_in(g, par):
                eng.wait_ge(s["xin_dma"], (g + 1) * 32)
                for u in range(2):
                    eng.bn_stats(bn[:, u, :], xin[:, u, :]).then_inc(s["bn"], 1)
                for u in range(2):
                    wait_apart(eng, s["bn"], g * 2 + u + 1)
                    eng.bn_aggr(mv[:, par, u, :], bn[:, u, :]).then_inc(s["stat"], 1)

            def dt_first(g):
                eng.wait_ge(s["dt_ps"], g + 1)
                eng.tensor_tensor(sp[:, 0, :].rearrange("p (u h) -> p u h", u=2),
                                  misc[:, 0:32].rearrange("p (u h) -> p u h", u=2),
                                  dt_bias[:, :].unsqueeze(1).broadcast_to([P, 2, HEADS]), ALU.add).then_inc(s["dt_v"], 1)
                eng.wait_ge(s["dt_v"], g + 1)
                eng.scalar_tensor_tensor(sp[:, 1, :], sp[:, 0, :], -1.0, sp[:, 0, :], ALU.mult, ALU.min)\
                   .then_inc(s["dt_neg"], 1)

            def dt_rest(g, par):
                v, e, q, ss, s2, pl = (sp[:, i, :] for i in (0, 2, 3, 4, 5, 6))
                flat = lambda t: t[:, :, :].rearrange("p u h -> p (u h)")
                eng.wait_ge(s["dt_exp"], g + 1)
                steps = [lambda: eng.tensor_scalar(q, e, 2.0, None, ALU.add),
                         lambda: eng.reciprocal(q, q),
                         lambda: eng.tensor_tensor(ss, e, q, ALU.mult),
                         lambda: eng.tensor_tensor(s2, ss, ss, ALU.mult),
                         lambda: eng.tensor_scalar(pl, s2, 1.0 / 15, None, ALU.mult)]
                for cf in softplus_dt_steps():
                    steps.append(lambda cf=cf: eng.scalar_tensor_tensor(pl, pl, cf, s2, ALU.add, ALU.mult))
                steps += [lambda: eng.scalar_tensor_tensor(pl, pl, 1.0, ss, ALU.add, ALU.mult),
                          lambda: eng.tensor_scalar(v, v, 0.0, None, ALU.max),
                          lambda: eng.scalar_tensor_tensor(flat(dt[par]), pl, 2.0, v, ALU.mult, ALU.add)]
                assert len(steps) == NDT
                for i, step in enumerate(steps):
                    if i:
                        eng.wait_ge(s["dt_step"], g * NDT + i)
                    step().then_inc(s["dt_step"], 1)
                eng.wait_ge(s["dt_step"], g * NDT + NDT)
                eng.tensor_tensor(da[:, :, :], dt[par][:, :, :], a_neg[:, :].unsqueeze(1).broadcast_to([P, 2, HEADS]),
                                  ALU.mult).then_inc(s["dt_done"], 1)
                eng.wait_ge(s["dt_done"], g * 3 + 1)
                eng.tensor_copy(da_hi[par][:, :, :], da[:, :, :]).then_inc(s["dt_done"], 1)
                eng.wait_ge(s["dt_done"], g * 3 + 2)
                eng.tensor_tensor(da_lo[par][:, :, :], da[:, :, :], da_hi[par][:, :, :].bitcast(F32),
                                  ALU.subtract).then_inc(s["dt_done"], 1)

            def taps(g, ch):
                n = g * NCH + ch
                eng.wait_ge(s["ch_copied"], n + 1)
                for t in range(TAPS - 1):
                    if t:
                        eng.wait_ge(s["tap"], n * 3 + t)
                    eng.scalar_tensor_tensor(acc[ch % 3][:, :], raw[:, ch, t:t + GR], conv_w[:, ch, t:t + 1],
                                             acc[ch % 3][:, :], ALU.mult, ALU.add).then_inc(s["tap"], 1)

            def silu_ch(g, par, ch):
                n = g * NCH + ch
                eng.wait_ge(s["ch_tanh"], n + 1)
                eng.scalar_tensor_tensor(cv[par][:, ch, :], tnh[ch % 2][:, :], 1.0, acc[ch % 3][:, :],
                                         ALU.add, ALU.mult).then_inc(s["ch_done"], 1)

            rows_in(0, 0)
            norm_rows(0, 0)
            eng.wait_ge(s["w_dma"], 16 * NW)
            for k in range(KD):
                eng.tensor_scalar(w_in[:, k, :], w_in[:, k, :], ln1[:, k:k + 1], None, ALU.mult)
            eng.tensor_scalar(conv_w[:, :, :], conv_w[:, :, :], 0.5, None, ALU.mult)
            eng.tensor_scalar(conv_b[:, :], conv_b[:, :], 0.5, None, ALU.mult)
            eng.wait_ge(s["a_exp"], 1)
            eng.tensor_scalar(a_neg[:, :], a_neg[:, :], -1.0, None, ALU.mult)
            eng.wait_ge(s["consts"], 9)
            eng.tensor_copy(tri_r[:, :], tri[:, :])
            eng.tensor_copy(mask_r[:, :], mask[:, :])
            eng.tensor_copy(ident_r[:, :], ident[:, :]).then_inc(s["folded"], 1)
            for k in range(DI // P):
                last = eng.tensor_scalar(w_out[:, k, :], w_out[:, k, :], normw[:, k:k + 1], None, ALU.mult)
            last.then_inc(s["folded"], 1)
            eng.wait_ge(s["folded"], 2)
            dt_first(0)
            dt_rest(0, 0)
            for ch in range(NCH):
                taps(0, ch)
                if ch:
                    silu_ch(0, 0, ch - 1)
            silu_ch(0, 0, NCH - 1)
            rows_in(1, 1)
            norm_rows(1, 1)

            def slot(c, k, gf, front, pre):
                u, par = k % 2, (k // 2) % 2
                half = u * (NCH // 2)
                for j in range(2):
                    eng.wait_ge(s["z_tanh"], c * 2 + j + 1)
                    zj = zs[:, j * 512:(j + 1) * 512]
                    eng.scalar_tensor_tensor(zj, zj, 1.0, proj_ps[j][:, :], ALU.add, ALU.mult)\
                       .then_inc(s["z_gate"], 1)
                eng.wait_ge(s["xb_row"], c + 1)
                eng.wait_ge(s["yd1"], c * 2 + 1)
                eng.wait_ge(s["xdd"], c + 1)
                xr = xb_row[:, 0, :].rearrange("p (g d) -> p g d", g=NG).unsqueeze(2).broadcast_to([P, NG, HPG, HD])
                eng.tensor_tensor(xdt[:, :].rearrange("p (g r d) -> p g r d", g=NG, r=HPG), xr,
                                  dt[par][:, u, :].rearrange("p (g r) -> p g r", g=NG).unsqueeze(3)
                                  .broadcast_to([P, NG, HPG, HD]), ALU.mult).then_inc(s["xdt"], 1)
                eng.wait_ge(s["xres_dma"], (c + 1) * 16)
                eng.tensor_scalar(yres[:, :], xres[:, :], mv[:, par, u, 0:1], lnq[:, par, u, 1:2],
                                  ALU.subtract, ALU.mult).then_inc(s["yres"], 1)

                def scores(hg):
                    eng.wait_ge(exp_s[hg % 2], c * 2 + hg // 2 + 2)
                    eng.wait_ge(s["cb"], c * 4 + hg + 1)
                    eng.wait_ge(yd_s[hg % 2], c * 2 + hg // 2 + 1)
                    eng.tensor_tensor(score[hg % 2][:, :, :], decay[hg % 2][:, :, :],
                                      cb_ps[:, :].rearrange("p (j q) -> p j q", j=HPG), ALU.mult)\
                       .then_inc(sc_s[hg % 2], 1)

                def sums(hg):
                    n = c * 4 + hg
                    eng.wait_ge(yd_s[hg % 2], c * 2 + hg // 2 + 2)
                    if hg == 0:
                        eng.wait_ge(s["dx"], c + 1)
                    ps = y_ps[hg % 2]
                    yd = head_cols(ydiag, hg)
                    eng.tensor_tensor(yd, ps[:, 0:HPG * HD], head_cols(dx, hg), ALU.add).then_inc(s["yread_a"], 1)
                    eng.tensor_tensor(yoff[:, :].rearrange("p (j d) -> p j d", j=HPG),
                                      ps[:, HPG * HD:2 * HPG * HD].rearrange("p (j d) -> p j d", j=HPG),
                                      exp_cum[par][:, u, hg * HPG:(hg + 1) * HPG].unsqueeze(2)
                                      .broadcast_to([P, HPG, HD]), ALU.mult).then_inc(yread_s[hg % 2], 1)
                    eng.wait_ge(s["yread_a"], n + 1)
                    eng.wait_ge(yread_s[hg % 2], c * 2 + hg // 2 + 2)
                    eng.tensor_tensor(yd, yd, yoff[:, :], ALU.add).then_inc(s["ysum"], 1)

                def gate(j):
                    eng.wait_ge(s["ysum"], c * 4 + 2 * j + 6)
                    eng.wait_ge(s["z_gate"], c * 2 + j + 1)
                    eng.wait_ge(s["yT_ps"], c * 2 + j + 1)
                    h = slice(j * 512, (j + 1) * 512)
                    eng.tensor_tensor(yg[:, h], ydiag[:, h], zs[:, h], ALU.mult).then_inc(s["ygate"], 1)

                scores(0)
                if front:
                    taps(gf, half + 0)
                if front and u == 0:
                    dt_first(gf)
                sums(0)
                scores(1)
                if front:
                    taps(gf, half + 1)
                    silu_ch(gf, 1 - par, half + 0)
                if front and u == 0:
                    dt_rest(gf, 1 - par)
                if pre and u == 1:
                    rows_in(gf + 1, par)
                sums(1)
                gate(0)
                scores(2)
                if front:
                    taps(gf, half + 2)
                    silu_ch(gf, 1 - par, half + 1)
                if pre and u == 1:
                    norm_rows(gf + 1, par)
                sums(2)
                scores(3)
                if front:
                    taps(gf, half + 3)
                    silu_ch(gf, 1 - par, half + 2)
                sums(3)
                eng.wait_ge(s["state_ps"], c + 2)
                eng.wait_ge(s["carry_decayed"], c + 1)
                eng.tensor_tensor(carry[:, :, :, :].rearrange("p a j d -> p (a j d)"),
                                  carry[:, :, :, :].rearrange("p a j d -> p (a j d)"), misc[:, :], ALU.add)\
                   .then_inc(s["carry_done"], 1)
                gate(1)
                if front:
                    for i in (4, 5):
                        taps(gf, half + i)
                        silu_ch(gf, 1 - par, half + i - 1)
                    silu_ch(gf, 1 - par, half + 5)
                eng.wait_ge(s["out_ps"], c + 2)
                eng.wait_ge(s["r_step"], c * NR + NR)
                eng.wait_ge(s["yres"], c + 1)
                eng.wait_ge(s["h2_step"], c * NH2 + 1)
                eng.scalar_tensor_tensor(hres[:, :], misc[:, :], sumsq[:, 3:4], yres[:, :], ALU.mult, ALU.add)\
                   .then_inc(s["h_done"], 1)

            slots(slot, eng)

        @block.tensor
        def _(eng):
            def row_transposes(g, par, u):
                eng.wait_ge(s["normed"], g * 2 + u + 1)
                for k in range(KD):
                    last = eng.transpose(misc[:, k * P:(k + 1) * P], xin[:, u, k * P:(k + 1) * P], ident[:, :])
                last.then_inc(s["rowT"], 1)

            def dt_proj(g, par):
                eng.wait_ge(s["hT_done"], g * 2 + 2)
                for u in range(2):
                    for k in range(KD):
                        last = eng.matmul(misc[:, u * HEADS:(u + 1) * HEADS], hT[par][:, k, u * P:(u + 1) * P],
                                          w_in[:, k, DT0:DIN], start=(k == 0), stop=(k == KD - 1))
                last.then_inc(s["dt_ps"], 1)

            def cum_sums(g, par):
                eng.wait_ge(s["dt_done"], g * 3 + 3)
                rhs = da[:, :, :].rearrange("p u h -> p (u h)")
                for i, w in enumerate((tri, suffix, ones)):
                    last = eng.matmul(misc[:, i * 32:(i + 1) * 32], w[:, :], rhs, start=True, stop=True)
                last.then_inc(s["cum_ps"], 1)

            def channel_block(g, par, ch):
                col = CH0 + ch * P
                for k in range(KD):
                    last = eng.matmul(proj_ps[ch % 2][:, 0:GR], w_in[:, k, col:col + P], hT[par][:, k, :],
                                      start=(k == 0), stop=(k == KD - 1))
                last.then_inc(s["ch_ps"], 1)

            row_transposes(0, 0, 0)
            eng.wait_ge(s["hT_done"], 1)
            row_transposes(0, 0, 1)
            eng.wait_ge(s["folded"], 2)
            dt_proj(0, 0)
            cum_sums(0, 0)
            for ch in range(NCH):
                if ch >= 2:
                    eng.wait_ge(s["ch_copied"], ch - 1)
                channel_block(0, 0, ch)
            eng.wait_ge(s["cum_done"], 1)
            row_transposes(1, 1, 0)
            eng.wait_ge(s["hT_done"], 3)
            row_transposes(1, 1, 1)

            def slot(c, k, gf, front, pre):
                u, par = k % 2, (k // 2) % 2
                half = u * (NCH // 2)
                tile = slice(u * P, (u + 1) * P)
                const = isinstance(c, int)
                blocks_before = min(NCH + 6 * c, NCH * NGRP) if const else c * 6 + NCH
                pre_before = min(4 + c - u, TILES) if const else c + 4 - u

                eng.wait_ge(s["ch_copied"], blocks_before)
                if const and c > 14:
                    eng.wait_ge(s["z_gate"], c * 2)
                for j in range(2):
                    for q in range(KD):
                        last = eng.matmul(proj_ps[j][:, :], hT[par][:, q, tile], w_in[:, q, j * 512:(j + 1) * 512],
                                          start=(q == 0), stop=(q == KD - 1))
                    last.then_inc(s["z_ps"], 1)

                eng.wait_ge(s["h_done"], c + 1)
                eng.wait_ge(s["hT_done"], pre_before)
                eng.wait_ge(s["ch_done"], gf * NCH + 3)
                for i in range(4):
                    last = eng.transpose(misc[:, i * P:(i + 1) * P], cv[par][:, i, tile], ident[:, :])
                last.then_inc(s["xb_ps"], 1)

                def seg(hg):
                    eng.wait_ge(exp_s[hg % 2], c * 2 + hg // 2 + 1)
                    ps = seg_ps[hg % 2]
                    eng.matmul(ps[:, :], ident_r[:, :], mask_r[:, :].unsqueeze(1).broadcast_to([P, HPG, P]),
                               start=True, stop=False, skip_group_check=True)
                    for j in range(HPG):
                        h = hg * HPG + j
                        for part in (da_hi, da_lo):
                            last = eng.matmul(ps[:, j * P:(j + 1) * P],
                                              part[par][:, u, h:h + 1].broadcast_to([P, P]), tri_r[:, :],
                                              start=False, stop=(part is da_lo and j == HPG - 1),
                                              skip_group_check=True)
                    last.then_inc(seg_s[hg % 2], 1)

                def b_dot_c(hg):
                    a, b = hg // 2, hg % 2
                    p = slice(b * HD, (b + 1) * HD)
                    eng.wait_ge(sc_s[(hg + 1) % 2], c * 2 + (hg + 1) // 2 + 1)
                    eng.matmul(cb_ps[:, :], cv[par][p, 2 + a, tile],
                               cv[par][p, 4 + 4 * a:8 + 4 * a, tile], start=True, stop=True).then_inc(s["cb"], 1)

                def outputs(hg):
                    a, b = hg // 2, hg % 2
                    p = slice(b * HD, (b + 1) * HD)
                    if hg == 0:
                        eng.wait_ge(s["carry_done"], c + 1)
                        eng.wait_ge(s["xdt"], c + 2)
                    eng.wait_ge(yread_s[hg % 2], c * 2 + hg // 2 + 1)
                    n = HPG * HD
                    for j in range(HPG):
                        eng.matmul(y_ps[hg % 2][:, n + j * HD:n + (j + 1) * HD], cv[par][p, 4 + 4 * a + j, tile],
                                   carry[p, a, j, :], start=True, stop=True)
                    eng.wait_ge(sc_s[hg % 2], c * 2 + hg // 2 + 2)
                    for j in range(HPG):
                        h = hg * HPG + j
                        last = eng.matmul(y_ps[hg % 2][:, j * HD:(j + 1) * HD], score[hg % 2][:, j, :],
                                          xdt[:, h * HD:(h + 1) * HD], start=True, stop=True)
                    last.then_inc(yd_s[hg % 2], 1)

                def front_block(i):
                    if i < 2:
                        eng.wait_ge(s["z_gate"], c * 2 + i + 1)
                    else:
                        eng.wait_ge(s["ch_copied"], gf * NCH + half + i - 1)
                    channel_block(gf, 1 - par, half + i)

                seg(0)
                b_dot_c(0)
                if front:
                    if u == 0:
                        eng.wait_ge(s["xb_row"], c + 1)
                        dt_proj(gf, 1 - par)
                    front_block(0)
                seg(1)
                outputs(0)
                b_dot_c(1)
                if front:
                    front_block(1)
                seg(2)
                outputs(1)
                b_dot_c(2)
                if front:
                    front_block(2)
                if front and u == 0:
                    cum_sums(gf, 1 - par)
                seg(3)
                outputs(2)
                b_dot_c(3)
                if front:
                    front_block(3)
                eng.wait_ge(s["xb_row"], c + 1)
                if front and u == 0:
                    eng.wait_ge(s["cum_done"], gf + 1)
                eng.wait_ge(s["xdd"], c + 2)
                for hg in range(NG):
                    a, b = hg // 2, hg % 2
                    n = HPG * HD
                    last = eng.matmul(misc[b * HD:(b + 1) * HD, a * n:(a + 1) * n],
                                      xb_row[:, 1, hg * HD:(hg + 1) * HD], xdd[:, hg * n:(hg + 1) * n],
                                      start=True, stop=True)
                last.then_inc(s["state_ps"], 1)
                outputs(3)
                if front:
                    front_block(4)
                if pre and u == 1:
                    eng.wait_ge(s["carry_done"], c + 2)
                    row_transposes(gf + 1, par, 0)
                if front:
                    front_block(5)
                if pre and u == 1:
                    eng.wait_ge(s["hT_done"], gf * 2 + 3)
                    row_transposes(gf + 1, par, 1)
                    eng.wait_ge(s["hT_done"], gf * 2 + 4)
                eng.wait_ge(s["carry_done"], c + 2)
                for j in range(2):
                    eng.wait_ge(s["ygate"], c * 2 + j + 3)
                    if j:
                        eng.wait_ge(s["yT_done"], c * 2 + 1)
                    for i in range(4):
                        f = (j * 4 + i) * P
                        last = eng.transpose(misc[:, i * P:(i + 1) * P], yg[:, f:f + P], ident[:, :])
                    last.then_inc(s["yT_ps"], 1)
                eng.wait_ge(s["yT_done"], c * 2 + 2)
                for i in range(DI // P):
                    last = eng.matmul(misc[:, :], yT[:, i, :], w_out[:, i, :], start=(i == 0), stop=(i == DI // P - 1))
                last.then_inc(s["out_ps"], 1)

            slots(slot, eng)


def constants(nc, ident, ones):
    with nc.semaphore("ident_step") as step, nc.Block() as block:
        @block.gpsimd
        def _(eng):
            eng.memset(ones[:, :], 1.0)
            eng.memset(ident[:, :], 0.0).then_inc(step, 1)
            eng.wait_ge(step, 1)
            eng.affine_select(out=ident[:, :], in_=ident[:, :], compare_op=ALU.not_equal, fill=1.0, base=0,
                              pattern=[[-1, P]], channel_multiplier=1)


def feed_forward(nc, ins, dr, ident, acc):
    NB, NI, RG = FF // FB, FB // P, 512
    NR = ROWS // RG
    TPR = RG // P
    with ExitStack() as ctx:
        def sb(name, shape, dt=F32):
            return ctx.enter_context(nc.sbuf_tensor(name, shape, dt))

        zeros = sb("zeros", [P, D])
        rows = [sb(f"ff_rows{i}", [P, D]) for i in range(2)]
        hT_hi = sb("ff_hT_hi", [P, KD, ROWS], F32R)
        hT_lo = sb("ff_hT_lo", [P, KD, ROWS], F32R)
        stage = [sb(f"ff_stage{i}", [P, KD * FB]) for i in range(3)]
        w_hi = [[sb(f"ff_w_hi{i}{j}", [P, KD * FB], F32R) for j in range(3)] for i in range(2)]
        w_lo = [[sb(f"ff_w_lo{i}{j}", [P, KD * FB], F32R) for j in range(3)] for i in range(2)]
        prod = [sb(f"ff_prod{i}", [P, RG]) for i in range(2)]
        p_hi = [sb(f"ff_p_hi{i}", [P, NI, RG], F32R) for i in range(2)]
        p_lo = [sb(f"ff_p_lo{i}", [P, NI, RG], F32R) for i in range(2)]
        bank = [ctx.enter_context(nc.psum_tensor(f"ff_bank{i}", [P, 512], F32)) for i in range(8)]
        gate_ps, up_ps, down_ps = bank[0:2], bank[2:4], bank[4:8]
        assert NI * D == KD * FB and TPR == 4
        s = {n: ctx.enter_context(nc.semaphore("ff_" + n)) for n in (
            "zeroed", "cleared", "acc_dma", "rows_dma0", "rows_dma1", "rowT", "hT_hi", "hT_lo", "w_dma0", "w_dma1", "w_dma2", "w_hi", "w_lo",
            "gate_ps", "up_ps", "silu", "prod", "p_hi", "p_lo", "down", "add")}
        CR = 2 * TPR
        rows_dma = [s["rows_dma0"], s["rows_dma1"]]
        w_dma = [s["w_dma0"], s["w_dma1"], s["w_dma2"]]
        block = ctx.enter_context(nc.Block())

        def as_in(t):
            return t[:, :].rearrange("p (k n) -> p k n", k=KD)

        def as_down(t):
            return t[:, :].rearrange("p (c n) -> p c n", c=NI)

        @block.sync
        def _(eng):
            def load_piece(b, j):
                if j < 2:
                    src = ins["L0_attn_gate_w" if j == 0 else "L0_attn_up_w"].rearrange("(k p) n -> p k n", p=P)
                    eng.dma_start(as_in(stage[j]), src[:, :, bass.ds(b * FB, FB)]).then_inc(w_dma[j], 16)
                else:
                    src = ins["L0_attn_down_w"][bass.ds(b * FB, FB), :].rearrange("(c p) n -> p c n", p=P)
                    eng.dma_start(as_down(stage[j]), src).then_inc(w_dma[j], 16)

            for t in range(2):
                eng.dma_start(rows[t][:, :], dr["h2"][bass.ds(t * P, P), :]).then_inc(rows_dma[t], 16)
            for j in range(3):
                load_piece(0, j)
            with eng.Fori(1, TILES // 2) as i:
                for t in range(2):
                    eng.wait_ge(s["rowT"], i * 2 + t - 1)
                    eng.dma_start(rows[t][:, :], dr["h2"][bass.ds((i * 2 + t) * P, P), :]).then_inc(rows_dma[t], 16)
            eng.dma_start(acc[:, :, :], dr["xh"].rearrange("(t p) n -> p t n", p=P)).then_inc(s["acc_dma"], 16)
            eng.wait_ge(s["zeroed"], 1)
            eng.dma_start(dr["sorted"].rearrange("(t p) n -> p t n", p=P),
                          zeros[:, :].unsqueeze(1).broadcast_to([P, SORT_TILES, D])).then_inc(s["cleared"], 16)
            with eng.Fori(1, NB) as b:
                for j in range(3):
                    eng.wait_ge(s["w_lo"], b * 3 + j - 2)
                    load_piece(b, j)
            eng.wait_ge(s["cleared"], 16)

        @block.gpsimd
        def _(eng):
            for name, n in (("silu", 2), ("prod", 2), ("p_lo", 2), ("down", CR), ("add", TPR), ("hT_lo", 2)):
                eng.sem_inc(s[name], n)
            eng.memset(zeros[:, :], 0.0).then_inc(s["zeroed"], 1)

            def low_parts(b, par):
                for j in range(3):
                    eng.wait_ge(w_dma[j], (b + 1) * 16)
                    eng.wait_ge(s["w_hi"], b * 3 + j + 1)
                    eng.tensor_tensor(w_lo[par][j][:, :], stage[j][:, :], w_hi[par][j][:, :].bitcast(F32),
                                      ALU.subtract).then_inc(s["w_lo"], 1)

            with eng.Fori(0, NB // 2) as i:
                for par in range(2):
                    low_parts(i * 2 + par, par)


        def steps(body, eng):
            with eng.Fori(0, NB // 2 - 1) as i:
                for k in range(2 * NR):
                    body(i * 2 + k // NR, k)
            for k in range(2 * NR):
                body(NB - 2 + k // NR, k)

        def following(width, b, k):
            if not (isinstance(b, int) and b * NR + k % NR == NB * NR - 1):
                width(b + (k + 1) // NR - k // NR, (k + 1) % (2 * NR))

        @block.scalar
        def _(eng):
            for j in range(3):
                eng.wait_ge(w_dma[j], 16)
                eng.activation(w_hi[0][j][:, :], stage[j][:, :], ACT.Copy).then_inc(s["w_hi"], 1)
            with eng.Fori(0, TILES // 2) as i:
                for v in range(2):
                    eng.wait_ge(s["rowT"], i * 2 + v + 1)
                    eng.activation(hT_hi[:, :, bass.ds((i * 2 + v) * P, P)],
                                   bank[v][:, :].rearrange("p (k n) -> p k n", k=KD), ACT.Copy).then_inc(s["hT_hi"], 1)

            def width(b, k):
                step = b * NR + k % NR
                for c in range(NI):
                    n = step * NI + c
                    eng.wait_ge(s["gate_ps"], n + 1)
                    eng.wait_ge(s["p_lo"], n + 1)
                    eng.activation(prod[c][:, :], gate_ps[c][:, :], ACT.Silu).then_inc(s["silu"], 1)
                    eng.wait_ge(s["prod"], n + 3)
                    eng.wait_ge(s["down"], step * TPR + TPR)
                    eng.activation(p_hi[k % 2][:, c, :], prod[c][:, :], ACT.Copy).then_inc(s["p_hi"], 1)

            width(0, 0)

            def body(b, k):
                if k % NR and not (isinstance(b, int) and b == NB - 1):
                    j = k % NR - 1
                    eng.wait_ge(w_dma[j], b * 16 + 32)
                    eng.wait_ge(s["down"], b * NR * TPR + CR)
                    eng.activation(w_hi[(k // NR + 1) % 2][j][:, :], stage[j][:, :], ACT.Copy)\
                       .then_inc(s["w_hi"], 1)
                following(width, b, k)

            steps(body, eng)

        @block.vector
        def _(eng):
            with eng.Fori(0, TILES // 2) as i:
                for v in range(2):
                    eng.wait_ge(s["hT_hi"], i * 2 + v + 1)
                    cols = bass.ds((i * 2 + v) * P, P)
                    eng.tensor_tensor(hT_lo[:, :, cols], bank[v][:, :].rearrange("p (k n) -> p k n", k=KD),
                                      hT_hi[:, :, cols].bitcast(F32), ALU.subtract).then_inc(s["hT_lo"], 1)

            def width(b, k):
                for c in range(NI):
                    n = (b * NR + k % NR) * NI + c
                    eng.wait_ge(s["silu"], n + 3)
                    eng.wait_ge(s["up_ps"], n + 1)
                    eng.tensor_tensor(prod[c][:, :], prod[c][:, :], up_ps[c][:, :], ALU.mult).then_inc(s["prod"], 1)
                    eng.wait_ge(s["prod"], n + 3)
                    eng.wait_ge(s["p_hi"], n + 1)
                    eng.tensor_tensor(p_lo[k % 2][:, c, :], prod[c][:, :], p_hi[k % 2][:, c, :].bitcast(F32),
                                      ALU.subtract).then_inc(s["p_lo"], 1)

            width(0, 0)
            eng.wait_ge(s["acc_dma"], 16)

            def body(b, k):
                following(width, b, k)
                for t in range(TPR):
                    eng.wait_ge(s["down"], (b * NR + k % NR) * TPR + t + 1 + CR)
                    row = acc[:, (k % NR) * TPR + t, :]
                    eng.tensor_tensor(row, down_ps[t][:, :], row, ALU.add).then_inc(s["add"], 1)

            steps(body, eng)

        @block.tensor
        def _(eng):
            with eng.Fori(0, TILES // 2) as i:
                for v in range(2):
                    eng.wait_ge(rows_dma[v], i * 16 + 16)
                    eng.wait_ge(s["hT_lo"], i * 2 + v + 1)
                    for k in range(KD):
                        last = eng.transpose(bank[v][:, k * P:(k + 1) * P], rows[v][:, k * P:(k + 1) * P], ident[:, :])
                    last.then_inc(s["rowT"], 1)
            eng.wait_ge(s["hT_lo"], TILES + 2)

            def three(ps, w, x, first, last):
                for i, (a, b) in enumerate(((0, 0), (0, 1), (1, 0))):
                    mm = eng.matmul(ps, w[a], x[b], start=first and i == 0, stop=last and i == 2)
                return mm

            def width(b, k):
                par, r = k // NR % 2, k % NR
                if r == 0:
                    eng.wait_ge(s["w_lo"], b * 3 + 3)
                cols = slice(r * RG, (r + 1) * RG)
                for c in range(NI):
                    n = (b * NR + r) * NI + c
                    for j, ps, free, done in ((0, gate_ps[c], "silu", "gate_ps"), (1, up_ps[c], "prod", "up_ps")):
                        eng.wait_ge(s[free], n + 1)
                        for q in range(KD):
                            w = [as_in(t[par][j])[:, q, c * P:(c + 1) * P] for t in (w_hi, w_lo)]
                            x = [t[:, q, cols] for t in (hT_hi, hT_lo)]
                            mm = three(ps[:, :], w, x, q == 0, q == KD - 1)
                        mm.then_inc(s[done], 1)

            def out(b, k):
                par, step = k // NR % 2, b * NR + k % NR
                eng.wait_ge(s["p_lo"], step * NI + NI + 2)
                for t in range(TPR):
                    eng.wait_ge(s["add"], step * TPR + t + 1)
                    for c in range(NI):
                        x = [v[k % 2][:, c, t * P:(t + 1) * P] for v in (p_hi, p_lo)]
                        w = [as_down(v[par][2])[:, c, :] for v in (w_hi, w_lo)]
                        mm = three(down_ps[t][:, :], x, w, c == 0, c == NI - 1)
                    mm.then_inc(s["down"], 1)

            width(0, 0)

            def body(b, k):
                following(width, b, k)
                out(b, k)

            steps(body, eng)


def experts(nc, ins, dr, out_d, ident, ones, acc):
    with ExitStack() as ctx:
        def sb(name, shape, dt=F32, where=ctx):
            return where.enter_context(nc.sbuf_tensor(name, shape, dt))

        def sem(name):
            return ctx.enter_context(nc.semaphore("moe_" + name))

        w_gu = sb("w_gu", [P, 2, E * KD, EI])
        w_dn = sb("w_dn", [P, E * len(IC), D])
        mv = sb("moe_mv", [P, TILES, 2])
        rstd = sb("moe_rstd", [P, TILES])
        weight = sb("moe_weight", [P, 2, TILES])
        slot = sb("moe_slot", [P, 2 * TILES], U32)
        tile_expert = sb("tile_expert", [1, SORT_TILES], mybir.dt.int32)
        s_w = sem("w_dma")
        NW = 2 * E + 2 * E

        with ExitStack() as rctx:
            xm = [sb(f"xm{i}", [P, D], where=rctx) for i in range(4)]
            xmT = [sb(f"xmT{i}", [P, KD, P], where=rctx) for i in range(2)]
            wr = sb("wr", [P, KD, E], where=rctx)
            bn = sb("moe_bn", [P, TILES, 6], where=rctx)
            half_neg = sb("moe_half_neg", [P, TILES], where=rctx)
            strict = sb("strict", [P, P], where=rctx)
            iota_e = sb("iota_e", [P, E], mybir.dt.int32, where=rctx)
            iota_t = sb("iota_t", [P, SORT_TILES + 1], mybir.dt.int32, where=rctx)
            ef = sb("ef", [P, E], where=rctx)
            tf = sb("tf", [P, SORT_TILES + 1], where=rctx)
            t3 = lambda name: sb(name, [P, TILES, E], where=rctx)
            prob, top, hot0, hot1, hot, run_a, run_b, place = map(
                t3, ("prob", "top", "hot0", "hot1", "hot", "run_a", "run_b", "place"))
            idx = sb("idx", [P, TILES, E], U32, where=rctx)
            idx_f = sb("idx_f", [P, TILES, 2], where=rctx)
            red = sb("red", [P, 4, TILES], where=rctx)
            cmp_n = sb("cmp_n", [P, E, TILES], where=rctx)
            ends = sb("ends", [P, 4, E], where=rctx)
            cmp_t = sb("cmp_t", [P, SORT_TILES, E], where=rctx)
            slot_f = sb("slot_f", [P, 2 * TILES], where=rctx)
            te_f = sb("te_f", [P, SORT_TILES], where=rctx)
            bank = [rctx.enter_context(nc.psum_tensor(f"rt_bank{i}", [P, 512], F32)) for i in range(4)]
            s = {n: rctx.enter_context(nc.semaphore("rt_" + n)) for n in (
                "wr_dma", "const", "bn", "stat", "rstd", "xm", "rowT", "xmT", "logits", "route", "exp", "counts",
                "again", "scat0", "scat1", "scat2", "scat3")}
            scat = [s[f"scat{i}"] for i in range(4)]
            HOT = 5 + 2 * TILES + 8
            block = rctx.enter_context(nc.Block())

            @block.sync
            def _(eng):
                eng.dma_start(wr[:, :, :], ins["L0_ffn_Wr"].rearrange("(k p) e -> p k e", p=P)).then_inc(s["wr_dma"], 16)
                for e in range(E):
                    for j, name in enumerate(("L0_ffn_Wg", "L0_ffn_Wu")):
                        eng.dma_start(w_gu[:, j, e * KD:(e + 1) * KD, :],
                                      ins[name][e].rearrange("(k p) i -> p k i", p=P)).then_inc(s_w, 16)
                    n, full = len(IC), EI // P
                    src = ins["L0_ffn_Wd"][e]
                    eng.dma_start(w_dn[:, e * n:e * n + full, :],
                                  src[0:full * P, :].rearrange("(c p) n -> p c n", p=P)).then_inc(s_w, 16)
                    eng.dma_start(w_dn[0:EI - full * P, e * n + full, :], src[full * P:EI, :]).then_inc(s_w, 16)
                eng.wait_ge(s["wr_dma"], 16)

            @block.gpsimd
            def _(eng):
                eng.sem_inc(s["xmT"], 2)
                eng.sem_inc(s["logits"], 2)
                eng.memset(half_neg[:, :], -0.5).then_inc(s["const"], 1)
                eng.memset(strict[:, :], 1.0).then_inc(s["const"], 1)
                eng.iota(iota_e[:, :], pattern=[[1, E]], base=0, channel_multiplier=0).then_inc(s["const"], 1)
                eng.iota(iota_t[:, :], pattern=[[1, SORT_TILES + 1]], base=0, channel_multiplier=0)\
                   .then_inc(s["const"], 1)
                eng.wait_ge(s["const"], 4)
                eng.affine_select(out=strict[:, :], in_=strict[:, :], compare_op=ALU.is_gt, fill=0.0, base=0,
                                  pattern=[[1, P]], channel_multiplier=-1).then_inc(s["const"], 1)
                eng.wait_ge(s["stat"], TILES)
                eng.tensor_scalar(rstd[:, :], mv[:, :, 1], EPS, None, ALU.add).then_inc(s["rstd"], 1)
                eng.wait_ge(s["rstd"], 1)
                eng.tensor_tensor(rstd[:, :], rstd[:, :], half_neg[:, :], ALU.pow).then_inc(s["rstd"], 1)
                for t in range(TILES):
                    eng.wait_ge(s["again"], t + 1)
                    for k in range(2):
                        n = 2 * t + k
                        eng.indirect_dma_start(out=dr["sorted"][:, :],
                                               out_offset=bass.IndirectOffsetOnAxis(ap=slot[:, k * TILES + t:k * TILES + t + 1], axis=0),
                                               in_=xm[t % 4][:, :], in_offset=None).then_inc(scat[t % 4], 16)
                for i in range(4):
                    eng.wait_ge(scat[i], 2 * 16 * (TILES // 4))

            @block.scalar
            def _(eng):
                with eng.Fori(0, TILES // 2) as i:
                    for v in range(2):
                        eng.wait_ge(s["rowT"], i * 2 + v + 1)
                        eng.wait_ge(s["logits"], i * 2 + v + 1)
                        eng.activation(xmT[v][:, :, :].rearrange("p k n -> p (k n)"), bank[v][:, :], ACT.Copy)\
                           .then_inc(s["xmT"], 1)
                eng.wait_ge(s["route"], 2)
                eng.activation(prob[:, :, :], prob[:, :, :], ACT.Exp).then_inc(s["exp"], 1)

            @block.tensor
            def _(eng):
                eng.wait_ge(s["wr_dma"], 16)
                for i in range(TILES // 2):
                    for v in range(2):
                        t = i * 2 + v
                        eng.wait_ge(s["xm"], t + 1)
                        eng.wait_ge(s["xmT"], t + 1)
                        for k in range(KD):
                            last = eng.transpose(bank[v][:, k * P:(k + 1) * P], xm[t % 4][:, k * P:(k + 1) * P],
                                                 ident[:, :])
                        last.then_inc(s["rowT"], 1)
                        eng.wait_ge(s["xmT"], t + 3)
                        for k in range(KD):
                            last = eng.matmul(bank[2][:, t * E:(t + 1) * E], xmT[v][:, k, :], wr[:, k, :],
                                              start=(k == 0), stop=(k == KD - 1))
                        last.then_inc(s["logits"], 1)
                eng.wait_ge(s["const"], 5)
                eng.wait_ge(s["route"], HOT)
                flat = hot[:, :, :].rearrange("p t e -> p (t e)")
                eng.matmul(bank[3][:, 0:P], strict[:, :], flat, start=True, stop=True)
                eng.matmul(bank[3][:, P:2 * P], ones[:, :], flat, start=True, stop=True).then_inc(s["counts"], 1)

            @block.vector
            def _(eng):
                done = [0]

                def step(ins_):
                    ins_.then_inc(s["route"], 1)
                    done[0] += 1
                    eng.wait_ge(s["route"], done[0])

                def per_tile(a):
                    return a.unsqueeze(2).broadcast_to([P, TILES, E])

                def normed(t):
                    return eng.tensor_scalar(xm[t % 4][:, :], acc[:, t, :], mv[:, t, 0:1], rstd[:, t:t + 1],
                                             ALU.subtract, ALU.mult)

                for t in range(TILES):
                    eng.bn_stats(bn[:, t, :], acc[:, t, :]).then_inc(s["bn"], 1)
                for t in range(TILES):
                    eng.wait_ge(s["bn"], t + 1)
                    eng.bn_aggr(mv[:, t, :], bn[:, t, :]).then_inc(s["stat"], 1)
                eng.wait_ge(s["rstd"], 2)
                for t in range(TILES):
                    if t >= 4:
                        eng.wait_ge(s["rowT"], t - 3)
                    normed(t).then_inc(s["xm"], 1)
                eng.wait_ge(s["logits"], TILES + 2)
                logits = bank[2][:, 0:TILES * E].rearrange("p (t e) -> p t e", e=E)
                step(eng.tensor_reduce(red[:, 0, :], logits, AX_X, ALU.max))
                step(eng.tensor_tensor(prob[:, :, :], logits, per_tile(red[:, 0, :]), ALU.subtract))
                eng.wait_ge(s["exp"], 1)
                step(eng.tensor_reduce(red[:, 1, :], prob[:, :, :], AX_X, ALU.add))
                step(eng.reciprocal(red[:, 2, :], red[:, 1, :]))
                step(eng.tensor_tensor(prob[:, :, :], prob[:, :, :], per_tile(red[:, 2, :]), ALU.mult))
                for t in range(TILES):
                    step(eng.max(top[:, t, :], prob[:, t, :]))
                    step(eng.max_index(idx[:, t, :], top[:, t, :], prob[:, t, :]))
                eng.wait_ge(s["const"], 5)
                step(eng.tensor_copy(ef[:, :], iota_e[:, :]))
                step(eng.tensor_copy(tf[:, :], iota_t[:, :]))
                step(eng.tensor_copy(idx_f[:, :, :], idx[:, :, 0:2]))
                e_of = ef[:, :].unsqueeze(1).broadcast_to([P, TILES, E])
                for k, h in enumerate((hot0, hot1)):
                    step(eng.tensor_tensor(h[:, :, :], e_of, per_tile(idx_f[:, :, k]), ALU.is_equal))
                step(eng.tensor_tensor(hot[:, :, :], hot0[:, :, :], hot1[:, :, :], ALU.add))
                step(eng.tensor_tensor(red[:, 0, :], top[:, :, 0], top[:, :, 1], ALU.add))
                step(eng.reciprocal(red[:, 3, :], red[:, 0, :]))
                assert done[0] == HOT
                for k in range(2):
                    step(eng.tensor_tensor(weight[:, k, :], top[:, :, k], red[:, 3, :], ALU.mult))
                eng.wait_ge(s["counts"], 1)
                before = bank[3][:, 0:P].rearrange("p (t e) -> p t e", e=E)
                total = bank[3][:, P:2 * P].rearrange("p (t e) -> p t e", e=E)
                step(eng.tensor_copy(run_a[:, :, :], total))
                a, b = run_a, run_b
                sh = 1
                while sh < TILES:
                    step(eng.tensor_copy(b[:, 0:sh, :], a[:, 0:sh, :]))
                    step(eng.tensor_tensor(b[:, sh:TILES, :], a[:, sh:TILES, :], a[:, 0:TILES - sh, :], ALU.add))
                    a, b, sh = b, a, 2 * sh
                step(eng.tensor_scalar(tf[:, :], tf[:, :], float(P), None, ALU.mult))
                step(eng.tensor_tensor(cmp_n[:, :, :], a[:, TILES - 1, :].unsqueeze(2).broadcast_to([P, E, TILES]),
                                       tf[:, 0:TILES].unsqueeze(1).broadcast_to([P, E, TILES]), ALU.is_gt))
                step(eng.tensor_reduce(ends[:, 0, :], cmp_n[:, :, :], AX_X, ALU.add))
                step(eng.tensor_scalar(ends[:, 1, :], ends[:, 0, :], float(P), None, ALU.mult))
                step(eng.tensor_copy(ends[:, 3, :], ends[:, 1, :]))
                x, y, sh = 1, 2, 1
                while sh < E:
                    step(eng.tensor_copy(ends[:, y, 0:sh], ends[:, x, 0:sh]))
                    step(eng.tensor_tensor(ends[:, y, sh:E], ends[:, x, sh:E], ends[:, x, 0:E - sh], ALU.add))
                    x, y, sh = y, x, 2 * sh
                step(eng.tensor_tensor(ends[:, y, :], ends[:, x, :], ends[:, 3, :], ALU.subtract))
                step(eng.tensor_tensor(place[:, :, :], a[:, :, :], total, ALU.subtract))
                step(eng.tensor_tensor(place[:, :, :], place[:, :, :], before, ALU.add))
                step(eng.tensor_tensor(place[:, :, :], place[:, :, :],
                                       ends[:, y, :].unsqueeze(1).broadcast_to([P, TILES, E]), ALU.add))
                for k, h in enumerate((hot0, hot1)):
                    step(eng.tensor_tensor(h[:, :, :], h[:, :, :], place[:, :, :], ALU.mult))
                    step(eng.tensor_reduce(slot_f[:, k * TILES:(k + 1) * TILES], h[:, :, :], AX_X, ALU.add))
                step(eng.tensor_copy(slot[:, :], slot_f[:, :]))
                for t in range(TILES):
                    if t >= 4:
                        eng.wait_ge(scat[t % 4], 32 * (t // 4))
                    normed(t).then_inc(s["again"], 1)
                step(eng.tensor_tensor(cmp_t[:, :, :], ends[:, x, :].unsqueeze(1).broadcast_to([P, SORT_TILES, E]),
                                       tf[:, 0:SORT_TILES].unsqueeze(2).broadcast_to([P, SORT_TILES, E]), ALU.is_le))
                step(eng.tensor_reduce(te_f[:, :], cmp_t[:, :, :], AX_X, ALU.add))
                step(eng.tensor_scalar(te_f[:, :], te_f[:, :], float(E - 1), None, ALU.min))
                step(eng.tensor_copy(tile_expert[:, :], te_f[0:1, :]))

        with ExitStack() as ectx:
            NI = len(IC)
            xs = [sb(f"xs{i}", [P, D], where=ectx) for i in range(4)]
            xT = [sb(f"xT{i}", [P, KD, P], where=ectx) for i in range(2)]
            act_g = [sb(f"act_g{i}", [P, EI], where=ectx) for i in range(2)]
            hT = [sb(f"moe_hT{i}", [P, NI, P], where=ectx) for i in range(2)]
            ys = [sb(f"ys{i}", [P, D], where=ectx) for i in range(2)]
            bank = [ectx.enter_context(nc.psum_tensor(f"ex_bank{i}", [P, 512], F32)) for i in range(8)]
            xT_ps, gate_ps, up_ps, hT_ps, y_ps = bank[0], bank[1:3], bank[3:5], bank[5], bank[6:8]
            s = {n: ectx.enter_context(nc.semaphore("ex_" + n)) for n in (
                "xs0", "xs1", "xT_ps", "xT", "gate_ps", "up_ps", "silu", "h", "hT_ps", "hT", "y_ps", "y", "ys0", "ys1",
                "got0", "got1", "sum", "out")}
            xs_s, ys_s, got = ([s[n + "0"], s[n + "1"]] for n in ("xs", "ys", "got"))
            gat = xs
            block = ectx.enter_context(nc.Block())

            def ahead(body, eng):
                n = (SORT_TILES - 3) // 2
                with eng.Fori(0, n) as i:
                    for v in range(2):
                        body(i * 2 + v, v)
                for j in range(2 * n, SORT_TILES):
                    body(j, j % 2)

            @block.sync
            def _(eng):
                def load(j, v):
                    eng.wait_ge(s["xT_ps"], j + 1)
                    eng.dma_start(xs[v][:, :], dr["sorted"][bass.ds(j * P, P), :]).then_inc(xs_s[v], 16)

                def body(j, v):
                    if not (isinstance(j, int) and j + 2 >= SORT_TILES):
                        load(j + 2, v)
                    eng.wait_ge(s["y"], j + 3)
                    eng.dma_start(dr["done"][bass.ds(j * P, P), :], ys[v][:, :]).then_inc(ys_s[v], 16)

                load(0, 0)
                load(1, 1)
                ahead(body, eng)
                for t in range(TILES):
                    eng.wait_ge(s["sum"], 2 * t + 2)
                    eng.dma_start(out_d[bass.ds(t * P, P), :], acc[:, t, :]).then_inc(s["out"], 16)
                eng.wait_ge(s["out"], 16 * TILES)

            @block.gpsimd
            def _(eng):
                for name, n in (("xT_ps", 2), ("xT", 1), ("silu", 2), ("h", 2), ("gate_ps", 2), ("hT_ps", 2),
                                ("hT", 1), ("y_ps", 2), ("y", 2), ("ys0", 16), ("ys1", 16)):
                    eng.sem_inc(s[name], n)
                for v in range(2):
                    eng.wait_ge(ys_s[v], 16 + 16 * ((SORT_TILES + 1 - v) // 2))
                for t in range(TILES):
                    for k in range(2):
                        v = 2 * (t % 2) + k
                        if t >= 2:
                            eng.wait_ge(s["sum"], 2 * (t - 2) + k + 1)
                        eng.indirect_dma_start(out=gat[v][:, :], out_offset=None, in_=dr["done"][:, :],
                                               in_offset=bass.IndirectOffsetOnAxis(ap=slot[:, k * TILES + t:k * TILES + t + 1], axis=0))\
                           .then_inc(got[t % 2], 16)

            @block.scalar
            def _(eng):
                def turned(j, v):
                    eng.wait_ge(s["xT_ps"], j + 3)
                    eng.wait_ge(s["gate_ps"], j + 1)
                    eng.activation(xT[v][:, :, :].rearrange("p k n -> p (k n)"), xT_ps[:, :], ACT.Copy)\
                       .then_inc(s["xT"], 1)

                def gate(j, v):
                    eng.wait_ge(s["gate_ps"], j + 3)
                    eng.wait_ge(s["hT_ps"], j + 1)
                    eng.activation(act_g[v][:, :], gate_ps[v][:, 0:EI], ACT.Silu).then_inc(s["silu"], 1)

                def y_out(j, v):
                    eng.wait_ge(s["y_ps"], j + 3)
                    eng.wait_ge(ys_s[v], (j - v) * 8 + 16)
                    eng.activation(ys[v][:, :], y_ps[v][:, :], ACT.Copy).then_inc(s["y"], 1)

                turned(0, 0)
                gate(0, 0)
                turned(1, 1)

                def body(j, v):
                    last = isinstance(j, int)
                    if not (last and j + 1 >= SORT_TILES):
                        gate(j + 1, 1 - v)
                    if not (last and j + 2 >= SORT_TILES):
                        turned(j + 2, v)
                    y_out(j, v)

                ahead(body, eng)

            @block.vector
            def _(eng):
                def product(j, v):
                    eng.wait_ge(s["silu"], j + 3)
                    eng.wait_ge(s["up_ps"], j + 1)
                    eng.tensor_tensor(act_g[v][:, :], act_g[v][:, :], up_ps[v][:, 0:EI], ALU.mult).then_inc(s["h"], 1)

                def turned(j, v):
                    eng.wait_ge(s["hT_ps"], j + 3)
                    eng.wait_ge(s["y_ps"], j + 1)
                    for c, (i, n) in enumerate(IC):
                        if n == P and c == 0:
                            full = EI // P
                            eng.tensor_copy(hT[v][:, 0:full, :].rearrange("p c n -> p (c n)"), hT_ps[:, 0:full * P])
                        elif n < P:
                            eng.tensor_copy(hT[v][0:n, c, :], hT_ps[0:n, c * P:(c + 1) * P]).then_inc(s["hT"], 1)

                product(0, 0)

                def body(j, v):
                    turned(j, v)
                    if not (isinstance(j, int) and j + 1 >= SORT_TILES):
                        product(j + 1, 1 - v)

                ahead(body, eng)
                for t in range(TILES):
                    eng.wait_ge(got[t % 2], 32 * (t // 2 + 1))
                    for k in range(2):
                        if k:
                            eng.wait_ge(s["sum"], 2 * t + 1)
                        eng.scalar_tensor_tensor(acc[:, t, :], gat[2 * (t % 2) + k][:, :], weight[:, k, t:t + 1],
                                                 acc[:, t, :], ALU.mult, ALU.add).then_inc(s["sum"], 1)

            @block.tensor
            def _(eng):
                eng.wait_ge(s_w, 16 * NW)

                def turn_rows(j, v):
                    eng.wait_ge(xs_s[v], (j - v) * 8 + 16)
                    eng.wait_ge(s["xT"], j + 1)
                    for k in range(KD):
                        last = eng.transpose(xT_ps[:, k * P:(k + 1) * P], xs[v][:, k * P:(k + 1) * P], ident[:, :])
                    last.then_inc(s["xT_ps"], 1)

                def width(j, v):
                    e = eng.value_load(tile_expert[0:1, bass.ds(j, 1)], min_val=0, max_val=E - 1)
                    eng.wait_ge(s["xT"], j + 2)
                    for i, (ps, free, done) in enumerate(((gate_ps[v], "silu", "gate_ps"), (up_ps[v], "h", "up_ps"))):
                        eng.wait_ge(s[free], j + 1)
                        for k in range(KD):
                            mm = eng.matmul(ps[:, 0:EI], xT[v][:, k, :],
                                            w_gu[:, i, bass.ds(e * KD + k, 1), :].rearrange("p a n -> p (a n)"),
                                            start=(k == 0), stop=(k == KD - 1))
                        mm.then_inc(s[done], 1)
                    return e

                def turn_width(j, v):
                    eng.wait_ge(s["h"], j + 3)
                    eng.wait_ge(s["hT"], j + 1)
                    for c, (i, n) in enumerate(IC):
                        last = eng.transpose(hT_ps[0:n, c * P:(c + 1) * P], act_g[v][:, i:i + n], ident[:, :])
                    last.then_inc(s["hT_ps"], 1)

                def out(j, v):
                    e = eng.value_load(tile_expert[0:1, bass.ds(j, 1)], min_val=0, max_val=E - 1)
                    eng.wait_ge(s["hT"], j + 2)
                    eng.wait_ge(s["y"], j + 1)
                    for c, (i, n) in enumerate(IC):
                        mm = eng.matmul(y_ps[v][:, :], hT[v][0:n, c, :],
                                        w_dn[0:n, bass.ds(e * NI + c, 1), :].rearrange("p a n -> p (a n)"),
                                        start=(c == 0), stop=(c == NI - 1))
                    mm.then_inc(s["y_ps"], 1)

                turn_rows(0, 0)
                width(0, 0)
                turn_rows(1, 1)

                def body(j, v):
                    last = isinstance(j, int)
                    turn_width(j, v)
                    if not (last and j + 1 >= SORT_TILES):
                        width(j + 1, 1 - v)
                    if not (last and j + 2 >= SORT_TILES):
                        turn_rows(j + 2, v)
                    out(j, v)

                ahead(body, eng)


def mixer_ffn_experts_kernel(nc, ins, out):
    out_d = out.rearrange("b s d -> (b s) d")
    dr = {name: nc.dram_tensor(name + "_rows", (n, D), F32, kind="Internal").ap()
          for name, n in (("xh", ROWS), ("h2", ROWS), ("sorted", SORT_TILES * P), ("done", SORT_TILES * P))}
    with nc.sbuf_tensor("ident", [P, P], F32) as ident, nc.sbuf_tensor("ones", [P, P], F32) as ones:
        constants(nc, ident, ones)
        mixer(nc, ins, dr, ident, ones)
        with nc.sbuf_tensor("acc_rows", [P, TILES, D], F32) as acc:
            feed_forward(nc, ins, dr, ident, acc)
            experts(nc, ins, dr, out_d, ident, ones, acc)


_INS = ["L0_attn_hidden_states", "L0_attn_in_proj_w", "L0_attn_conv_w", "L0_attn_conv_b", "L0_attn_dt_bias",
        "L0_attn_A_log", "L0_attn_D", "L0_attn_norm_w", "L0_attn_out_proj_w", "L0_attn_ln1_w", "L0_attn_ln2_w",
        "L0_attn_gate_w", "L0_attn_up_w", "L0_attn_down_w", "L0_ffn_Wr", "L0_ffn_Wg", "L0_ffn_Wu", "L0_ffn_Wd"]
_OUT = ((1, ROWS, D), "float32")


def kernel(**inputs):
    import numpy as _np
    import concourse.bacc as _bacc
    from concourse import mybir as _mybir
    from concourse.bass_utils import run_bass_kernel_spmd as _run

    nc = _bacc.Bacc("TRN2", target_bir_lowering=False, num_devices=1)
    arrays, ins = {}, {}
    for name in _INS:
        a = _np.ascontiguousarray(inputs[name])
        arrays[f"in_{name}_dram"] = a
        ins[name] = nc.dram_tensor(f"in_{name}_dram", a.shape, _mybir.dt.from_np(a.dtype), kind="ExternalInput").ap()
    out = nc.dram_tensor("out_0_dram", _OUT[0], _mybir.dt.from_np(_np.dtype(_OUT[1])), kind="ExternalOutput").ap()
    mixer_ffn_experts_kernel(nc, ins, out)
    r = _run(nc, [arrays], core_ids=[0])
    return r.results[0]["out_0_dram"]
```

```python
from contextlib import ExitStack

import concourse.bass as bass
from concourse import mybir

F32 = mybir.dt.float32
F32R = mybir.dt.float32r
U32 = mybir.dt.uint32
ALU = mybir.AluOpType
ACT = mybir.ActivationFunctionType
AX_X = mybir.AxisListType.X

P = 128
EPS = 1e-5
ROWS = 2048
D = 512
KD = D // P
DI = 1024
HEADS, HD, DST, NG = 16, 64, 64, 4
HPG = HEADS // NG
DXB = NG * HD
NCH = (2 * DXB + DI) // P
TAPS = 4
DIN = DI + 2 * DXB + DI + HEADS
CH0 = DI
DT0 = DIN - HEADS
TILES = ROWS // P
GR = 256
NGRP = ROWS // GR
FF, FB = 2048, 256
E, EI = 8, 352
MASKED = -1.0e30
SORT_TILES = 2 * ROWS // P + E - 1
IC = [(i, min(P, EI - i)) for i in range(0, EI, P)]


def softplus_dt_steps():
    return [1.0 / n for n in (13, 11, 9, 7, 5, 3)]


def mixer(nc, ins, dr, ident, ones):
    x_d = ins["L0_attn_hidden_states"].rearrange("b s d -> (b s) d")
    with ExitStack() as ctx:
        def sb(name, shape, dt=F32):
            return ctx.enter_context(nc.sbuf_tensor(name, shape, dt))

        def sem(name):
            return ctx.enter_context(nc.semaphore(name))

        w_in = sb("w_in", [P, KD, DIN])
        w_out = sb("w_out", [P, DI // P, D])
        ln1 = sb("ln1", [P, KD])
        ln2_row = sb("ln2_row", [P, D])
        normw = sb("normw", [P, DI // P])
        conv_w = sb("conv_w", [P, NCH, TAPS])
        conv_b = sb("conv_b", [P, NCH])
        a_neg = sb("a_neg", [P, HEADS])
        dt_bias = sb("dt_bias", [P, HEADS])
        d_skip = sb("d_skip", [P, HEADS])
        tri = sb("tri", [P, P])
        suffix = sb("suffix", [P, P])
        mask = sb("mask", [P, P])
        tri_r = sb("tri_r", [P, P], F32R)
        ident_r = sb("ident_r", [P, P], F32R)
        mask_r = sb("mask_r", [P, P], F32R)
        half_neg = sb("half_neg", [P, 1])
        xin = sb("xin", [P, 2, D])
        bn = sb("bn", [P, 2, 6])
        mv = sb("mv", [P, 2, 2, 2])
        lnq = sb("lnq", [P, 2, 2, 4])
        hT = [sb(f"hT{i}", [P, KD, GR]) for i in range(2)]
        halo = sb("halo", [P, NCH, TAPS - 1])
        raw = [sb(f"raw{i}", [P, TAPS - 1 + GR]) for i in range(3)]
        acc = [sb(f"acc{i}", [P, GR]) for i in range(3)]
        tnh = [sb(f"tnh{i}", [P, GR]) for i in range(2)]
        cv = [sb(f"cv{i}", [P, NCH, GR]) for i in range(2)]
        sp = sb("sp", [P, 8, 2 * HEADS])
        dt = [sb(f"dt{i}", [P, 2, HEADS]) for i in range(2)]
        da = sb("da", [P, 2, HEADS])
        da_hi = [sb(f"da_hi{i}", [P, 2, HEADS], F32R) for i in range(2)]
        da_lo = [sb(f"da_lo{i}", [P, 2, HEADS], F32R) for i in range(2)]
        neg_cum = [sb(f"neg_cum{i}", [P, 2, HEADS]) for i in range(2)]
        exp_cum = [sb(f"exp_cum{i}", [P, 2, HEADS]) for i in range(2)]
        exp_suf = [sb(f"exp_suf{i}", [P, 2, HEADS]) for i in range(2)]
        chunk_decay = [sb(f"chunk_decay{i}", [P, 2, 2, HPG]) for i in range(2)]
        zs = sb("zs", [P, DI])
        xb_row = sb("xb_row", [P, 2, DXB])
        xdt = sb("xdt", [P, DI])
        dx = sb("dx", [P, DI])
        xdd = sb("xdd", [P, DI])
        decay = [sb(f"decay{i}", [P, HPG, P]) for i in range(2)]
        yrow = sb("yrow", [P, DI])
        yoff = sb("yoff", [P, HPG * HD])
        junk = sb("junk", [P, 3, D], mybir.dt.bfloat16)
        sumsq = sb("sumsq", [P, 8])
        carry = sb("carry", [P, 2, HPG, HD])
        yT = sb("yT", [P, DI // P, P])
        xres = [sb(f"xres{i}", [P, D]) for i in range(2)]
        yres = sb("yres", [P, D])
        hres = sb("hres", [P, D])
        h2 = sb("h2", [P, D])

        bank = [ctx.enter_context(nc.psum_tensor(f"mix_bank{i}", [P, 512], F32)) for i in range(8)]
        proj_ps, seg_ps, y_ps, cb_ps, misc = bank[0:2], bank[2:4], bank[4:6], bank[6], bank[7]

        s = {n: sem(n) for n in (
            "v_dma", "wa_dma", "wc_dma", "wz_dma", "wo_dma", "xin_dma", "xres_dma0", "xres_dma1",
            "xh_stored0", "xh_stored1", "h2_stored", "consts", "cast", "a_exp", "folded",
            "bn", "stat", "lnq_step", "normed", "rowT", "hT_done",
            "dt_ps", "dt_v", "dt_neg", "dt_exp", "dt_step", "dt_done", "cum_ps", "cum_done",
            "ch_ps", "halo", "ch_copied", "tap", "ch_tanh", "ch_done",
            "z_ps", "z_tanh", "z_gate", "xb_ps", "xb_row", "xdt", "dx", "xdd",
            "seg0", "seg1", "cb", "exp0", "exp1", "sc0", "sc1", "yd0", "yd1", "yo0", "yo1", "yread0", "yread1",
            "yread_a", "ysum", "ygate", "state_ps", "carry_decayed", "carry_done", "sq", "r_step",
            "yT_ps", "yT_done", "out_ps", "yres", "h_done", "xh_done", "hsq", "h2_step", "passed")}
        seg_s, exp_s, sc_s, yd_s, yread_s = (
            [s[n + "0"], s[n + "1"]] for n in ("seg", "exp", "sc", "yd", "yread"))
        xres_dma, xh_stored = ([s[n + "0"], s[n + "1"]] for n in ("xres_dma", "xh_stored"))
        NLN, NDT, NR, NH2 = 6, 14, 4, 4

        def wait_apart(eng, which, value):
            eng.wait_ge(which, value)
            eng.sem_inc(s["passed"], 1)

        def head_cols(t, g):
            return t[:, g * HPG * HD:(g + 1) * HPG * HD]

        def vector_loads(cw, cb, nb):
            loads = [(ln1[:, :], ins["L0_attn_ln1_w"].rearrange("(k p) -> p k", p=P)),
                     (normw[:, :], ins["L0_attn_norm_w"].rearrange("(k p) -> p k", p=P)),
                     (a_neg[:, :], ins["L0_attn_A_log"].partition_broadcast(P)),
                     (dt_bias[:, :], ins["L0_attn_dt_bias"].partition_broadcast(P)),
                     (d_skip[:, :], ins["L0_attn_D"].partition_broadcast(P)),
                     (ln2_row[:, :], ins["L0_attn_ln2_w"].partition_broadcast(P)),
                     (conv_w[:, 0:nb, :], cw[0:2 * DXB, :].rearrange("(k p) t -> p k t", p=P)),
                     (conv_b[:, 0:nb], cb[0:2 * DXB].rearrange("(k p) -> p k", p=P))]
            for a in range(2):
                for b in range(2):
                    half, at, src = slice(b * HD, (b + 1) * HD), nb + HPG * a, 2 * DXB + (2 * a + b) * HPG * DST
                    loads += [(conv_w[half, at:at + HPG, :],
                               cw[src:src + HPG * DST, :].rearrange("(j n) t -> n j t", j=HPG)),
                              (conv_b[half, at:at + HPG],
                               cb[src:src + HPG * DST].rearrange("(j n) -> n j", j=HPG))]
            return loads

        NV = 16
        block = ctx.enter_context(nc.Block())


        def slots(run, eng):
            run(0, 0, True, False)
            with eng.Fori(0, (TILES - 4) // 4) as i:
                for k in range(1, 5):
                    run(i, k, True, k % 2 == 1)
            for k in range(1, 4):
                run(TILES // 4 - 1, k, k < 2, False)

        def first(i, k):
            return k == 0

        def last_chunk(i, k):
            return isinstance(i, int) and 4 * i + k == TILES - 1

        @block.sync
        def _(eng):
            def load_pre(g):
                for u in range(2):
                    eng.dma_start(xin[:, u, :], x_d[bass.ds((g * 2 + u) * P, P), :]).then_inc(s["xin_dma"], 16)

            def load_xres(c, b):
                eng.dma_start(xres[b][:, :], x_d[bass.ds(c * P, P), :]).then_inc(xres_dma[b], 16)

            load_pre(0)
            cw, cb = ins["L0_attn_conv_w"], ins["L0_attn_conv_b"]
            nb = 2 * DXB // P
            for dst, src in vector_loads(cw, cb, nb):
                with nc.allow_non_contiguous_dma("small vectors"):
                    eng.dma_start(dst, src).then_inc(s["v_dma"], 16)
            wr = ins["L0_attn_in_proj_w"].rearrange("(k p) n -> p k n", p=P)
            c0 = CH0 + 2 * DXB
            eng.dma_start(w_in[:, :, DT0:DIN], wr[:, :, DT0:DIN]).then_inc(s["wa_dma"], 16)
            eng.dma_start(w_in[:, :, CH0:c0], wr[:, :, CH0:c0]).then_inc(s["wa_dma"], 16)
            for k in range(KD):
                for a in range(2):
                    for b in range(2):
                        lo, src = c0 + a * DI // 2, c0 + (2 * a + b) * HPG * DST
                        eng.dma_start(
                            w_in[:, k, lo:lo + DI // 2].rearrange("p (j b n) -> p j b n", j=HPG, b=2)[:, :, b, :],
                            wr[:, k, src:src + HPG * DST].rearrange("p (j n) -> p j n", j=HPG)
                        ).then_inc(s["wc_dma"], 16)
            eng.wait_ge(s["rowT"], 2)
            load_pre(1)
            eng.dma_start(w_in[:, :, 0:DI], wr[:, :, 0:DI]).then_inc(s["wz_dma"], 16)
            for b in range(2):
                load_xres(b, b)
            eng.dma_start(w_out[:, :, :], ins["L0_attn_out_proj_w"].rearrange("(k p) n -> p k n", p=P))\
               .then_inc(s["wo_dma"], 16)

            def slot(i, k, front, pre):
                c, gf = i * 4 + k, i * 2 + k // 2 + 1
                if pre:
                    eng.wait_ge(s["rowT"], gf * 2 + 2)
                    load_pre(gf + 1)
                if first(i, k):
                    return
                b, n = (k - 1) % 2, i * 32 + (k - 1) // 2 * 16
                eng.wait_ge(s["xh_done"], c)
                eng.dma_start(dr["xh"][bass.ds((c - 1) * P, P), :], xres[b][:, :]).then_inc(xh_stored[b], 16)
                if not last_chunk(i, k):
                    eng.wait_ge(xh_stored[b], n + 16)
                    load_xres(c + 1, b)
                eng.wait_ge(s["h2_step"], (c - 1) * NH2 + NH2 + 1)
                eng.dma_start(dr["h2"][bass.ds((c - 1) * P, P), :], h2[:, :]).then_inc(s["h2_stored"], 16)

            slots(slot, eng)
            eng.wait_ge(s["xh_done"], TILES)
            eng.dma_start(dr["xh"][(TILES - 1) * P:ROWS, :], xres[(TILES - 1) % 2][:, :])\
               .then_inc(xh_stored[(TILES - 1) % 2], 16)
            eng.wait_ge(s["h2_step"], TILES * NH2 + 1)
            eng.dma_start(dr["h2"][(TILES - 1) * P:ROWS, :], h2[:, :]).then_inc(s["h2_stored"], 16)
            for b in range(2):
                eng.wait_ge(xh_stored[b], 16 * TILES // 2)
            eng.wait_ge(s["h2_stored"], 16 + 16 * TILES)

        @block.gpsimd
        def _(eng):
            for name, n in (("h2_stored", 16), ("ch_done", 3), ("h_done", 1), ("sc0", 1), ("sc1", 1),
                            ("exp0", 1), ("exp1", 1), ("yread0", 1), ("yread1", 1), ("yd0", 1), ("yd1", 1),
                            ("xdd", 1),
                            ("ygate", 2), ("yT_ps", 2), ("out_ps", 1), ("state_ps", 1), ("carry_done", 1),
                            ("ysum", 4), ("xdt", 1), ("h2_step", 1)):
                eng.sem_inc(s[name], n)
            eng.memset(tri[:, :], 1.0).then_inc(s["consts"], 1)
            eng.memset(suffix[:, :], 1.0).then_inc(s["consts"], 1)
            eng.memset(mask[:, :], 0.0).then_inc(s["consts"], 1)
            eng.memset(half_neg[:, :], -0.5).then_inc(s["consts"], 1)
            eng.memset(halo[:, :, :], 0.0).then_inc(s["consts"], 1)
            eng.memset(carry[:, :, :, :], 0.0).then_inc(s["consts"], 1)
            eng.wait_ge(s["consts"], 6)
            eng.affine_select(out=tri[:, :], in_=tri[:, :], compare_op=ALU.is_ge, fill=0.0, base=0,
                              pattern=[[1, P]], channel_multiplier=-1).then_inc(s["consts"], 1)
            eng.affine_select(out=suffix[:, :], in_=suffix[:, :], compare_op=ALU.is_gt, fill=0.0, base=0,
                              pattern=[[-1, P]], channel_multiplier=1).then_inc(s["consts"], 1)
            eng.affine_select(out=mask[:, :], in_=mask[:, :], compare_op=ALU.is_ge, fill=MASKED, base=0,
                              pattern=[[1, P]], channel_multiplier=-1).then_inc(s["consts"], 1)

            def norms(g, par):
                for u in range(2):
                    n = (g * 2 + u) * NLN
                    v, q = mv[:, par, u, 1:2], lnq[:, par, u, :]
                    wait_apart(eng, s["stat"], g * 2 + u + 1)
                    steps = [lambda: eng.tensor_scalar(q[:, 0:1], v, EPS, None, ALU.add),
                             lambda: eng.tensor_tensor(q[:, 1:2], q[:, 0:1], half_neg[:, :], ALU.pow),
                             lambda: eng.tensor_tensor(q[:, 0:1], q[:, 1:2], q[:, 1:2], ALU.mult),
                             lambda: eng.tensor_scalar(q[:, 0:1], q[:, 0:1], v, EPS, ALU.mult, ALU.add),
                             lambda: eng.tensor_tensor(q[:, 2:3], q[:, 0:1], half_neg[:, :], ALU.pow),
                             lambda: eng.tensor_tensor(q[:, 3:4], q[:, 1:2], q[:, 2:3], ALU.mult)]
                    for i, step in enumerate(steps):
                        if i:
                            wait_apart(eng, s["lnq_step"], n + i)
                        step().then_inc(s["lnq_step"], 1)

            norms(0, 0)
            eng.wait_ge(s["v_dma"], 16 * NV)
            norms(1, 1)

            def scaled_x(i, k):
                c, g, u, par = i * 4 + k, i * 2 + k // 2, k % 2, (k // 2) % 2
                hb = lambda t: t.unsqueeze(2).broadcast_to([P, HEADS, HD])
                xr = xb_row[:, 0, :].rearrange("p (g d) -> p g d", g=NG).unsqueeze(2).broadcast_to([P, NG, HPG, HD])
                eng.wait_ge(s["xb_row"], c + 1)
                eng.wait_ge(s["ysum"], c * 4 + 4)
                eng.tensor_tensor(dx[:, :].rearrange("p (g r d) -> p g r d", g=NG, r=HPG), xr,
                                  d_skip[:, :].rearrange("p (g r) -> p g r", g=NG).unsqueeze(3)
                                  .broadcast_to([P, NG, HPG, HD]), ALU.mult).then_inc(s["dx"], 1)
                eng.wait_ge(s["xdt"], c + 2)
                eng.wait_ge(s["cum_done"], g + 1)
                eng.wait_ge(s["state_ps"], c + 1)
                eng.tensor_tensor(xdd[:, :].rearrange("p (h d) -> p h d", h=HEADS),
                                  xdt[:, :].rearrange("p (h d) -> p h d", h=HEADS),
                                  hb(exp_suf[par][:, u, :]), ALU.mult).then_inc(s["xdd"], 1)

            def norm_scale(e):
                n = e * NR
                eng.wait_ge(s["sq"], e * 2 + 2)
                a = sumsq[:, 2:3]
                steps = [lambda: eng.tensor_tensor(a, sumsq[:, 0:1], sumsq[:, 1:2], ALU.add),
                         lambda: eng.tensor_scalar(a, a, 0.25 / DI, EPS, ALU.mult, ALU.add),
                         lambda: eng.tensor_tensor(a, a, half_neg[:, :], ALU.pow),
                         lambda: eng.tensor_scalar(sumsq[:, 3:4], a, 0.5, None, ALU.mult)]
                for i, step in enumerate(steps):
                    if i:
                        wait_apart(eng, s["r_step"], n + i)
                    step().then_inc(s["r_step"], 1)

            def residual(e, b):
                eng.wait_ge(s["h_done"], e + 2)
                eng.tensor_tensor(xres[b][:, :], hres[:, :], xres[b][:, :], ALU.add).then_inc(s["xh_done"], 1)

            def second_norm(e):
                n = e * NH2
                wait_apart(eng, s["hsq"], e + 1)
                b = sumsq[:, 5:6]
                steps = [lambda: eng.tensor_scalar(b, sumsq[:, 4:5], 1.0 / D, EPS, ALU.mult, ALU.add),
                         lambda: eng.tensor_tensor(b, b, half_neg[:, :], ALU.pow),
                         lambda: eng.tensor_scalar(h2[:, :], hres[:, :], b, None, ALU.mult),
                         lambda: eng.tensor_tensor(h2[:, :], h2[:, :], ln2_row[:, :], ALU.mult)]
                for i, step in enumerate(steps):
                    if i == 2:
                        wait_apart(eng, s["h2_stored"], e * 16 + 16)
                    if i:
                        wait_apart(eng, s["h2_step"], n + i + 1)
                    step().then_inc(s["h2_step"], 1)

            scaled_x(0, 0)

            def slot(i, k, front, pre):
                c, gf, u, par = i * 4 + k, i * 2 + k // 2 + 1, k % 2, (k // 2) % 2
                if not first(i, k):
                    norm_scale(c - 1)
                    residual(c - 1, (k - 1) % 2)
                if pre:
                    norms(gf + 1, par)
                if not first(i, k):
                    second_norm(c - 1)
                eng.wait_ge(s["yd1"], c * 2 + 3)
                eng.wait_ge(s["carry_done"], c + 1)
                eng.tensor_tensor(carry[:, :, :, :].rearrange("p a j d -> p (a j) d"),
                                  carry[:, :, :, :].rearrange("p a j d -> p (a j) d"),
                                  chunk_decay[par][:, u, :, :].rearrange("p a j -> p (a j)").unsqueeze(2)
                                  .broadcast_to([P, 2 * HPG, HD]), ALU.mult).then_inc(s["carry_decayed"], 1)
                if not last_chunk(i, k):
                    scaled_x(i, k + 1)

            slots(slot, eng)
            norm_scale(TILES - 1)
            residual(TILES - 1, (TILES - 1) % 2)
            second_norm(TILES - 1)

        @block.scalar
        def _(eng):
            eng.wait_ge(s["v_dma"], 16 * NV)
            eng.activation(a_neg[:, :], a_neg[:, :], ACT.Exp).then_inc(s["a_exp"], 1)

            def copy_hT(g, par, u):
                eng.wait_ge(s["rowT"], g * 2 + u + 1)
                eng.activation(hT[par][:, :, u * P:(u + 1) * P], misc[:, :].rearrange("p (k n) -> p k n", k=KD),
                               ACT.Copy).then_inc(s["hT_done"], 1)

            def dt_exp(g):
                eng.wait_ge(s["dt_neg"], g + 1)
                eng.activation(sp[:, 2, :], sp[:, 1, :], ACT.Exp).then_inc(s["dt_exp"], 1)

            def cum_exps(g, par):
                eng.wait_ge(s["cum_ps"], g + 1)
                f = lambda t: t[:, :, :].rearrange("p u h -> p (u h)")
                eng.activation(f(neg_cum[par]), misc[:, 0:32], ACT.Copy, scale=-1.0)
                eng.activation(f(exp_cum[par]), misc[:, 0:32], ACT.Exp)
                eng.activation(f(exp_suf[par]), misc[:, 32:64], ACT.Exp)
                for b in range(2):
                    h = slice(b * HD, (b + 1) * HD)
                    tot = misc[h, 64:96].rearrange("p (u a b j) -> p (u a) b j", u=2, a=2, b=2)[:, :, b, :]
                    last = eng.activation(chunk_decay[par][h, :, :, :].rearrange("p u a j -> p (u a) j"), tot, ACT.Exp)
                last.then_inc(s["cum_done"], 1)

            def copy_ch(g, ch):
                n = g * NCH + ch
                eng.wait_ge(s["ch_ps"], n + 1)
                eng.wait_ge(s["ch_done"], n + 1)
                ps = proj_ps[ch % 2][:, 0:GR]
                eng.activation(raw[ch % 3][:, 0:TAPS - 1], halo[:, ch, :], ACT.Copy).then_inc(s["halo"], 1)
                eng.activation(acc[ch % 3][:, :], ps, ACT.Identity, bias=conv_b[:, ch:ch + 1],
                               scale=conv_w[:, ch, TAPS - 1:TAPS])
                eng.wait_ge(s["halo"], n + 1)
                eng.activation(halo[:, ch, :], proj_ps[ch % 2][:, GR - TAPS + 1:GR], ACT.Copy)
                eng.activation(raw[ch % 3][:, TAPS - 1:TAPS - 1 + GR], ps, ACT.Copy).then_inc(s["ch_copied"], 1)

            def tanh_ch(g, ch):
                n = g * NCH + ch
                eng.wait_ge(s["tap"], n * 3 + 3)
                eng.wait_ge(s["ch_done"], n + 2)
                eng.activation(tnh[ch % 2][:, :], acc[ch % 3][:, :], ACT.Tanh).then_inc(s["ch_tanh"], 1)

            eng.wait_ge(s["consts"], 9)
            for u in range(2):
                copy_hT(0, 0, u)
            eng.wait_ge(s["folded"], 1)
            dt_exp(0)
            cum_exps(0, 0)
            for ch in range(NCH):
                copy_ch(0, ch)
                if ch:
                    tanh_ch(0, ch - 1)
            tanh_ch(0, NCH - 1)
            for u in range(2):
                copy_hT(1, 1, u)

            def next_rows(c):
                for j in range(2):
                    eng.wait_ge(s["z_ps"], c * 2 + j + 1)
                    eng.wait_ge(s["ygate"], c * 2 + j + 1)
                    eng.activation(zs[:, j * 512:(j + 1) * 512], proj_ps[j][:, :], ACT.Tanh, scale=0.5)\
                       .then_inc(s["z_tanh"], 1)
                eng.wait_ge(s["xb_ps"], c + 1)
                eng.wait_ge(s["xdd"], c + 1)
                eng.wait_ge(s["state_ps"], c + 1)
                eng.activation(xb_row[:, :, :].rearrange("p a d -> p (a d)"), misc[:, :], ACT.Copy)\
                   .then_inc(s["xb_row"], 1)

            def turned(e, j):
                eng.wait_ge(s["yT_ps"], e * 2 + j + 3)
                eng.wait_ge(s["out_ps"], e + 1)
                eng.activation(yT[:, j * 4:j * 4 + 4, :].rearrange("p k n -> p (k n)"), misc[:, :], ACT.Copy)\
                   .then_inc(s["yT_done"], 1)

            def h_squares(e):
                eng.wait_ge(s["h_done"], e + 2)
                eng.activation(junk[:, 2, :], hres[:, :], ACT.Square, accum_out=sumsq[:, 4:5]).then_inc(s["hsq"], 1)

            next_rows(0)

            def slot(i, k, front, pre):
                c, gf, u, par = i * 4 + k, i * 2 + k // 2 + 1, k % 2, (k // 2) % 2
                half = u * (NCH // 2)

                def exps(hg):
                    eng.wait_ge(seg_s[hg % 2], c * 2 + hg // 2 + 1)
                    eng.wait_ge(yd_s[hg % 2], c * 2 + hg // 2 + 1)
                    for j in range(HPG):
                        last = eng.activation(decay[hg % 2][:, j, :], seg_ps[hg % 2][:, j * P:(j + 1) * P], ACT.Exp,
                                              bias=neg_cum[par][:, u, hg * HPG + j:hg * HPG + j + 1])
                    last.then_inc(exp_s[hg % 2], 1)

                exps(0)
                if not first(i, k):
                    turned(c - 1, 0)
                if front:
                    copy_ch(gf, half + 0)
                if not first(i, k):
                    turned(c - 1, 1)
                exps(1)
                if front:
                    tanh_ch(gf, half + 0)
                    copy_ch(gf, half + 1)
                if not first(i, k):
                    h_squares(c - 1)
                exps(2)
                if front:
                    tanh_ch(gf, half + 1)
                    if u == 0:
                        dt_exp(gf)
                    copy_ch(gf, half + 2)
                exps(3)
                if front:
                    tanh_ch(gf, half + 2)
                if pre:
                    copy_hT(gf + 1, par, 0)
                if front:
                    copy_ch(gf, half + 3)
                if pre:
                    copy_hT(gf + 1, par, 1)
                if front:
                    tanh_ch(gf, half + 3)
                    if u == 0:
                        cum_exps(gf, 1 - par)
                    for n in (4, 5):
                        copy_ch(gf, half + n)
                        tanh_ch(gf, half + n)
                for j in range(2):
                    eng.wait_ge(s["ygate"], c * 2 + j + 3)
                    eng.activation(junk[:, j, :], yrow[:, j * 512:(j + 1) * 512], ACT.Square,
                                   accum_out=sumsq[:, j:j + 1]).then_inc(s["sq"], 1)
                if not last_chunk(i, k):
                    next_rows(c + 1)

            slots(slot, eng)
            for j in range(2):
                turned(TILES - 1, j)
            h_squares(TILES - 1)

        @block.vector
        def _(eng):
            def norm_rows(g, par):
                for u in range(2):
                    eng.wait_ge(s["lnq_step"], (g * 2 + u + 1) * NLN)
                    eng.tensor_scalar(xin[:, u, :], xin[:, u, :], mv[:, par, u, 0:1], lnq[:, par, u, 3:4],
                                      ALU.subtract, ALU.mult).then_inc(s["normed"], 1)

            def rows_in(g, par):
                eng.wait_ge(s["xin_dma"], (g + 1) * 32)
                for u in range(2):
                    eng.bn_stats(bn[:, u, :], xin[:, u, :]).then_inc(s["bn"], 1)
                for u in range(2):
                    wait_apart(eng, s["bn"], g * 2 + u + 1)
                    eng.bn_aggr(mv[:, par, u, :], bn[:, u, :]).then_inc(s["stat"], 1)

            def dt_first(g):
                eng.wait_ge(s["dt_ps"], g + 1)
                eng.tensor_tensor(sp[:, 0, :].rearrange("p (u h) -> p u h", u=2),
                                  misc[:, 0:32].rearrange("p (u h) -> p u h", u=2),
                                  dt_bias[:, :].unsqueeze(1).broadcast_to([P, 2, HEADS]), ALU.add).then_inc(s["dt_v"], 1)
                eng.wait_ge(s["dt_v"], g + 1)
                eng.scalar_tensor_tensor(sp[:, 1, :], sp[:, 0, :], -1.0, sp[:, 0, :], ALU.mult, ALU.min)\
                   .then_inc(s["dt_neg"], 1)

            def dt_rest(g, par):
                v, e, q, ss, s2, pl = (sp[:, i, :] for i in (0, 2, 3, 4, 5, 6))
                flat = lambda t: t[:, :, :].rearrange("p u h -> p (u h)")
                eng.wait_ge(s["dt_exp"], g + 1)
                steps = [lambda: eng.tensor_scalar(q, e, 2.0, None, ALU.add),
                         lambda: eng.reciprocal(q, q),
                         lambda: eng.tensor_tensor(ss, e, q, ALU.mult),
                         lambda: eng.tensor_tensor(s2, ss, ss, ALU.mult),
                         lambda: eng.tensor_scalar(pl, s2, 1.0 / 15, None, ALU.mult)]
                for cf in softplus_dt_steps():
                    steps.append(lambda cf=cf: eng.scalar_tensor_tensor(pl, pl, cf, s2, ALU.add, ALU.mult))
                steps += [lambda: eng.scalar_tensor_tensor(pl, pl, 1.0, ss, ALU.add, ALU.mult),
                          lambda: eng.tensor_scalar(v, v, 0.0, None, ALU.max),
                          lambda: eng.scalar_tensor_tensor(flat(dt[par]), pl, 2.0, v, ALU.mult, ALU.add)]
                assert len(steps) == NDT
                for i, step in enumerate(steps):
                    if i:
                        eng.wait_ge(s["dt_step"], g * NDT + i)
                    step().then_inc(s["dt_step"], 1)
                eng.wait_ge(s["dt_step"], g * NDT + NDT)
                eng.tensor_tensor(da[:, :, :], dt[par][:, :, :], a_neg[:, :].unsqueeze(1).broadcast_to([P, 2, HEADS]),
                                  ALU.mult).then_inc(s["dt_done"], 1)
                eng.wait_ge(s["dt_done"], g * 3 + 1)
                eng.tensor_copy(da_hi[par][:, :, :], da[:, :, :]).then_inc(s["dt_done"], 1)
                eng.wait_ge(s["dt_done"], g * 3 + 2)
                eng.tensor_tensor(da_lo[par][:, :, :], da[:, :, :], da_hi[par][:, :, :].bitcast(F32),
                                  ALU.subtract).then_inc(s["dt_done"], 1)

            def taps(g, ch):
                n = g * NCH + ch
                eng.wait_ge(s["ch_copied"], n + 1)
                for t in range(TAPS - 1):
                    if t:
                        eng.wait_ge(s["tap"], n * 3 + t)
                    eng.scalar_tensor_tensor(acc[ch % 3][:, :], raw[ch % 3][:, t:t + GR], conv_w[:, ch, t:t + 1],
                                             acc[ch % 3][:, :], ALU.mult, ALU.add).then_inc(s["tap"], 1)

            def silu_ch(g, par, ch):
                n = g * NCH + ch
                eng.wait_ge(s["ch_tanh"], n + 1)
                eng.scalar_tensor_tensor(cv[par][:, ch, :], tnh[ch % 2][:, :], 1.0, acc[ch % 3][:, :],
                                         ALU.add, ALU.mult).then_inc(s["ch_done"], 1)

            def fold_in(lo, hi):
                for k in range(KD):
                    last = eng.tensor_scalar(w_in[:, k, lo:hi], w_in[:, k, lo:hi], ln1[:, k:k + 1], None, ALU.mult)
                last.then_inc(s["folded"], 1)

            rows_in(0, 0)
            norm_rows(0, 0)
            eng.wait_ge(s["v_dma"], 16 * NV)
            eng.tensor_scalar(conv_w[:, :, :], conv_w[:, :, :], 0.5, None, ALU.mult)
            eng.tensor_scalar(conv_b[:, :], conv_b[:, :], 0.5, None, ALU.mult)
            eng.wait_ge(s["a_exp"], 1)
            eng.tensor_scalar(a_neg[:, :], a_neg[:, :], -1.0, None, ALU.mult)
            eng.wait_ge(s["consts"], 9)
            eng.tensor_copy(tri_r[:, :], tri[:, :])
            eng.tensor_copy(mask_r[:, :], mask[:, :])
            eng.tensor_copy(ident_r[:, :], ident[:, :])
            eng.wait_ge(s["wa_dma"], 32)
            fold_in(DT0, DIN)
            fold_in(CH0, CH0 + 2 * DXB)
            eng.wait_ge(s["folded"], 2)
            dt_first(0)
            dt_rest(0, 0)
            eng.wait_ge(s["wc_dma"], 16 * 4 * KD)
            fold_in(CH0 + 2 * DXB, DT0)
            for ch in range(NCH):
                taps(0, ch)
                if ch:
                    silu_ch(0, 0, ch - 1)
            silu_ch(0, 0, NCH - 1)
            rows_in(1, 1)
            norm_rows(1, 1)
            eng.wait_ge(s["wz_dma"], 16)
            fold_in(0, DI)
            eng.wait_ge(s["wo_dma"], 16)
            for k in range(DI // P):
                last = eng.tensor_scalar(w_out[:, k, :], w_out[:, k, :], normw[:, k:k + 1], None, ALU.mult)
            last.then_inc(s["folded"], 1)

            def next_rows(i, k):
                c, u, par = i * 4 + k, k % 2, (k // 2) % 2
                for j in range(2):
                    eng.wait_ge(s["z_tanh"], c * 2 + j + 1)
                    zj = zs[:, j * 512:(j + 1) * 512]
                    eng.scalar_tensor_tensor(zj, zj, 1.0, proj_ps[j][:, :], ALU.add, ALU.mult)\
                       .then_inc(s["z_gate"], 1)
                eng.wait_ge(s["xb_row"], c + 1)
                eng.wait_ge(s["yd1"], c * 2 + 1)
                eng.wait_ge(s["xdd"], c + 1)
                xr = xb_row[:, 0, :].rearrange("p (g d) -> p g d", g=NG).unsqueeze(2).broadcast_to([P, NG, HPG, HD])
                eng.tensor_tensor(xdt[:, :].rearrange("p (g r d) -> p g r d", g=NG, r=HPG), xr,
                                  dt[par][:, u, :].rearrange("p (g r) -> p g r", g=NG).unsqueeze(3)
                                  .broadcast_to([P, NG, HPG, HD]), ALU.mult).then_inc(s["xdt"], 1)

            def outcome(e):
                eng.wait_ge(s["out_ps"], e + 2)
                eng.wait_ge(s["r_step"], e * NR + NR)
                eng.wait_ge(s["h2_step"], e * NH2 + 1)
                eng.wait_ge(s["yres"], e + 1)
                eng.scalar_tensor_tensor(hres[:, :], misc[:, :], sumsq[:, 3:4], yres[:, :], ALU.mult, ALU.add)\
                   .then_inc(s["h_done"], 1)

            next_rows(0, 0)

            def slot(i, k, front, pre):
                c, gf, u, par = i * 4 + k, i * 2 + k // 2 + 1, k % 2, (k // 2) % 2
                half = u * (NCH // 2)

                def scores(hg):
                    eng.wait_ge(exp_s[hg % 2], c * 2 + hg // 2 + 2)
                    eng.wait_ge(s["cb"], c * 4 + hg + 1)
                    eng.tensor_tensor(decay[hg % 2][:, :, :], decay[hg % 2][:, :, :],
                                      cb_ps[:, :].rearrange("p (j q) -> p j q", j=HPG), ALU.mult)\
                       .then_inc(sc_s[hg % 2], 1)

                def sums(hg):
                    n = c * 4 + hg
                    eng.wait_ge(yd_s[hg % 2], c * 2 + hg // 2 + 2)
                    if hg == 0:
                        eng.wait_ge(s["xdd"], c + 2)
                    if hg % 2 == 0:
                        eng.wait_ge(s["yT_ps"], c * 2 + hg // 2 + 1)
                    ps = y_ps[hg % 2]
                    yd = head_cols(yrow, hg)
                    eng.tensor_tensor(yd, ps[:, 0:HPG * HD], head_cols(dx, hg), ALU.add).then_inc(s["yread_a"], 1)
                    eng.tensor_tensor(yoff[:, :].rearrange("p (j d) -> p j d", j=HPG),
                                      ps[:, HPG * HD:2 * HPG * HD].rearrange("p (j d) -> p j d", j=HPG),
                                      exp_cum[par][:, u, hg * HPG:(hg + 1) * HPG].unsqueeze(2)
                                      .broadcast_to([P, HPG, HD]), ALU.mult).then_inc(yread_s[hg % 2], 1)
                    eng.wait_ge(s["yread_a"], n + 1)
                    eng.wait_ge(yread_s[hg % 2], c * 2 + hg // 2 + 2)
                    eng.tensor_tensor(yd, yd, yoff[:, :], ALU.add).then_inc(s["ysum"], 1)

                def gate(j):
                    eng.wait_ge(s["ysum"], c * 4 + 2 * j + 6)
                    eng.wait_ge(s["z_gate"], c * 2 + j + 1)
                    h = slice(j * 512, (j + 1) * 512)
                    eng.tensor_tensor(yrow[:, h], yrow[:, h], zs[:, h], ALU.mult).then_inc(s["ygate"], 1)

                scores(0)
                if front:
                    taps(gf, half + 0)
                sums(0)
                scores(1)
                if not first(i, k):
                    outcome(c - 1)
                eng.wait_ge(s["h_done"], c + 1)
                eng.wait_ge(xres_dma[u], i * 32 + k // 2 * 16 + 16)
                eng.tensor_scalar(yres[:, :], xres[u][:, :], mv[:, par, u, 0:1], lnq[:, par, u, 1:2],
                                  ALU.subtract, ALU.mult).then_inc(s["yres"], 1)
                if pre:
                    rows_in(gf + 1, par)
                if front:
                    silu_ch(gf, 1 - par, half + 0)
                    taps(gf, half + 1)
                sums(1)
                gate(0)
                scores(2)
                if front and u == 0:
                    dt_first(gf)
                if front:
                    silu_ch(gf, 1 - par, half + 1)
                    taps(gf, half + 2)
                if pre:
                    norm_rows(gf + 1, par)
                sums(2)
                scores(3)
                if front and u == 0:
                    dt_rest(gf, 1 - par)
                if front:
                    silu_ch(gf, 1 - par, half + 2)
                    taps(gf, half + 3)
                sums(3)
                gate(1)
                if front:
                    silu_ch(gf, 1 - par, half + 3)
                    taps(gf, half + 4)
                eng.wait_ge(s["state_ps"], c + 2)
                eng.wait_ge(s["carry_decayed"], c + 1)
                eng.tensor_tensor(carry[:, :, :, :].rearrange("p a j d -> p (a j d)"),
                                  carry[:, :, :, :].rearrange("p a j d -> p (a j d)"), misc[:, :], ALU.add)\
                   .then_inc(s["carry_done"], 1)
                if front:
                    silu_ch(gf, 1 - par, half + 4)
                    taps(gf, half + 5)
                    silu_ch(gf, 1 - par, half + 5)
                if not last_chunk(i, k):
                    next_rows(i, k + 1)

            slots(slot, eng)
            outcome(TILES - 1)

        @block.tensor
        def _(eng):
            def row_transposes(g, par, u):
                eng.wait_ge(s["normed"], g * 2 + u + 1)
                for k in range(KD):
                    last = eng.transpose(misc[:, k * P:(k + 1) * P], xin[:, u, k * P:(k + 1) * P], ident[:, :])
                last.then_inc(s["rowT"], 1)

            def dt_proj(g, par):
                eng.wait_ge(s["hT_done"], g * 2 + 2)
                for u in range(2):
                    for k in range(KD):
                        last = eng.matmul(misc[:, u * HEADS:(u + 1) * HEADS], hT[par][:, k, u * P:(u + 1) * P],
                                          w_in[:, k, DT0:DIN], start=(k == 0), stop=(k == KD - 1))
                last.then_inc(s["dt_ps"], 1)

            def cum_sums(g, par):
                eng.wait_ge(s["dt_done"], g * 3 + 3)
                rhs = da[:, :, :].rearrange("p u h -> p (u h)")
                for i, w in enumerate((tri, suffix, ones)):
                    last = eng.matmul(misc[:, i * 32:(i + 1) * 32], w[:, :], rhs, start=True, stop=True)
                last.then_inc(s["cum_ps"], 1)

            def channel_block(g, par, ch):
                col = CH0 + ch * P
                for k in range(KD):
                    last = eng.matmul(proj_ps[ch % 2][:, 0:GR], w_in[:, k, col:col + P], hT[par][:, k, :],
                                      start=(k == 0), stop=(k == KD - 1))
                last.then_inc(s["ch_ps"], 1)

            def z_rows(i, k):
                c, u, par = i * 4 + k, k % 2, (k // 2) % 2
                for j in range(2):
                    for q in range(KD):
                        last = eng.matmul(proj_ps[j][:, :], hT[par][:, q, u * P:(u + 1) * P],
                                          w_in[:, q, j * 512:(j + 1) * 512], start=(q == 0), stop=(q == KD - 1))
                    last.then_inc(s["z_ps"], 1)

            def xb_rows(i, k):
                g, u, par = i * 2 + k // 2, k % 2, (k // 2) % 2
                eng.wait_ge(s["ch_done"], g * NCH + 4 + 3)
                for n in range(4):
                    last = eng.transpose(misc[:, n * P:(n + 1) * P], cv[par][:, n, u * P:(u + 1) * P], ident[:, :])
                last.then_inc(s["xb_ps"], 1)

            def turn_gated(e, j):
                eng.wait_ge(s["ygate"], e * 2 + j + 3)
                for n in range(4):
                    f = (j * 4 + n) * P
                    last = eng.transpose(misc[:, n * P:(n + 1) * P], yrow[:, f:f + P], ident[:, :])
                last.then_inc(s["yT_ps"], 1)

            def out_proj(e):
                eng.wait_ge(s["folded"], 5)
                eng.wait_ge(s["yT_done"], e * 2 + 2)
                for n in range(DI // P):
                    last = eng.matmul(misc[:, :], yT[:, n, :], w_out[:, n, :], start=(n == 0), stop=(n == DI // P - 1))
                last.then_inc(s["out_ps"], 1)

            row_transposes(0, 0, 0)
            eng.wait_ge(s["hT_done"], 1)
            row_transposes(0, 0, 1)
            eng.wait_ge(s["folded"], 2)
            dt_proj(0, 0)
            cum_sums(0, 0)
            for ch in range(NCH):
                if ch == 4:
                    eng.wait_ge(s["folded"], 3)
                if ch >= 2:
                    eng.wait_ge(s["ch_copied"], ch - 1)
                channel_block(0, 0, ch)
            eng.wait_ge(s["cum_done"], 1)
            row_transposes(1, 1, 0)
            eng.wait_ge(s["hT_done"], 3)
            row_transposes(1, 1, 1)
            eng.wait_ge(s["folded"], 4)
            eng.wait_ge(s["ch_copied"], NCH)
            z_rows(0, 0)
            eng.wait_ge(s["hT_done"], 4)
            xb_rows(0, 0)

            def slot(i, k, front, pre):
                c, gf, u, par = i * 4 + k, i * 2 + k // 2 + 1, k % 2, (k // 2) % 2
                half = u * (NCH // 2)
                tile = slice(u * P, (u + 1) * P)

                def seg(hg):
                    eng.wait_ge(exp_s[hg % 2], c * 2 + hg // 2 + 1)
                    ps = seg_ps[hg % 2]
                    eng.matmul(ps[:, :], ident_r[:, :], mask_r[:, :].unsqueeze(1).broadcast_to([P, HPG, P]),
                               start=True, stop=False, skip_group_check=True)
                    for j in range(HPG):
                        h = hg * HPG + j
                        for part in (da_hi, da_lo):
                            last = eng.matmul(ps[:, j * P:(j + 1) * P],
                                              part[par][:, u, h:h + 1].broadcast_to([P, P]), tri_r[:, :],
                                              start=False, stop=(part is da_lo and j == HPG - 1),
                                              skip_group_check=True)
                    last.then_inc(seg_s[hg % 2], 1)

                def b_dot_c(hg):
                    a, b = hg // 2, hg % 2
                    p = slice(b * HD, (b + 1) * HD)
                    if hg == 0:
                        eng.wait_ge(s["ch_done"], gf * NCH + 3)
                    eng.wait_ge(sc_s[(hg + 1) % 2], c * 2 + (hg + 1) // 2 + 1)
                    eng.matmul(cb_ps[:, :], cv[par][p, 2 + a, tile],
                               cv[par][p, 4 + 4 * a:8 + 4 * a, tile], start=True, stop=True).then_inc(s["cb"], 1)

                def outputs(hg):
                    a, b = hg // 2, hg % 2
                    p = slice(b * HD, (b + 1) * HD)
                    if hg == 0:
                        eng.wait_ge(s["carry_done"], c + 1)
                        eng.wait_ge(s["xdt"], c + 2)
                    eng.wait_ge(yread_s[hg % 2], c * 2 + hg // 2 + 1)
                    n = HPG * HD
                    for j in range(HPG):
                        eng.matmul(y_ps[hg % 2][:, n + j * HD:n + (j + 1) * HD], cv[par][p, 4 + 4 * a + j, tile],
                                   carry[p, a, j, :], start=True, stop=True)
                    eng.wait_ge(sc_s[hg % 2], c * 2 + hg // 2 + 2)
                    for j in range(HPG):
                        h = hg * HPG + j
                        last = eng.matmul(y_ps[hg % 2][:, j * HD:(j + 1) * HD], decay[hg % 2][:, j, :],
                                          xdt[:, h * HD:(h + 1) * HD], start=True, stop=True)
                    last.then_inc(yd_s[hg % 2], 1)

                def front_block(i):
                    if i < 2:
                        eng.wait_ge(s["z_gate"], c * 2 + i + 1)
                    else:
                        eng.wait_ge(s["ch_copied"], gf * NCH + half + i - 1)
                    channel_block(gf, 1 - par, half + i)

                def states():
                    eng.wait_ge(s["xdd"], c + 2)
                    n = HPG * HD
                    for hg in range(NG):
                        a, b = hg // 2, hg % 2
                        last = eng.matmul(misc[b * HD:(b + 1) * HD, a * n:(a + 1) * n],
                                          xb_row[:, 1, hg * HD:(hg + 1) * HD], xdd[:, hg * n:(hg + 1) * n],
                                          start=True, stop=True)
                    last.then_inc(s["state_ps"], 1)

                seg(0)
                b_dot_c(0)
                eng.wait_ge(s["xb_row"], c + 1)
                if not first(i, k):
                    turn_gated(c - 1, 0)
                if front:
                    front_block(0)
                if not first(i, k):
                    eng.wait_ge(s["yT_done"], c * 2 - 1)
                    turn_gated(c - 1, 1)
                seg(1)
                outputs(0)
                b_dot_c(1)
                if not first(i, k):
                    out_proj(c - 1)
                if front:
                    front_block(1)
                seg(2)
                outputs(1)
                b_dot_c(2)
                eng.wait_ge(s["h_done"], c + 1)
                if front and u == 0:
                    dt_proj(gf, 1 - par)
                if front:
                    front_block(2)
                seg(3)
                outputs(2)
                b_dot_c(3)
                if pre:
                    row_transposes(gf + 1, par, 0)
                if front:
                    front_block(3)
                outputs(3)
                if front and u == 0:
                    cum_sums(gf, 1 - par)
                if pre:
                    eng.wait_ge(s["hT_done"], gf * 2 + 3)
                    row_transposes(gf + 1, par, 1)
                if front:
                    front_block(4)
                if front and u == 0:
                    eng.wait_ge(s["cum_done"], gf + 1)
                if pre:
                    eng.wait_ge(s["hT_done"], gf * 2 + 4)
                states()
                if front:
                    front_block(5)
                if not last_chunk(i, k):
                    if front:
                        eng.wait_ge(s["ch_copied"], gf * NCH + half + NCH // 2)
                    else:
                        eng.wait_ge(s["z_gate"], c * 2 + 2)
                    z_rows(i, k + 1)
                    eng.wait_ge(s["carry_done"], c + 2)
                    xb_rows(i, k + 1)

            slots(slot, eng)
            eng.wait_ge(s["carry_done"], TILES + 1)
            for j in range(2):
                if j:
                    eng.wait_ge(s["yT_done"], TILES * 2 - 1)
                turn_gated(TILES - 1, j)
            out_proj(TILES - 1)


def constants(nc, ident, ones):
    with nc.semaphore("ident_step") as step, nc.Block() as block:
        @block.gpsimd
        def _(eng):
            eng.memset(ones[:, :], 1.0)
            eng.memset(ident[:, :], 0.0).then_inc(step, 1)
            eng.wait_ge(step, 1)
            eng.affine_select(out=ident[:, :], in_=ident[:, :], compare_op=ALU.not_equal, fill=1.0, base=0,
                              pattern=[[-1, P]], channel_multiplier=1)


def feed_forward(nc, ins, dr, ident, acc):
    NB, NI, RG = FF // FB, FB // P, 512
    NR = ROWS // RG
    TPR = RG // P
    with ExitStack() as ctx:
        def sb(name, shape, dt=F32):
            return ctx.enter_context(nc.sbuf_tensor(name, shape, dt))

        zeros = sb("zeros", [P, D])
        rows = [sb(f"ff_rows{i}", [P, D]) for i in range(2)]
        hT_hi = sb("ff_hT_hi", [P, KD, ROWS], F32R)
        hT_lo = sb("ff_hT_lo", [P, KD, ROWS], F32R)
        stage = [sb(f"ff_stage{i}", [P, KD * FB]) for i in range(3)]
        w_hi = [[sb(f"ff_w_hi{i}{j}", [P, KD * FB], F32R) for j in range(3)] for i in range(2)]
        w_lo = [[sb(f"ff_w_lo{i}{j}", [P, KD * FB], F32R) for j in range(3)] for i in range(2)]
        prod = [sb(f"ff_prod{i}", [P, RG]) for i in range(2)]
        p_hi = [sb(f"ff_p_hi{i}", [P, NI, RG], F32R) for i in range(2)]
        p_lo = [sb(f"ff_p_lo{i}", [P, NI, RG], F32R) for i in range(2)]
        bank = [ctx.enter_context(nc.psum_tensor(f"ff_bank{i}", [P, 512], F32)) for i in range(8)]
        gate_ps, up_ps, down_ps = bank[0:2], bank[2:4], bank[4:8]
        assert NI * D == KD * FB and TPR == 4
        s = {n: ctx.enter_context(nc.semaphore("ff_" + n)) for n in (
            "zeroed", "cleared", "acc_dma", "rows_dma0", "rows_dma1", "rowT", "hT_hi", "hT_lo", "w_dma0", "w_dma1", "w_dma2", "w_hi", "w_lo",
            "gate_ps", "up_ps", "silu", "prod", "p_hi", "p_lo", "down", "add")}
        CR = 2 * TPR
        rows_dma = [s["rows_dma0"], s["rows_dma1"]]
        w_dma = [s["w_dma0"], s["w_dma1"], s["w_dma2"]]
        block = ctx.enter_context(nc.Block())

        def as_in(t):
            return t[:, :].rearrange("p (k n) -> p k n", k=KD)

        def as_down(t):
            return t[:, :].rearrange("p (c n) -> p c n", c=NI)

        @block.sync
        def _(eng):
            def load_piece(b, j):
                if j < 2:
                    src = ins["L0_attn_gate_w" if j == 0 else "L0_attn_up_w"].rearrange("(k p) n -> p k n", p=P)
                    eng.dma_start(as_in(stage[j]), src[:, :, bass.ds(b * FB, FB)]).then_inc(w_dma[j], 16)
                else:
                    src = ins["L0_attn_down_w"][bass.ds(b * FB, FB), :].rearrange("(c p) n -> p c n", p=P)
                    eng.dma_start(as_down(stage[j]), src).then_inc(w_dma[j], 16)

            for t in range(2):
                eng.dma_start(rows[t][:, :], dr["h2"][bass.ds(t * P, P), :]).then_inc(rows_dma[t], 16)
            for j in range(3):
                load_piece(0, j)
            with eng.Fori(1, TILES // 2) as i:
                for t in range(2):
                    eng.wait_ge(s["rowT"], i * 2 + t - 1)
                    eng.dma_start(rows[t][:, :], dr["h2"][bass.ds((i * 2 + t) * P, P), :]).then_inc(rows_dma[t], 16)
            eng.dma_start(acc[:, :, :], dr["xh"].rearrange("(t p) n -> p t n", p=P)).then_inc(s["acc_dma"], 16)
            eng.wait_ge(s["zeroed"], 1)
            eng.dma_start(dr["sorted"].rearrange("(t p) n -> p t n", p=P),
                          zeros[:, :].unsqueeze(1).broadcast_to([P, SORT_TILES, D])).then_inc(s["cleared"], 16)
            with eng.Fori(1, NB) as b:
                for j in range(3):
                    eng.wait_ge(s["w_lo"], b * 3 + j - 2)
                    load_piece(b, j)
            eng.wait_ge(s["cleared"], 16)

        @block.gpsimd
        def _(eng):
            for name, n in (("silu", 2), ("prod", 2), ("p_lo", 2), ("down", CR), ("add", TPR), ("hT_lo", 2)):
                eng.sem_inc(s[name], n)
            eng.memset(zeros[:, :], 0.0).then_inc(s["zeroed"], 1)

            def low_parts(b, par):
                for j in range(3):
                    eng.wait_ge(w_dma[j], (b + 1) * 16)
                    eng.wait_ge(s["w_hi"], b * 3 + j + 1)
                    eng.tensor_tensor(w_lo[par][j][:, :], stage[j][:, :], w_hi[par][j][:, :].bitcast(F32),
                                      ALU.subtract).then_inc(s["w_lo"], 1)

            with eng.Fori(0, NB // 2) as i:
                for par in range(2):
                    low_parts(i * 2 + par, par)


        def steps(body, eng):
            with eng.Fori(0, NB // 2 - 1) as i:
                for k in range(2 * NR):
                    body(i * 2 + k // NR, k)
            for k in range(2 * NR):
                body(NB - 2 + k // NR, k)

        def following(width, b, k):
            if not (isinstance(b, int) and b * NR + k % NR == NB * NR - 1):
                width(b + (k + 1) // NR - k // NR, (k + 1) % (2 * NR))

        @block.scalar
        def _(eng):
            for j in range(3):
                eng.wait_ge(w_dma[j], 16)
                eng.activation(w_hi[0][j][:, :], stage[j][:, :], ACT.Copy).then_inc(s["w_hi"], 1)
            with eng.Fori(0, TILES // 2) as i:
                for v in range(2):
                    eng.wait_ge(s["rowT"], i * 2 + v + 1)
                    eng.activation(hT_hi[:, :, bass.ds((i * 2 + v) * P, P)],
                                   bank[v][:, :].rearrange("p (k n) -> p k n", k=KD), ACT.Copy).then_inc(s["hT_hi"], 1)

            def width(b, k):
                step = b * NR + k % NR
                for c in range(NI):
                    n = step * NI + c
                    eng.wait_ge(s["gate_ps"], n + 1)
                    eng.wait_ge(s["p_lo"], n + 1)
                    eng.activation(prod[c][:, :], gate_ps[c][:, :], ACT.Silu).then_inc(s["silu"], 1)
                    eng.wait_ge(s["prod"], n + 3)
                    eng.wait_ge(s["down"], step * TPR + TPR)
                    eng.activation(p_hi[k % 2][:, c, :], prod[c][:, :], ACT.Copy).then_inc(s["p_hi"], 1)

            width(0, 0)

            def body(b, k):
                if k % NR and not (isinstance(b, int) and b == NB - 1):
                    j = k % NR - 1
                    eng.wait_ge(w_dma[j], b * 16 + 32)
                    eng.wait_ge(s["down"], b * NR * TPR + CR)
                    eng.activation(w_hi[(k // NR + 1) % 2][j][:, :], stage[j][:, :], ACT.Copy)\
                       .then_inc(s["w_hi"], 1)
                following(width, b, k)

            steps(body, eng)

        @block.vector
        def _(eng):
            with eng.Fori(0, TILES // 2) as i:
                for v in range(2):
                    eng.wait_ge(s["hT_hi"], i * 2 + v + 1)
                    cols = bass.ds((i * 2 + v) * P, P)
                    eng.tensor_tensor(hT_lo[:, :, cols], bank[v][:, :].rearrange("p (k n) -> p k n", k=KD),
                                      hT_hi[:, :, cols].bitcast(F32), ALU.subtract).then_inc(s["hT_lo"], 1)

            def width(b, k):
                for c in range(NI):
                    n = (b * NR + k % NR) * NI + c
                    eng.wait_ge(s["silu"], n + 3)
                    eng.wait_ge(s["up_ps"], n + 1)
                    eng.tensor_tensor(prod[c][:, :], prod[c][:, :], up_ps[c][:, :], ALU.mult).then_inc(s["prod"], 1)
                    eng.wait_ge(s["prod"], n + 3)
                    eng.wait_ge(s["p_hi"], n + 1)
                    eng.tensor_tensor(p_lo[k % 2][:, c, :], prod[c][:, :], p_hi[k % 2][:, c, :].bitcast(F32),
                                      ALU.subtract).then_inc(s["p_lo"], 1)

            width(0, 0)
            eng.wait_ge(s["acc_dma"], 16)

            def body(b, k):
                following(width, b, k)
                for t in range(TPR):
                    eng.wait_ge(s["down"], (b * NR + k % NR) * TPR + t + 1 + CR)
                    row = acc[:, (k % NR) * TPR + t, :]
                    eng.tensor_tensor(row, down_ps[t][:, :], row, ALU.add).then_inc(s["add"], 1)

            steps(body, eng)

        @block.tensor
        def _(eng):
            with eng.Fori(0, TILES // 2) as i:
                for v in range(2):
                    eng.wait_ge(rows_dma[v], i * 16 + 16)
                    eng.wait_ge(s["hT_lo"], i * 2 + v + 1)
                    for k in range(KD):
                        last = eng.transpose(bank[v][:, k * P:(k + 1) * P], rows[v][:, k * P:(k + 1) * P], ident[:, :])
                    last.then_inc(s["rowT"], 1)
            eng.wait_ge(s["hT_lo"], TILES + 2)

            def three(ps, w, x, first, last):
                for i, (a, b) in enumerate(((0, 0), (0, 1), (1, 0))):
                    mm = eng.matmul(ps, w[a], x[b], start=first and i == 0, stop=last and i == 2)
                return mm

            def width(b, k):
                par, r = k // NR % 2, k % NR
                if r == 0:
                    eng.wait_ge(s["w_lo"], b * 3 + 3)
                cols = slice(r * RG, (r + 1) * RG)
                for c in range(NI):
                    n = (b * NR + r) * NI + c
                    for j, ps, free, done in ((0, gate_ps[c], "silu", "gate_ps"), (1, up_ps[c], "prod", "up_ps")):
                        eng.wait_ge(s[free], n + 1)
                        for q in range(KD):
                            w = [as_in(t[par][j])[:, q, c * P:(c + 1) * P] for t in (w_hi, w_lo)]
                            x = [t[:, q, cols] for t in (hT_hi, hT_lo)]
                            mm = three(ps[:, :], w, x, q == 0, q == KD - 1)
                        mm.then_inc(s[done], 1)

            def out(b, k):
                par, step = k // NR % 2, b * NR + k % NR
                eng.wait_ge(s["p_lo"], step * NI + NI + 2)
                for t in range(TPR):
                    eng.wait_ge(s["add"], step * TPR + t + 1)
                    for c in range(NI):
                        x = [v[k % 2][:, c, t * P:(t + 1) * P] for v in (p_hi, p_lo)]
                        w = [as_down(v[par][2])[:, c, :] for v in (w_hi, w_lo)]
                        mm = three(down_ps[t][:, :], x, w, c == 0, c == NI - 1)
                    mm.then_inc(s["down"], 1)

            width(0, 0)

            def body(b, k):
                following(width, b, k)
                out(b, k)

            steps(body, eng)


def experts(nc, ins, dr, out_d, ident, ones, acc):
    with ExitStack() as ctx:
        def sb(name, shape, dt=F32, where=ctx):
            return where.enter_context(nc.sbuf_tensor(name, shape, dt))

        def sem(name):
            return ctx.enter_context(nc.semaphore("moe_" + name))

        w_gu = sb("w_gu", [P, 2, E * KD, EI])
        w_dn = sb("w_dn", [P, E * len(IC), D])
        mv = sb("moe_mv", [P, TILES, 2])
        rstd = sb("moe_rstd", [P, TILES])
        weight = sb("moe_weight", [P, 2, TILES])
        slot = sb("moe_slot", [P, 2 * TILES], U32)
        tile_expert = sb("tile_expert", [1, SORT_TILES], mybir.dt.int32)
        s_w = sem("w_dma")
        NW = 2 * E + 2 * E

        with ExitStack() as rctx:
            xm = [sb(f"xm{i}", [P, D], where=rctx) for i in range(4)]
            xmT = [sb(f"xmT{i}", [P, KD, P], where=rctx) for i in range(2)]
            wr = sb("wr", [P, KD, E], where=rctx)
            bn = sb("moe_bn", [P, TILES, 6], where=rctx)
            half_neg = sb("moe_half_neg", [P, TILES], where=rctx)
            strict = sb("strict", [P, P], where=rctx)
            iota_e = sb("iota_e", [P, E], mybir.dt.int32, where=rctx)
            iota_t = sb("iota_t", [P, SORT_TILES + 1], mybir.dt.int32, where=rctx)
            ef = sb("ef", [P, E], where=rctx)
            tf = sb("tf", [P, SORT_TILES + 1], where=rctx)
            t3 = lambda name: sb(name, [P, TILES, E], where=rctx)
            prob, top, hot0, hot1, hot, run_a, run_b, place = map(
                t3, ("prob", "top", "hot0", "hot1", "hot", "run_a", "run_b", "place"))
            idx = sb("idx", [P, TILES, E], U32, where=rctx)
            idx_f = sb("idx_f", [P, TILES, 2], where=rctx)
            red = sb("red", [P, 4, TILES], where=rctx)
            cmp_n = sb("cmp_n", [P, E, TILES], where=rctx)
            ends = sb("ends", [P, 4, E], where=rctx)
            cmp_t = sb("cmp_t", [P, SORT_TILES, E], where=rctx)
            slot_f = sb("slot_f", [P, 2 * TILES], where=rctx)
            te_f = sb("te_f", [P, SORT_TILES], where=rctx)
            bank = [rctx.enter_context(nc.psum_tensor(f"rt_bank{i}", [P, 512], F32)) for i in range(4)]
            s = {n: rctx.enter_context(nc.semaphore("rt_" + n)) for n in (
                "wr_dma", "const", "bn", "stat", "rstd", "xm", "rowT", "xmT", "logits", "route", "exp", "counts",
                "again", "scat0", "scat1", "scat2", "scat3")}
            scat = [s[f"scat{i}"] for i in range(4)]
            HOT = 5 + 2 * TILES + 8
            block = rctx.enter_context(nc.Block())

            @block.sync
            def _(eng):
                eng.dma_start(wr[:, :, :], ins["L0_ffn_Wr"].rearrange("(k p) e -> p k e", p=P)).then_inc(s["wr_dma"], 16)
                for e in range(E):
                    for j, name in enumerate(("L0_ffn_Wg", "L0_ffn_Wu")):
                        eng.dma_start(w_gu[:, j, e * KD:(e + 1) * KD, :],
                                      ins[name][e].rearrange("(k p) i -> p k i", p=P)).then_inc(s_w, 16)
                    n, full = len(IC), EI // P
                    src = ins["L0_ffn_Wd"][e]
                    eng.dma_start(w_dn[:, e * n:e * n + full, :],
                                  src[0:full * P, :].rearrange("(c p) n -> p c n", p=P)).then_inc(s_w, 16)
                    eng.dma_start(w_dn[0:EI - full * P, e * n + full, :], src[full * P:EI, :]).then_inc(s_w, 16)
                eng.wait_ge(s["wr_dma"], 16)

            @block.gpsimd
            def _(eng):
                eng.sem_inc(s["xmT"], 2)
                eng.sem_inc(s["logits"], 2)
                eng.memset(half_neg[:, :], -0.5).then_inc(s["const"], 1)
                eng.memset(strict[:, :], 1.0).then_inc(s["const"], 1)
                eng.iota(iota_e[:, :], pattern=[[1, E]], base=0, channel_multiplier=0).then_inc(s["const"], 1)
                eng.iota(iota_t[:, :], pattern=[[1, SORT_TILES + 1]], base=0, channel_multiplier=0)\
                   .then_inc(s["const"], 1)
                eng.wait_ge(s["const"], 4)
                eng.affine_select(out=strict[:, :], in_=strict[:, :], compare_op=ALU.is_gt, fill=0.0, base=0,
                                  pattern=[[1, P]], channel_multiplier=-1).then_inc(s["const"], 1)
                eng.wait_ge(s["stat"], TILES)
                eng.tensor_scalar(rstd[:, :], mv[:, :, 1], EPS, None, ALU.add).then_inc(s["rstd"], 1)
                eng.wait_ge(s["rstd"], 1)
                eng.tensor_tensor(rstd[:, :], rstd[:, :], half_neg[:, :], ALU.pow).then_inc(s["rstd"], 1)
                for t in range(TILES):
                    eng.wait_ge(s["again"], t + 1)
                    for k in range(2):
                        n = 2 * t + k
                        eng.indirect_dma_start(out=dr["sorted"][:, :],
                                               out_offset=bass.IndirectOffsetOnAxis(ap=slot[:, k * TILES + t:k * TILES + t + 1], axis=0),
                                               in_=xm[t % 4][:, :], in_offset=None).then_inc(scat[t % 4], 16)
                for i in range(4):
                    eng.wait_ge(scat[i], 2 * 16 * (TILES // 4))

            @block.scalar
            def _(eng):
                with eng.Fori(0, TILES // 2) as i:
                    for v in range(2):
                        eng.wait_ge(s["rowT"], i * 2 + v + 1)
                        eng.wait_ge(s["logits"], i * 2 + v + 1)
                        eng.activation(xmT[v][:, :, :].rearrange("p k n -> p (k n)"), bank[v][:, :], ACT.Copy)\
                           .then_inc(s["xmT"], 1)
                eng.wait_ge(s["route"], 2)
                eng.activation(prob[:, :, :], prob[:, :, :], ACT.Exp).then_inc(s["exp"], 1)

            @block.tensor
            def _(eng):
                eng.wait_ge(s["wr_dma"], 16)
                for i in range(TILES // 2):
                    for v in range(2):
                        t = i * 2 + v
                        eng.wait_ge(s["xm"], t + 1)
                        eng.wait_ge(s["xmT"], t + 1)
                        for k in range(KD):
                            last = eng.transpose(bank[v][:, k * P:(k + 1) * P], xm[t % 4][:, k * P:(k + 1) * P],
                                                 ident[:, :])
                        last.then_inc(s["rowT"], 1)
                        eng.wait_ge(s["xmT"], t + 3)
                        for k in range(KD):
                            last = eng.matmul(bank[2][:, t * E:(t + 1) * E], xmT[v][:, k, :], wr[:, k, :],
                                              start=(k == 0), stop=(k == KD - 1))
                        last.then_inc(s["logits"], 1)
                eng.wait_ge(s["const"], 5)
                eng.wait_ge(s["route"], HOT)
                flat = hot[:, :, :].rearrange("p t e -> p (t e)")
                eng.matmul(bank[3][:, 0:P], strict[:, :], flat, start=True, stop=True)
                eng.matmul(bank[3][:, P:2 * P], ones[:, :], flat, start=True, stop=True).then_inc(s["counts"], 1)

            @block.vector
            def _(eng):
                done = [0]

                def step(ins_):
                    ins_.then_inc(s["route"], 1)
                    done[0] += 1
                    eng.wait_ge(s["route"], done[0])

                def per_tile(a):
                    return a.unsqueeze(2).broadcast_to([P, TILES, E])

                def normed(t):
                    return eng.tensor_scalar(xm[t % 4][:, :], acc[:, t, :], mv[:, t, 0:1], rstd[:, t:t + 1],
                                             ALU.subtract, ALU.mult)

                for t in range(TILES):
                    eng.bn_stats(bn[:, t, :], acc[:, t, :]).then_inc(s["bn"], 1)
                for t in range(TILES):
                    eng.wait_ge(s["bn"], t + 1)
                    eng.bn_aggr(mv[:, t, :], bn[:, t, :]).then_inc(s["stat"], 1)
                eng.wait_ge(s["rstd"], 2)
                for t in range(TILES):
                    if t >= 4:
                        eng.wait_ge(s["rowT"], t - 3)
                    normed(t).then_inc(s["xm"], 1)
                eng.wait_ge(s["logits"], TILES + 2)
                logits = bank[2][:, 0:TILES * E].rearrange("p (t e) -> p t e", e=E)
                step(eng.tensor_reduce(red[:, 0, :], logits, AX_X, ALU.max))
                step(eng.tensor_tensor(prob[:, :, :], logits, per_tile(red[:, 0, :]), ALU.subtract))
                eng.wait_ge(s["exp"], 1)
                step(eng.tensor_reduce(red[:, 1, :], prob[:, :, :], AX_X, ALU.add))
                step(eng.reciprocal(red[:, 2, :], red[:, 1, :]))
                step(eng.tensor_tensor(prob[:, :, :], prob[:, :, :], per_tile(red[:, 2, :]), ALU.mult))
                for t in range(TILES):
                    step(eng.max(top[:, t, :], prob[:, t, :]))
                    step(eng.max_index(idx[:, t, :], top[:, t, :], prob[:, t, :]))
                eng.wait_ge(s["const"], 5)
                step(eng.tensor_copy(ef[:, :], iota_e[:, :]))
                step(eng.tensor_copy(tf[:, :], iota_t[:, :]))
                step(eng.tensor_copy(idx_f[:, :, :], idx[:, :, 0:2]))
                e_of = ef[:, :].unsqueeze(1).broadcast_to([P, TILES, E])
                for k, h in enumerate((hot0, hot1)):
                    step(eng.tensor_tensor(h[:, :, :], e_of, per_tile(idx_f[:, :, k]), ALU.is_equal))
                step(eng.tensor_tensor(hot[:, :, :], hot0[:, :, :], hot1[:, :, :], ALU.add))
                step(eng.tensor_tensor(red[:, 0, :], top[:, :, 0], top[:, :, 1], ALU.add))
                step(eng.reciprocal(red[:, 3, :], red[:, 0, :]))
                assert done[0] == HOT
                for k in range(2):
                    step(eng.tensor_tensor(weight[:, k, :], top[:, :, k], red[:, 3, :], ALU.mult))
                eng.wait_ge(s["counts"], 1)
                before = bank[3][:, 0:P].rearrange("p (t e) -> p t e", e=E)
                total = bank[3][:, P:2 * P].rearrange("p (t e) -> p t e", e=E)
                step(eng.tensor_copy(run_a[:, :, :], total))
                a, b = run_a, run_b
                sh = 1
                while sh < TILES:
                    step(eng.tensor_copy(b[:, 0:sh, :], a[:, 0:sh, :]))
                    step(eng.tensor_tensor(b[:, sh:TILES, :], a[:, sh:TILES, :], a[:, 0:TILES - sh, :], ALU.add))
                    a, b, sh = b, a, 2 * sh
                step(eng.tensor_scalar(tf[:, :], tf[:, :], float(P), None, ALU.mult))
                step(eng.tensor_tensor(cmp_n[:, :, :], a[:, TILES - 1, :].unsqueeze(2).broadcast_to([P, E, TILES]),
                                       tf[:, 0:TILES].unsqueeze(1).broadcast_to([P, E, TILES]), ALU.is_gt))
                step(eng.tensor_reduce(ends[:, 0, :], cmp_n[:, :, :], AX_X, ALU.add))
                step(eng.tensor_scalar(ends[:, 1, :], ends[:, 0, :], float(P), None, ALU.mult))
                step(eng.tensor_copy(ends[:, 3, :], ends[:, 1, :]))
                x, y, sh = 1, 2, 1
                while sh < E:
                    step(eng.tensor_copy(ends[:, y, 0:sh], ends[:, x, 0:sh]))
                    step(eng.tensor_tensor(ends[:, y, sh:E], ends[:, x, sh:E], ends[:, x, 0:E - sh], ALU.add))
                    x, y, sh = y, x, 2 * sh
                step(eng.tensor_tensor(ends[:, y, :], ends[:, x, :], ends[:, 3, :], ALU.subtract))
                step(eng.tensor_tensor(place[:, :, :], a[:, :, :], total, ALU.subtract))
                step(eng.tensor_tensor(place[:, :, :], place[:, :, :], before, ALU.add))
                step(eng.tensor_tensor(place[:, :, :], place[:, :, :],
                                       ends[:, y, :].unsqueeze(1).broadcast_to([P, TILES, E]), ALU.add))
                for k, h in enumerate((hot0, hot1)):
                    step(eng.tensor_tensor(h[:, :, :], h[:, :, :], place[:, :, :], ALU.mult))
                    step(eng.tensor_reduce(slot_f[:, k * TILES:(k + 1) * TILES], h[:, :, :], AX_X, ALU.add))
                step(eng.tensor_copy(slot[:, :], slot_f[:, :]))
                for t in range(TILES):
                    if t >= 4:
                        eng.wait_ge(scat[t % 4], 32 * (t // 4))
                    normed(t).then_inc(s["again"], 1)
                step(eng.tensor_tensor(cmp_t[:, :, :], ends[:, x, :].unsqueeze(1).broadcast_to([P, SORT_TILES, E]),
                                       tf[:, 0:SORT_TILES].unsqueeze(2).broadcast_to([P, SORT_TILES, E]), ALU.is_le))
                step(eng.tensor_reduce(te_f[:, :], cmp_t[:, :, :], AX_X, ALU.add))
                step(eng.tensor_scalar(te_f[:, :], te_f[:, :], float(E - 1), None, ALU.min))
                step(eng.tensor_copy(tile_expert[:, :], te_f[0:1, :]))

        with ExitStack() as ectx:
            NI = len(IC)
            xs = [sb(f"xs{i}", [P, D], where=ectx) for i in range(4)]
            xT = [sb(f"xT{i}", [P, KD, P], where=ectx) for i in range(2)]
            act_g = [sb(f"act_g{i}", [P, EI], where=ectx) for i in range(2)]
            hT = [sb(f"moe_hT{i}", [P, NI, P], where=ectx) for i in range(2)]
            ys = [sb(f"ys{i}", [P, D], where=ectx) for i in range(2)]
            bank = [ectx.enter_context(nc.psum_tensor(f"ex_bank{i}", [P, 512], F32)) for i in range(8)]
            xT_ps, gate_ps, up_ps, hT_ps, y_ps = bank[0], bank[1:3], bank[3:5], bank[5], bank[6:8]
            s = {n: ectx.enter_context(nc.semaphore("ex_" + n)) for n in (
                "xs0", "xs1", "xT_ps", "xT", "gate_ps", "up_ps", "silu", "h", "hT_ps", "hT", "y_ps", "y", "ys0", "ys1",
                "got0", "got1", "sum", "out")}
            xs_s, ys_s, got = ([s[n + "0"], s[n + "1"]] for n in ("xs", "ys", "got"))
            gat = xs
            block = ectx.enter_context(nc.Block())

            def ahead(body, eng):
                n = (SORT_TILES - 3) // 2
                with eng.Fori(0, n) as i:
                    for v in range(2):
                        body(i * 2 + v, v)
                for j in range(2 * n, SORT_TILES):
                    body(j, j % 2)

            @block.sync
            def _(eng):
                def load(j, v):
                    eng.wait_ge(s["xT_ps"], j + 1)
                    eng.dma_start(xs[v][:, :], dr["sorted"][bass.ds(j * P, P), :]).then_inc(xs_s[v], 16)

                def body(j, v):
                    if not (isinstance(j, int) and j + 2 >= SORT_TILES):
                        load(j + 2, v)
                    eng.wait_ge(s["y"], j + 3)
                    eng.dma_start(dr["done"][bass.ds(j * P, P), :], ys[v][:, :]).then_inc(ys_s[v], 16)

                load(0, 0)
                load(1, 1)
                ahead(body, eng)
                for t in range(TILES):
                    eng.wait_ge(s["sum"], 2 * t + 2)
                    eng.dma_start(out_d[bass.ds(t * P, P), :], acc[:, t, :]).then_inc(s["out"], 16)
                eng.wait_ge(s["out"], 16 * TILES)

            @block.gpsimd
            def _(eng):
                for name, n in (("xT_ps", 2), ("xT", 1), ("silu", 2), ("h", 2), ("gate_ps", 2), ("hT_ps", 2),
                                ("hT", 1), ("y_ps", 2), ("y", 2), ("ys0", 16), ("ys1", 16)):
                    eng.sem_inc(s[name], n)
                for v in range(2):
                    eng.wait_ge(ys_s[v], 16 + 16 * ((SORT_TILES + 1 - v) // 2))
                for t in range(TILES):
                    for k in range(2):
                        v = 2 * (t % 2) + k
                        if t >= 2:
                            eng.wait_ge(s["sum"], 2 * (t - 2) + k + 1)
                        eng.indirect_dma_start(out=gat[v][:, :], out_offset=None, in_=dr["done"][:, :],
                                               in_offset=bass.IndirectOffsetOnAxis(ap=slot[:, k * TILES + t:k * TILES + t + 1], axis=0))\
                           .then_inc(got[t % 2], 16)

            @block.scalar
            def _(eng):
                def turned(j, v):
                    eng.wait_ge(s["xT_ps"], j + 3)
                    eng.wait_ge(s["gate_ps"], j + 1)
                    eng.activation(xT[v][:, :, :].rearrange("p k n -> p (k n)"), xT_ps[:, :], ACT.Copy)\
                       .then_inc(s["xT"], 1)

                def gate(j, v):
                    eng.wait_ge(s["gate_ps"], j + 3)
                    eng.wait_ge(s["hT_ps"], j + 1)
                    eng.activation(act_g[v][:, :], gate_ps[v][:, 0:EI], ACT.Silu).then_inc(s["silu"], 1)

                def y_out(j, v):
                    eng.wait_ge(s["y_ps"], j + 3)
                    eng.wait_ge(ys_s[v], (j - v) * 8 + 16)
                    eng.activation(ys[v][:, :], y_ps[v][:, :], ACT.Copy).then_inc(s["y"], 1)

                turned(0, 0)
                gate(0, 0)
                turned(1, 1)

                def body(j, v):
                    last = isinstance(j, int)
                    if not (last and j + 1 >= SORT_TILES):
                        gate(j + 1, 1 - v)
                    if not (last and j + 2 >= SORT_TILES):
                        turned(j + 2, v)
                    y_out(j, v)

                ahead(body, eng)

            @block.vector
            def _(eng):
                def product(j, v):
                    eng.wait_ge(s["silu"], j + 3)
                    eng.wait_ge(s["up_ps"], j + 1)
                    eng.tensor_tensor(act_g[v][:, :], act_g[v][:, :], up_ps[v][:, 0:EI], ALU.mult).then_inc(s["h"], 1)

                def turned(j, v):
                    eng.wait_ge(s["hT_ps"], j + 3)
                    eng.wait_ge(s["y_ps"], j + 1)
                    for c, (i, n) in enumerate(IC):
                        if n == P and c == 0:
                            full = EI // P
                            eng.tensor_copy(hT[v][:, 0:full, :].rearrange("p c n -> p (c n)"), hT_ps[:, 0:full * P])
                        elif n < P:
                            eng.tensor_copy(hT[v][0:n, c, :], hT_ps[0:n, c * P:(c + 1) * P]).then_inc(s["hT"], 1)

                product(0, 0)

                def body(j, v):
                    turned(j, v)
                    if not (isinstance(j, int) and j + 1 >= SORT_TILES):
                        product(j + 1, 1 - v)

                ahead(body, eng)
                for t in range(TILES):
                    eng.wait_ge(got[t % 2], 32 * (t // 2 + 1))
                    for k in range(2):
                        if k:
                            eng.wait_ge(s["sum"], 2 * t + 1)
                        eng.scalar_tensor_tensor(acc[:, t, :], gat[2 * (t % 2) + k][:, :], weight[:, k, t:t + 1],
                                                 acc[:, t, :], ALU.mult, ALU.add).then_inc(s["sum"], 1)

            @block.tensor
            def _(eng):
                eng.wait_ge(s_w, 16 * NW)

                def turn_rows(j, v):
                    eng.wait_ge(xs_s[v], (j - v) * 8 + 16)
                    eng.wait_ge(s["xT"], j + 1)
                    for k in range(KD):
                        last = eng.transpose(xT_ps[:, k * P:(k + 1) * P], xs[v][:, k * P:(k + 1) * P], ident[:, :])
                    last.then_inc(s["xT_ps"], 1)

                def width(j, v):
                    e = eng.value_load(tile_expert[0:1, bass.ds(j, 1)], min_val=0, max_val=E - 1)
                    eng.wait_ge(s["xT"], j + 2)
                    for i, (ps, free, done) in enumerate(((gate_ps[v], "silu", "gate_ps"), (up_ps[v], "h", "up_ps"))):
                        eng.wait_ge(s[free], j + 1)
                        for k in range(KD):
                            mm = eng.matmul(ps[:, 0:EI], xT[v][:, k, :],
                                            w_gu[:, i, bass.ds(e * KD + k, 1), :].rearrange("p a n -> p (a n)"),
                                            start=(k == 0), stop=(k == KD - 1))
                        mm.then_inc(s[done], 1)
                    return e

                def turn_width(j, v):
                    eng.wait_ge(s["h"], j + 3)
                    eng.wait_ge(s["hT"], j + 1)
                    for c, (i, n) in enumerate(IC):
                        last = eng.transpose(hT_ps[0:n, c * P:(c + 1) * P], act_g[v][:, i:i + n], ident[:, :])
                    last.then_inc(s["hT_ps"], 1)

                def out(j, v):
                    e = eng.value_load(tile_expert[0:1, bass.ds(j, 1)], min_val=0, max_val=E - 1)
                    eng.wait_ge(s["hT"], j + 2)
                    eng.wait_ge(s["y"], j + 1)
                    for c, (i, n) in enumerate(IC):
                        mm = eng.matmul(y_ps[v][:, :], hT[v][0:n, c, :],
                                        w_dn[0:n, bass.ds(e * NI + c, 1), :].rearrange("p a n -> p (a n)"),
                                        start=(c == 0), stop=(c == NI - 1))
                    mm.then_inc(s["y_ps"], 1)

                turn_rows(0, 0)
                width(0, 0)
                turn_rows(1, 1)

                def body(j, v):
                    last = isinstance(j, int)
                    turn_width(j, v)
                    if not (last and j + 1 >= SORT_TILES):
                        width(j + 1, 1 - v)
                    if not (last and j + 2 >= SORT_TILES):
                        turn_rows(j + 2, v)
                    out(j, v)

                ahead(body, eng)


def mixer_ffn_experts_kernel(nc, ins, out):
    out_d = out.rearrange("b s d -> (b s) d")
    dr = {name: nc.dram_tensor(name + "_rows", (n, D), F32, kind="Internal").ap()
          for name, n in (("xh", ROWS), ("h2", ROWS), ("sorted", SORT_TILES * P), ("done", SORT_TILES * P))}
    with nc.sbuf_tensor("ident", [P, P], F32) as ident, nc.sbuf_tensor("ones", [P, P], F32) as ones:
        constants(nc, ident, ones)
        mixer(nc, ins, dr, ident, ones)
        with nc.sbuf_tensor("acc_rows", [P, TILES, D], F32) as acc:
            feed_forward(nc, ins, dr, ident, acc)
            experts(nc, ins, dr, out_d, ident, ones, acc)


_INS = ["L0_attn_hidden_states", "L0_attn_in_proj_w", "L0_attn_conv_w", "L0_attn_conv_b", "L0_attn_dt_bias",
        "L0_attn_A_log", "L0_attn_D", "L0_attn_norm_w", "L0_attn_out_proj_w", "L0_attn_ln1_w", "L0_attn_ln2_w",
        "L0_attn_gate_w", "L0_attn_up_w", "L0_attn_down_w", "L0_ffn_Wr", "L0_ffn_Wg", "L0_ffn_Wu", "L0_ffn_Wd"]
_OUT = ((1, ROWS, D), "float32")


def kernel(**inputs):
    import numpy as _np
    import concourse.bacc as _bacc
    from concourse import mybir as _mybir
    from concourse.bass_utils import run_bass_kernel_spmd as _run

    nc = _bacc.Bacc("TRN2", target_bir_lowering=False, num_devices=1)
    arrays, ins = {}, {}
    for name in _INS:
        a = _np.ascontiguousarray(inputs[name])
        arrays[f"in_{name}_dram"] = a
        ins[name] = nc.dram_tensor(f"in_{name}_dram", a.shape, _mybir.dt.from_np(a.dtype), kind="ExternalInput").ap()
    out = nc.dram_tensor("out_0_dram", _OUT[0], _mybir.dt.from_np(_np.dtype(_OUT[1])), kind="ExternalOutput").ap()
    mixer_ffn_experts_kernel(nc, ins, out)
    r = _run(nc, [arrays], core_ids=[0])
    return r.results[0]["out_0_dram"]
```

```python
from contextlib import ExitStack

import concourse.bass as bass
from concourse import mybir

F32 = mybir.dt.float32
F32R = mybir.dt.float32r
U32 = mybir.dt.uint32
ALU = mybir.AluOpType
ACT = mybir.ActivationFunctionType
AX_X = mybir.AxisListType.X

P = 128
EPS = 1e-5
ROWS = 2048
D = 512
KD = D // P
DI = 1024
HEADS, HD, DST, NG = 16, 64, 64, 4
HPG = HEADS // NG
DXB = NG * HD
NCH = (2 * DXB + DI) // P
TAPS = 4
DIN = DI + 2 * DXB + DI + HEADS
CH0 = DI
DT0 = DIN - HEADS
TILES = ROWS // P
GR = 256
NGRP = ROWS // GR
FF, FB = 2048, 256
E, EI = 8, 352
MASKED = -1.0e30
SORT_TILES = 2 * ROWS // P + E - 1
SD = D + 2
IC = [(i, min(P, EI - i)) for i in range(0, EI, P)]


def softplus_dt_steps():
    return [1.0 / n for n in (13, 11, 9, 7, 5, 3)]


def mixer(nc, ins, dr, ident, ones):
    x_d = ins["L0_attn_hidden_states"].rearrange("b s d -> (b s) d")
    with ExitStack() as ctx:
        def sb(name, shape, dt=F32):
            return ctx.enter_context(nc.sbuf_tensor(name, shape, dt))

        def sem(name):
            return ctx.enter_context(nc.semaphore(name))

        with nc.sbuf_tensor("w_c", [P, KD, DIN], F32) as w_c:
            pass
        w_in_hi = sb("w_in_hi", [P, KD, DIN], F32R)
        with nc.sbuf_tensor("w_in", [P, KD, DIN], F32) as w_in:
            pass
        w_in_lo = sb("w_in_lo", [P, KD, DIN], F32R)
        w_out = sb("w_out", [P, DI // P, D])
        ln1 = sb("ln1", [P, KD])
        ln2_row = sb("ln2_row", [P, D])
        normw = sb("normw", [P, DI // P])
        conv_w = sb("conv_w", [P, NCH, TAPS])
        conv_b = sb("conv_b", [P, NCH])
        a_neg = sb("a_neg", [P, HEADS])
        dt_bias = sb("dt_bias", [P, HEADS])
        d_skip = sb("d_skip", [P, HEADS])
        tri = sb("tri", [P, P])
        suffix = sb("suffix", [P, P])
        mask = sb("mask", [P, P])
        tri_r = sb("tri_r", [P, P], F32R)
        ident_r = sb("ident_r", [P, P], F32R)
        mask_r = sb("mask_r", [P, P], F32R)
        half_neg = sb("half_neg", [P, 1])
        xin = sb("xin", [P, 2, D])
        bn = sb("bn", [P, 2, 6])
        mv = sb("mv", [P, 2, 2, 2])
        lnq = sb("lnq", [P, 2, 2, 4])
        row_norm = sb("row_norm", [P, 2, 2])
        hT_hi = [sb(f"hT_hi{i}", [P, KD, GR], F32R) for i in range(2)]
        hT_lo = [sb(f"hT_lo{i}", [P, KD, GR], F32R) for i in range(2)]
        halo = sb("halo", [P, NCH, TAPS - 1])
        raw = [sb(f"raw{i}", [P, TAPS - 1 + GR]) for i in range(3)]
        acc = [sb(f"acc{i}", [P, GR]) for i in range(3)]
        tnh = [sb(f"tnh{i}", [P, GR]) for i in range(2)]
        cv = [sb(f"cv{i}", [P, NCH, GR]) for i in range(2)]
        sp = sb("sp", [P, 8, 2 * HEADS])
        dt = [sb(f"dt{i}", [P, 2, HEADS]) for i in range(2)]
        da = sb("da", [P, 2, HEADS])
        da_hi = [sb(f"da_hi{i}", [P, 2, HEADS], F32R) for i in range(2)]
        da_lo = [sb(f"da_lo{i}", [P, 2, HEADS], F32R) for i in range(2)]
        neg_cum = [sb(f"neg_cum{i}", [P, 2, HEADS]) for i in range(2)]
        exp_cum = [sb(f"exp_cum{i}", [P, 2, HEADS]) for i in range(2)]
        exp_suf = [sb(f"exp_suf{i}", [P, 2, HEADS]) for i in range(2)]
        chunk_decay = [sb(f"chunk_decay{i}", [P, 2, 2, HPG]) for i in range(2)]
        zs = sb("zs", [P, DI])
        xb_row = sb("xb_row", [P, 2, DXB])
        xdt = sb("xdt", [P, DI])
        dx = sb("dx", [P, DI])
        xdd = sb("xdd", [P, DI])
        decay = [sb(f"decay{i}", [P, HPG, P]) for i in range(2)]
        yrow = sb("yrow", [P, DI])
        yoff = sb("yoff", [P, HPG * HD])
        junk = sb("junk", [P, 3, D], mybir.dt.bfloat16)
        sumsq = sb("sumsq", [P, 8])
        carry = sb("carry", [P, 2, HPG, HD])
        yT = sb("yT", [P, DI // P, P])
        xres = [sb(f"xres{i}", [P, D]) for i in range(2)]
        yres = sb("yres", [P, D])
        hres = sb("hres", [P, D])
        h2 = sb("h2", [P, D])

        bank = [ctx.enter_context(nc.psum_tensor(f"mix_bank{i}", [P, 512], F32)) for i in range(8)]
        proj_ps, seg_ps, y_ps, cb_ps, misc = bank[0:2], bank[2:4], bank[4:6], bank[6], bank[7]

        s = {n: sem(n) for n in (
            "ln1_dma", "v_dma", "wa_dma", "wc_dma", "wz_dma", "wo_dma", "xin_dma", "xres_dma0", "xres_dma1",
            "xh_stored0", "xh_stored1", "h2_stored", "h2_free", "consts", "cast", "a_exp", "folded",
            "bn", "stat", "lnq_step", "normed", "row_norm", "rowT", "hT_hi", "hT_done", "w_hi", "c_hi", "z_scaled", "z_hi", "z_lo", "w_out",
            "dt_ps", "dt_v", "dt_neg", "dt_exp", "dt_step", "dt_done", "cum_ps", "cum_done",
            "ch_ps", "halo", "ch_copied", "tap", "ch_tanh", "ch_done",
            "z_ps", "z_tanh", "z_gate", "xb_ps", "xb_row", "xdt", "dx", "xdd",
            "seg0", "seg1", "cb", "exp0", "exp1", "sc0", "sc1", "yd0", "yd1", "yo0", "yo1", "yread0", "yread1",
            "yread_a", "ysum", "ygate", "state_ps", "carry_decayed", "carry_done", "sq", "r_step",
            "yT_ps", "yT_done", "out_ps", "yres", "h_done", "xh_done", "hsq", "h2_step", "passed")}
        seg_s, exp_s, sc_s, yd_s, yread_s = (
            [s[n + "0"], s[n + "1"]] for n in ("seg", "exp", "sc", "yd", "yread"))
        xres_dma, xh_stored = ([s[n + "0"], s[n + "1"]] for n in ("xres_dma", "xh_stored"))
        NLN, NDT, NR, NH2 = 6, 14, 4, 4

        def wait_apart(eng, which, value):
            eng.wait_ge(which, value)
            eng.sem_inc(s["passed"], 1)

        def head_cols(t, g):
            return t[:, g * HPG * HD:(g + 1) * HPG * HD]

        def vector_loads(cw, cb, nb):
            loads = [(normw[:, :], ins["L0_attn_norm_w"].rearrange("(k p) -> p k", p=P)),
                     (a_neg[:, :], ins["L0_attn_A_log"].partition_broadcast(P)),
                     (dt_bias[:, :], ins["L0_attn_dt_bias"].partition_broadcast(P)),
                     (d_skip[:, :], ins["L0_attn_D"].partition_broadcast(P)),
                     (ln2_row[:, :], ins["L0_attn_ln2_w"].partition_broadcast(P)),
                     (conv_w[:, 0:nb, :], cw[0:2 * DXB, :].rearrange("(k p) t -> p k t", p=P)),
                     (conv_b[:, 0:nb], cb[0:2 * DXB].rearrange("(k p) -> p k", p=P))]
            for a in range(2):
                for b in range(2):
                    half, at, src = slice(b * HD, (b + 1) * HD), nb + HPG * a, 2 * DXB + (2 * a + b) * HPG * DST
                    loads += [(conv_w[half, at:at + HPG, :],
                               cw[src:src + HPG * DST, :].rearrange("(j n) t -> n j t", j=HPG)),
                              (conv_b[half, at:at + HPG],
                               cb[src:src + HPG * DST].rearrange("(j n) -> n j", j=HPG))]
            return loads

        def c_parts():
            for k in range(KD):
                for a in range(2):
                    for b in range(2):
                        at, n = (2 * a + b) * HPG * DST, HPG * DST
                        cols = slice(c0 + a * DI // 2, c0 + (a + 1) * DI // 2)
                        yield [k, w_c[:, k, at:at + n].rearrange("p (j n) -> p j n", j=HPG)] + \
                            [w[:, k, cols].rearrange("p (j b n) -> p j b n", j=HPG, b=2)[:, :, b, :]
                             for w in (w_in_hi, w_in_lo)]

        NV = 15
        wr = ins["L0_attn_in_proj_w"].rearrange("(k p) n -> p k n", p=P)
        c0 = CH0 + 2 * DXB
        block = ctx.enter_context(nc.Block())


        def slots(run, eng):
            run(0, 0, True, False)
            with eng.Fori(0, (TILES - 4) // 4) as i:
                for k in range(1, 5):
                    run(i, k, True, k % 2 == 1)
            for k in range(1, 4):
                run(TILES // 4 - 1, k, k < 2, False)

        def first(i, k):
            return k == 0

        def last_chunk(i, k):
            return isinstance(i, int) and 4 * i + k == TILES - 1

        @block.sync
        def _(eng):
            def load_pre(g):
                for u in range(2):
                    eng.dma_start(xin[:, u, :], x_d[bass.ds((g * 2 + u) * P, P), :]).then_inc(s["xin_dma"], 16)

            def load_xres(c, b):
                eng.dma_start(xres[b][:, :], x_d[bass.ds(c * P, P), :]).then_inc(xres_dma[b], 16)

            load_pre(0)
            cw, cb = ins["L0_attn_conv_w"], ins["L0_attn_conv_b"]
            nb = 2 * DXB // P
            with nc.allow_non_contiguous_dma("small vectors"):
                eng.dma_start(ln1[:, :], ins["L0_attn_ln1_w"].rearrange("(k p) -> p k", p=P)).then_inc(s["ln1_dma"], 16)
                for dst, src in vector_loads(cw, cb, nb):
                    eng.dma_start(dst, src).then_inc(s["v_dma"], 16)
            eng.dma_start(w_c[:, :, 0:DI], wr[:, :, c0:c0 + DI]).then_inc(s["wc_dma"], 16)
            eng.dma_start(w_in[:, :, 0:DI], wr[:, :, 0:DI]).then_inc(s["wz_dma"], 16)
            eng.dma_start(w_out[:, :, :], ins["L0_attn_out_proj_w"].rearrange("(k p) n -> p k n", p=P))\
               .then_inc(s["wo_dma"], 16)
            for b in range(2):
                load_xres(b, b)

            def slot(i, k, front, pre):
                c, gf = i * 4 + k, i * 2 + k // 2 + 1
                if pre:
                    eng.wait_ge(s["rowT"], gf * 2 + 2)
                    load_pre(gf + 1)
                if first(i, k):
                    return
                b, n = (k - 1) % 2, i * 32 + (k - 1) // 2 * 16
                eng.wait_ge(s["xh_done"], c)
                eng.dma_start(dr["xh"][bass.ds((c - 1) * P, P), :], xres[b][:, :]).then_inc(xh_stored[b], 16)
                if not last_chunk(i, k):
                    eng.wait_ge(xh_stored[b], n + 16)
                    load_xres(c + 1, b)
                eng.wait_ge(s["h2_step"], (c - 1) * NH2 + NH2 + 1)
                eng.dma_start(dr["h2"][bass.ds((c - 1) * P, P), :], h2[:, :]).then_inc(s["h2_stored"], 16)
                eng.wait_ge(s["h2_stored"], c * 16)
                eng.sem_inc(s["h2_free"], 1)

            slots(slot, eng)
            eng.wait_ge(s["xh_done"], TILES)
            eng.dma_start(dr["xh"][(TILES - 1) * P:ROWS, :], xres[(TILES - 1) % 2][:, :])\
               .then_inc(xh_stored[(TILES - 1) % 2], 16)
            eng.wait_ge(s["h2_step"], TILES * NH2 + 1)
            eng.dma_start(dr["h2"][(TILES - 1) * P:ROWS, :], h2[:, :]).then_inc(s["h2_stored"], 16)
            for b in range(2):
                eng.wait_ge(xh_stored[b], 16 * TILES // 2)
            eng.wait_ge(s["h2_stored"], 16 * TILES)

        @block.gpsimd
        def _(eng):
            for name, n in (("h2_free", 1), ("ch_done", 3), ("h_done", 1), ("sc0", 1), ("sc1", 1),
                            ("exp0", 1), ("exp1", 1), ("yread0", 1), ("yread1", 1), ("yd0", 1), ("yd1", 1),
                            ("xdd", 1),
                            ("ygate", 2), ("yT_ps", 2), ("out_ps", 1), ("state_ps", 1), ("carry_done", 1),
                            ("ysum", 4), ("xdt", 1), ("h2_step", 1)):
                eng.sem_inc(s[name], n)
            eng.memset(tri[:, :], 1.0).then_inc(s["consts"], 1)
            eng.memset(suffix[:, :], 1.0).then_inc(s["consts"], 1)
            eng.memset(mask[:, :], 0.0).then_inc(s["consts"], 1)
            eng.memset(half_neg[:, :], -0.5).then_inc(s["consts"], 1)
            eng.memset(halo[:, :, :], 0.0).then_inc(s["consts"], 1)
            eng.memset(carry[:, :, :, :], 0.0).then_inc(s["consts"], 1)
            eng.wait_ge(s["consts"], 6)
            eng.affine_select(out=tri[:, :], in_=tri[:, :], compare_op=ALU.is_ge, fill=0.0, base=0,
                              pattern=[[1, P]], channel_multiplier=-1).then_inc(s["consts"], 1)
            eng.affine_select(out=suffix[:, :], in_=suffix[:, :], compare_op=ALU.is_gt, fill=0.0, base=0,
                              pattern=[[-1, P]], channel_multiplier=1).then_inc(s["consts"], 1)
            eng.affine_select(out=mask[:, :], in_=mask[:, :], compare_op=ALU.is_ge, fill=MASKED, base=0,
                              pattern=[[1, P]], channel_multiplier=-1).then_inc(s["consts"], 1)

            def norms(g, par):
                for u in range(2):
                    n = (g * 2 + u) * NLN
                    v, q = mv[:, par, u, 1:2], lnq[:, par, u, :]
                    wait_apart(eng, s["stat"], g * 2 + u + 1)
                    steps = [lambda: eng.tensor_scalar(q[:, 0:1], v, EPS, None, ALU.add),
                             lambda: eng.tensor_tensor(q[:, 1:2], q[:, 0:1], half_neg[:, :], ALU.pow),
                             lambda: eng.tensor_tensor(q[:, 0:1], q[:, 1:2], q[:, 1:2], ALU.mult),
                             lambda: eng.tensor_scalar(q[:, 0:1], q[:, 0:1], v, EPS, ALU.mult, ALU.add),
                             lambda: eng.tensor_tensor(q[:, 2:3], q[:, 0:1], half_neg[:, :], ALU.pow),
                             lambda: eng.tensor_tensor(q[:, 3:4], q[:, 1:2], q[:, 2:3], ALU.mult)]
                    for i, step in enumerate(steps):
                        if i:
                            wait_apart(eng, s["lnq_step"], n + i)
                        step().then_inc(s["lnq_step"], 1)

            norms(0, 0)
            eng.wait_ge(s["v_dma"], 16 * NV)
            def scale_z(start, stop):
                for k in range(start, stop):
                    eng.tensor_scalar(w_in[:, k, 0:DI], w_in[:, k, 0:DI], ln1[:, k:k + 1], None, ALU.mult)\
                       .then_inc(s["z_scaled"], 1)

            eng.wait_ge(s["wz_dma"], 16)
            scale_z(0, 3)
            norms(1, 1)
            scale_z(3, KD)
            for k in range(KD):
                eng.wait_ge(s["z_hi"], k + 1)
                eng.tensor_tensor(w_in_lo[:, k, 0:DI], w_in[:, k, 0:DI], w_in_hi[:, k, 0:DI].bitcast(F32),
                                  ALU.subtract).then_inc(s["z_lo"], 1)

            def scaled_x(i, k):
                c, g, u, par = i * 4 + k, i * 2 + k // 2, k % 2, (k // 2) % 2
                hb = lambda t: t.unsqueeze(2).broadcast_to([P, HEADS, HD])
                xr = xb_row[:, 0, :].rearrange("p (g d) -> p g d", g=NG).unsqueeze(2).broadcast_to([P, NG, HPG, HD])
                eng.wait_ge(s["xb_row"], c + 1)
                eng.wait_ge(s["ysum"], c * 4 + 4)
                eng.tensor_tensor(dx[:, :].rearrange("p (g r d) -> p g r d", g=NG, r=HPG), xr,
                                  d_skip[:, :].rearrange("p (g r) -> p g r", g=NG).unsqueeze(3)
                                  .broadcast_to([P, NG, HPG, HD]), ALU.mult).then_inc(s["dx"], 1)
                eng.wait_ge(s["xdt"], c + 2)
                eng.wait_ge(s["cum_done"], g + 1)
                eng.wait_ge(s["state_ps"], c + 1)
                eng.tensor_tensor(xdd[:, :].rearrange("p (h d) -> p h d", h=HEADS),
                                  xdt[:, :].rearrange("p (h d) -> p h d", h=HEADS),
                                  hb(exp_suf[par][:, u, :]), ALU.mult).then_inc(s["xdd"], 1)

            def norm_scale(e):
                n = e * NR
                eng.wait_ge(s["sq"], e * 2 + 2)
                a = sumsq[:, 2:3]
                steps = [lambda: eng.tensor_tensor(a, sumsq[:, 0:1], sumsq[:, 1:2], ALU.add),
                         lambda: eng.tensor_scalar(a, a, 0.25 / DI, EPS, ALU.mult, ALU.add),
                         lambda: eng.tensor_tensor(a, a, half_neg[:, :], ALU.pow),
                         lambda: eng.tensor_scalar(sumsq[:, 3:4], a, 0.5, None, ALU.mult)]
                for i, step in enumerate(steps):
                    if i:
                        wait_apart(eng, s["r_step"], n + i)
                    step().then_inc(s["r_step"], 1)

            def residual(e, b):
                eng.wait_ge(s["h_done"], e + 2)
                eng.tensor_tensor(xres[b][:, :], hres[:, :], xres[b][:, :], ALU.add).then_inc(s["xh_done"], 1)

            def second_norm(e):
                n = e * NH2
                wait_apart(eng, s["hsq"], e + 1)
                b = sumsq[:, 5:6]
                steps = [lambda: eng.tensor_scalar(b, sumsq[:, 4:5], 1.0 / D, EPS, ALU.mult, ALU.add),
                         lambda: eng.tensor_tensor(b, b, half_neg[:, :], ALU.pow),
                         lambda: eng.tensor_scalar(h2[:, :], hres[:, :], b, None, ALU.mult),
                         lambda: eng.tensor_tensor(h2[:, :], h2[:, :], ln2_row[:, :], ALU.mult)]
                for i, step in enumerate(steps):
                    if i == 2:
                        wait_apart(eng, s["h2_free"], e + 1)
                    if i:
                        wait_apart(eng, s["h2_step"], n + i + 1)
                    step().then_inc(s["h2_step"], 1)

            scaled_x(0, 0)

            def slot(i, k, front, pre):
                c, gf, u, par = i * 4 + k, i * 2 + k // 2 + 1, k % 2, (k // 2) % 2
                if not first(i, k):
                    norm_scale(c - 1)
                if pre:
                    norms(gf + 1, par)
                if not first(i, k):
                    residual(c - 1, (k - 1) % 2)
                    second_norm(c - 1)
                eng.wait_ge(s["yd1"], c * 2 + 3)
                eng.wait_ge(s["carry_done"], c + 1)
                eng.tensor_tensor(carry[:, :, :, :].rearrange("p a j d -> p (a j) d"),
                                  carry[:, :, :, :].rearrange("p a j d -> p (a j) d"),
                                  chunk_decay[par][:, u, :, :].rearrange("p a j -> p (a j)").unsqueeze(2)
                                  .broadcast_to([P, 2 * HPG, HD]), ALU.mult).then_inc(s["carry_decayed"], 1)
                if not last_chunk(i, k):
                    scaled_x(i, k + 1)

            slots(slot, eng)
            norm_scale(TILES - 1)
            residual(TILES - 1, (TILES - 1) % 2)
            second_norm(TILES - 1)

        @block.scalar
        def _(eng):
            eng.dma_start(w_in[:, :, DT0:DIN], wr[:, :, DT0:DIN]).then_inc(s["wa_dma"], 16)
            eng.dma_start(w_in[:, :, CH0:c0], wr[:, :, CH0:c0]).then_inc(s["wa_dma"], 16)
            def copy_hT(g, par, u):
                eng.wait_ge(s["rowT"], g * 2 + u + 1)
                eng.activation(hT_hi[par][:, :, u * P:(u + 1) * P], misc[:, :].rearrange("p (k n) -> p k n", k=KD),
                               ACT.Copy).then_inc(s["hT_hi"], 1)

            def fold_hi(lo, hi):
                for k in range(KD):
                    last = eng.activation(w_in_hi[:, k, lo:hi], w_in[:, k, lo:hi], ACT.Copy, scale=ln1[:, k:k + 1])
                last.then_inc(s["w_hi"], 1)

            def dt_exp(g):
                eng.wait_ge(s["dt_neg"], g + 1)
                eng.activation(sp[:, 2, :], sp[:, 1, :], ACT.Exp).then_inc(s["dt_exp"], 1)

            def cum_exps(g, par):
                eng.wait_ge(s["cum_ps"], g + 1)
                f = lambda t: t[:, :, :].rearrange("p u h -> p (u h)")
                eng.activation(f(neg_cum[par]), misc[:, 0:32], ACT.Copy, scale=-1.0)
                eng.activation(f(exp_cum[par]), misc[:, 0:32], ACT.Exp)
                eng.activation(f(exp_suf[par]), misc[:, 32:64], ACT.Exp)
                for b in range(2):
                    h = slice(b * HD, (b + 1) * HD)
                    tot = misc[h, 64:96].rearrange("p (u a b j) -> p (u a) b j", u=2, a=2, b=2)[:, :, b, :]
                    last = eng.activation(chunk_decay[par][h, :, :, :].rearrange("p u a j -> p (u a) j"), tot, ACT.Exp)
                last.then_inc(s["cum_done"], 1)

            def copy_ch(g, ch):
                n = g * NCH + ch
                eng.wait_ge(s["ch_ps"], n + 1)
                eng.wait_ge(s["ch_done"], n + 1)
                ps = proj_ps[ch % 2][:, 0:GR]
                eng.activation(raw[ch % 3][:, 0:TAPS - 1], halo[:, ch, :], ACT.Copy).then_inc(s["halo"], 1)
                eng.activation(acc[ch % 3][:, :], ps, ACT.Identity, bias=conv_b[:, ch:ch + 1],
                               scale=conv_w[:, ch, TAPS - 1:TAPS])
                eng.wait_ge(s["halo"], n + 1)
                eng.activation(halo[:, ch, :], proj_ps[ch % 2][:, GR - TAPS + 1:GR], ACT.Copy)
                eng.activation(raw[ch % 3][:, TAPS - 1:TAPS - 1 + GR], ps, ACT.Copy).then_inc(s["ch_copied"], 1)

            def tanh_ch(g, ch):
                n = g * NCH + ch
                eng.wait_ge(s["tap"], n * 3 + 3)
                eng.wait_ge(s["ch_done"], n + 2)
                eng.activation(tnh[ch % 2][:, :], acc[ch % 3][:, :], ACT.Tanh).then_inc(s["ch_tanh"], 1)

            eng.wait_ge(s["consts"], 9)
            for u in range(2):
                copy_hT(0, 0, u)
            for u in range(2):
                eng.dma_start(xin[:, u, :], x_d[(2 + u) * P:(3 + u) * P, :]).then_inc(s["xin_dma"], 16)
            eng.wait_ge(s["wa_dma"], 32)
            eng.wait_ge(s["ln1_dma"], 16)
            fold_hi(DT0, DIN)
            fold_hi(CH0, CH0 + 2 * DXB)
            eng.wait_ge(s["v_dma"], 16 * NV)
            eng.activation(a_neg[:, :], a_neg[:, :], ACT.Exp).then_inc(s["a_exp"], 1)
            eng.wait_ge(s["wc_dma"], 16)
            for k, src, hi, _ in c_parts():
                eng.activation(hi, src, ACT.Copy, scale=ln1[:, k:k + 1]).then_inc(s["c_hi"], 1)
            eng.wait_ge(s["folded"], 3)
            dt_exp(0)
            for ch in range(NCH):
                copy_ch(0, ch)
                if ch == 1:
                    cum_exps(0, 0)
                if ch in (2, 4):
                    copy_hT(1, 1, ch // 2 - 1)
                if ch:
                    tanh_ch(0, ch - 1)
                if 4 <= ch < 4 + KD:
                    if ch == 4:
                        eng.wait_ge(s["folded"], 4)
                    k = ch - 4
                    eng.wait_ge(s["z_scaled"], k + 1)
                    eng.activation(w_in_hi[:, k, 0:DI], w_in[:, k, 0:DI], ACT.Copy).then_inc(s["z_hi"], 1)
            tanh_ch(0, NCH - 1)
            eng.wait_ge(s["wo_dma"], 16)
            for k in range(DI // P):
                last = eng.activation(w_out[:, k, :], w_out[:, k, :], ACT.Copy, scale=normw[:, k:k + 1])
            last.then_inc(s["w_out"], 1)

            def next_rows(c):
                for j in range(2):
                    eng.wait_ge(s["z_ps"], c * 2 + j + 1)
                    eng.wait_ge(s["ygate"], c * 2 + j + 1)
                    eng.activation(zs[:, j * 512:(j + 1) * 512], proj_ps[j][:, :], ACT.Tanh, scale=0.5)\
                       .then_inc(s["z_tanh"], 1)
                eng.wait_ge(s["xb_ps"], c + 1)
                eng.wait_ge(s["xdd"], c + 1)
                eng.wait_ge(s["state_ps"], c + 1)
                eng.activation(xb_row[:, :, :].rearrange("p a d -> p (a d)"), misc[:, :], ACT.Copy)\
                   .then_inc(s["xb_row"], 1)

            def turned(e, j):
                eng.wait_ge(s["yT_ps"], e * 2 + j + 3)
                eng.wait_ge(s["out_ps"], e + 1)
                eng.activation(yT[:, j * 4:j * 4 + 4, :].rearrange("p k n -> p (k n)"), misc[:, :], ACT.Copy)\
                   .then_inc(s["yT_done"], 1)

            def h_squares(e):
                eng.wait_ge(s["h_done"], e + 2)
                eng.activation(junk[:, 2, :], hres[:, :], ACT.Square, accum_out=sumsq[:, 4:5]).then_inc(s["hsq"], 1)

            next_rows(0)

            def slot(i, k, front, pre):
                c, gf, u, par = i * 4 + k, i * 2 + k // 2 + 1, k % 2, (k // 2) % 2
                half = u * (NCH // 2)

                def exps(hg):
                    eng.wait_ge(seg_s[hg % 2], c * 2 + hg // 2 + 1)
                    eng.wait_ge(yd_s[hg % 2], c * 2 + hg // 2 + 1)
                    for j in range(HPG):
                        last = eng.activation(decay[hg % 2][:, j, :], seg_ps[hg % 2][:, j * P:(j + 1) * P], ACT.Exp,
                                              bias=neg_cum[par][:, u, hg * HPG + j:hg * HPG + j + 1])
                    last.then_inc(exp_s[hg % 2], 1)

                exps(0)
                if front:
                    copy_ch(gf, half + 0)
                if not first(i, k):
                    turned(c - 1, 0)
                exps(1)
                if not first(i, k):
                    turned(c - 1, 1)
                if front:
                    if u == 1:
                        cum_exps(gf, 1 - par)
                    tanh_ch(gf, half + 0)
                    copy_ch(gf, half + 1)
                exps(2)
                if front:
                    tanh_ch(gf, half + 1)
                    copy_ch(gf, half + 2)
                exps(3)
                if front:
                    tanh_ch(gf, half + 2)
                    copy_ch(gf, half + 3)
                if not first(i, k):
                    h_squares(c - 1)
                if front:
                    tanh_ch(gf, half + 3)
                    copy_ch(gf, half + 4)
                if pre:
                    copy_hT(gf + 1, par, 0)
                if front:
                    tanh_ch(gf, half + 4)
                    copy_ch(gf, half + 5)
                    if u == 0:
                        dt_exp(gf)
                if pre:
                    copy_hT(gf + 1, par, 1)
                if front:
                    tanh_ch(gf, half + 5)
                for j in range(2):
                    eng.wait_ge(s["ygate"], c * 2 + j + 3)
                    eng.activation(junk[:, j, :], yrow[:, j * 512:(j + 1) * 512], ACT.Square,
                                   accum_out=sumsq[:, j:j + 1]).then_inc(s["sq"], 1)
                if not last_chunk(i, k):
                    next_rows(c + 1)

            slots(slot, eng)
            for j in range(2):
                turned(TILES - 1, j)
            h_squares(TILES - 1)

        @block.vector
        def _(eng):
            def norm_rows(g, par):
                for u in range(2):
                    eng.wait_ge(s["lnq_step"], (g * 2 + u + 1) * NLN)
                    eng.tensor_scalar(xin[:, u, :], xin[:, u, :], mv[:, par, u, 0:1], lnq[:, par, u, 3:4],
                                      ALU.subtract, ALU.mult).then_inc(s["normed"], 1)

            def rows_in(g, par):
                eng.wait_ge(s["xin_dma"], (g + 1) * 32)
                for u in range(2):
                    eng.bn_stats(bn[:, u, :], xin[:, u, :]).then_inc(s["bn"], 1)
                for u in range(2):
                    wait_apart(eng, s["bn"], g * 2 + u + 1)
                    eng.bn_aggr(mv[:, par, u, :], bn[:, u, :]).then_inc(s["stat"], 1)

            def dt_first(g):
                eng.wait_ge(s["dt_ps"], g + 1)
                eng.tensor_tensor(sp[:, 0, :].rearrange("p (u h) -> p u h", u=2),
                                  misc[:, 0:32].rearrange("p (u h) -> p u h", u=2),
                                  dt_bias[:, :].unsqueeze(1).broadcast_to([P, 2, HEADS]), ALU.add).then_inc(s["dt_v"], 1)
                eng.wait_ge(s["dt_v"], g + 1)
                eng.scalar_tensor_tensor(sp[:, 1, :], sp[:, 0, :], -1.0, sp[:, 0, :], ALU.mult, ALU.min)\
                   .then_inc(s["dt_neg"], 1)

            def dt_rest(g, par):
                v, e, q, ss, s2, pl = (sp[:, i, :] for i in (0, 2, 3, 4, 5, 6))
                flat = lambda t: t[:, :, :].rearrange("p u h -> p (u h)")
                eng.wait_ge(s["dt_exp"], g + 1)
                steps = [lambda: eng.tensor_scalar(q, e, 2.0, None, ALU.add),
                         lambda: eng.reciprocal(q, q),
                         lambda: eng.tensor_tensor(ss, e, q, ALU.mult),
                         lambda: eng.tensor_tensor(s2, ss, ss, ALU.mult),
                         lambda: eng.tensor_scalar(pl, s2, 1.0 / 15, None, ALU.mult)]
                for cf in softplus_dt_steps():
                    steps.append(lambda cf=cf: eng.scalar_tensor_tensor(pl, pl, cf, s2, ALU.add, ALU.mult))
                steps += [lambda: eng.scalar_tensor_tensor(pl, pl, 1.0, ss, ALU.add, ALU.mult),
                          lambda: eng.tensor_scalar(v, v, 0.0, None, ALU.max),
                          lambda: eng.scalar_tensor_tensor(flat(dt[par]), pl, 2.0, v, ALU.mult, ALU.add)]
                assert len(steps) == NDT
                for i, step in enumerate(steps):
                    if i:
                        eng.wait_ge(s["dt_step"], g * NDT + i)
                    step().then_inc(s["dt_step"], 1)
                eng.wait_ge(s["dt_step"], g * NDT + NDT)
                eng.tensor_tensor(da[:, :, :], dt[par][:, :, :], a_neg[:, :].unsqueeze(1).broadcast_to([P, 2, HEADS]),
                                  ALU.mult).then_inc(s["dt_done"], 1)
                eng.wait_ge(s["dt_done"], g * 3 + 1)
                eng.tensor_copy(da_hi[par][:, :, :], da[:, :, :]).then_inc(s["dt_done"], 1)
                eng.wait_ge(s["dt_done"], g * 3 + 2)
                eng.tensor_tensor(da_lo[par][:, :, :], da[:, :, :], da_hi[par][:, :, :].bitcast(F32),
                                  ALU.subtract).then_inc(s["dt_done"], 1)

            def taps(g, ch):
                n = g * NCH + ch
                eng.wait_ge(s["ch_copied"], n + 1)
                for t in range(TAPS - 1):
                    if t:
                        eng.wait_ge(s["tap"], n * 3 + t)
                    eng.scalar_tensor_tensor(acc[ch % 3][:, :], raw[ch % 3][:, t:t + GR], conv_w[:, ch, t:t + 1],
                                             acc[ch % 3][:, :], ALU.mult, ALU.add).then_inc(s["tap"], 1)

            def silu_ch(g, par, ch):
                n = g * NCH + ch
                eng.wait_ge(s["ch_tanh"], n + 1)
                eng.scalar_tensor_tensor(cv[par][:, ch, :], tnh[ch % 2][:, :], 1.0, acc[ch % 3][:, :],
                                         ALU.add, ALU.mult).then_inc(s["ch_done"], 1)

            def low_hT(g, par, u):
                eng.wait_ge(s["hT_hi"], g * 2 + u + 1)
                cols = slice(u * P, (u + 1) * P)
                eng.tensor_tensor(hT_lo[par][:, :, cols], misc[:, :].rearrange("p (k n) -> p k n", k=KD),
                                  hT_hi[par][:, :, cols].bitcast(F32), ALU.subtract).then_inc(s["hT_done"], 1)

            folds = iter(range(1, 3))

            def fold_lo(lo, hi):
                eng.wait_ge(s["w_hi"], next(folds))
                for k in range(KD):
                    last = eng.scalar_tensor_tensor(w_in_lo[:, k, lo:hi], w_in[:, k, lo:hi], ln1[:, k:k + 1],
                                                    w_in_hi[:, k, lo:hi].bitcast(F32), ALU.mult, ALU.subtract)
                last.then_inc(s["folded"], 1)

            rows_in(0, 0)
            norm_rows(0, 0)
            for u in range(2):
                low_hT(0, 0, u)
            eng.wait_ge(s["wa_dma"], 32)
            fold_lo(DT0, DIN)
            fold_lo(CH0, CH0 + 2 * DXB)
            eng.wait_ge(s["v_dma"], 16 * NV)
            eng.tensor_scalar(conv_w[:, :, :], conv_w[:, :, :], 0.5, None, ALU.mult)
            eng.tensor_scalar(conv_b[:, :], conv_b[:, :], 0.5, None, ALU.mult)
            eng.wait_ge(s["a_exp"], 1)
            eng.tensor_scalar(a_neg[:, :], a_neg[:, :], -1.0, None, ALU.mult)
            eng.wait_ge(s["consts"], 9)
            eng.tensor_copy(tri_r[:, :], tri[:, :])
            eng.tensor_copy(mask_r[:, :], mask[:, :])
            eng.tensor_copy(ident_r[:, :], ident[:, :]).then_inc(s["folded"], 1)
            for n, (k, src, hi, lo) in enumerate(c_parts()):
                eng.wait_ge(s["c_hi"], n + 1)
                last = eng.scalar_tensor_tensor(lo, src, ln1[:, k:k + 1], hi.bitcast(F32), ALU.mult, ALU.subtract)
            last.then_inc(s["folded"], 1)
            eng.wait_ge(s["folded"], 4)
            dt_first(0)
            dt_rest(0, 0)
            for ch in range(NCH):
                taps(0, ch)
                if ch == 0:
                    rows_in(1, 1)
                if ch == 1:
                    norm_rows(1, 1)
                if ch in (2, 4):
                    low_hT(1, 1, ch // 2 - 1)
                if ch:
                    silu_ch(0, 0, ch - 1)
            silu_ch(0, 0, NCH - 1)

            def new_carry(c):
                eng.wait_ge(s["state_ps"], c + 2)
                eng.wait_ge(s["carry_decayed"], c + 1)
                eng.tensor_tensor(carry[:, :, :, :].rearrange("p a j d -> p (a j d)"),
                                  carry[:, :, :, :].rearrange("p a j d -> p (a j d)"), misc[:, :], ALU.add)\
                   .then_inc(s["carry_done"], 1)

            def next_rows(i, k, dt_of=None):
                c, u, par = i * 4 + k, k % 2, (k // 2) % 2
                for j in range(2):
                    if j == 1 and dt_of:
                        dt_rest(*dt_of)
                    if j == 1 and u == 0 and not first(i, k):
                        new_carry(c - 1)
                    eng.wait_ge(s["z_tanh"], c * 2 + j + 1)
                    zj = zs[:, j * 512:(j + 1) * 512]
                    eng.scalar_tensor_tensor(zj, zj, 1.0, proj_ps[j][:, :], ALU.add, ALU.mult)\
                       .then_inc(s["z_gate"], 1)
                eng.wait_ge(s["xb_row"], c + 1)
                eng.wait_ge(s["yd1"], c * 2 + 1)
                eng.wait_ge(s["xdd"], c + 1)
                xr = xb_row[:, 0, :].rearrange("p (g d) -> p g d", g=NG).unsqueeze(2).broadcast_to([P, NG, HPG, HD])
                eng.tensor_tensor(xdt[:, :].rearrange("p (g r d) -> p g r d", g=NG, r=HPG), xr,
                                  dt[par][:, u, :].rearrange("p (g r) -> p g r", g=NG).unsqueeze(3)
                                  .broadcast_to([P, NG, HPG, HD]), ALU.mult).then_inc(s["xdt"], 1)

            def outcome(e):
                eng.wait_ge(s["out_ps"], e + 2)
                eng.wait_ge(s["r_step"], e * NR + NR)
                eng.wait_ge(s["h2_step"], e * NH2 + 1)
                eng.wait_ge(s["yres"], e + 1)
                eng.scalar_tensor_tensor(hres[:, :], misc[:, :], sumsq[:, 3:4], yres[:, :], ALU.mult, ALU.add)\
                   .then_inc(s["h_done"], 1)

            next_rows(0, 0)

            def slot(i, k, front, pre):
                c, gf, u, par = i * 4 + k, i * 2 + k // 2 + 1, k % 2, (k // 2) % 2
                half = u * (NCH // 2)

                def scores(hg):
                    eng.wait_ge(exp_s[hg % 2], c * 2 + hg // 2 + 2)
                    eng.wait_ge(s["cb"], c * 4 + hg + 1)
                    eng.tensor_tensor(decay[hg % 2][:, :, :], decay[hg % 2][:, :, :],
                                      cb_ps[:, :].rearrange("p (j q) -> p j q", j=HPG), ALU.mult)\
                       .then_inc(sc_s[hg % 2], 1)

                def sums(hg):
                    n = c * 4 + hg
                    eng.wait_ge(yd_s[hg % 2], c * 2 + hg // 2 + 2)
                    if hg == 0:
                        eng.wait_ge(s["xdd"], c + 2)
                    if hg % 2 == 0:
                        eng.wait_ge(s["yT_ps"], c * 2 + hg // 2 + 1)
                    ps = y_ps[hg % 2]
                    yd = head_cols(yrow, hg)
                    eng.tensor_tensor(yd, ps[:, 0:HPG * HD], head_cols(dx, hg), ALU.add).then_inc(s["yread_a"], 1)
                    eng.tensor_tensor(yoff[:, :].rearrange("p (j d) -> p j d", j=HPG),
                                      ps[:, HPG * HD:2 * HPG * HD].rearrange("p (j d) -> p j d", j=HPG),
                                      exp_cum[par][:, u, hg * HPG:(hg + 1) * HPG].unsqueeze(2)
                                      .broadcast_to([P, HPG, HD]), ALU.mult).then_inc(yread_s[hg % 2], 1)
                    eng.wait_ge(s["yread_a"], n + 1)
                    eng.wait_ge(yread_s[hg % 2], c * 2 + hg // 2 + 2)
                    eng.tensor_tensor(yd, yd, yoff[:, :], ALU.add).then_inc(s["ysum"], 1)

                def gate(j):
                    eng.wait_ge(s["ysum"], c * 4 + 2 * j + 6)
                    eng.wait_ge(s["z_gate"], c * 2 + j + 1)
                    h = slice(j * 512, (j + 1) * 512)
                    eng.tensor_tensor(yrow[:, h], yrow[:, h], zs[:, h], ALU.mult).then_inc(s["ygate"], 1)

                scores(0)
                if front:
                    taps(gf, half + 0)
                if pre:
                    rows_in(gf + 1, par)
                sums(0)
                scores(1)
                if front:
                    silu_ch(gf, 1 - par, half + 0)
                    taps(gf, half + 1)
                sums(1)
                gate(0)
                scores(2)
                if front:
                    silu_ch(gf, 1 - par, half + 1)
                if pre:
                    norm_rows(gf + 1, par)
                if front:
                    taps(gf, half + 2)
                sums(2)
                scores(3)
                if front:
                    silu_ch(gf, 1 - par, half + 2)
                if not first(i, k):
                    outcome(c - 1)
                if front:
                    taps(gf, half + 3)
                    silu_ch(gf, 1 - par, half + 3)
                if pre:
                    low_hT(gf + 1, par, 0)
                if front:
                    taps(gf, half + 4)
                    if u == 0:
                        dt_first(gf)
                sums(3)
                gate(1)
                if u == 0:
                    new_carry(c)
                if pre:
                    low_hT(gf + 1, par, 1)
                if front:
                    silu_ch(gf, 1 - par, half + 4)
                    taps(gf, half + 5)
                    silu_ch(gf, 1 - par, half + 5)
                eng.wait_ge(s["h_done"], c + 1)
                if u == 0:
                    eng.tensor_copy(row_norm[:, :, 0], mv[:, par, :, 0]).then_inc(s["row_norm"], 1)
                    eng.tensor_copy(row_norm[:, :, 1], lnq[:, par, :, 1]).then_inc(s["row_norm"], 1)
                eng.wait_ge(s["row_norm"], i * 4 + k // 2 * 2 + 2)
                eng.wait_ge(xres_dma[u], i * 32 + k // 2 * 16 + 16)
                eng.tensor_scalar(yres[:, :], xres[u][:, :], row_norm[:, u, 0:1], row_norm[:, u, 1:2],
                                  ALU.subtract, ALU.mult).then_inc(s["yres"], 1)
                if not last_chunk(i, k):
                    next_rows(i, k + 1, (gf, 1 - par) if front and u == 0 else None)

            slots(slot, eng)
            new_carry(TILES - 1)
            outcome(TILES - 1)

        @block.tensor
        def _(eng):
            def hT_parts(par, cols):
                return [t[par][:, :, cols] for t in (hT_hi, hT_lo)]

            def w_parts(lo, hi):
                return [t[:, :, lo:hi] for t in (w_in_hi, w_in_lo)]

            def product(ps, x, w):
                for k in range(KD):
                    for n, (i, j) in enumerate(((0, 0), (0, 1), (1, 0))):
                        mm = eng.matmul(ps, x[i][:, k, :], w[j][:, k, :], start=(k == 0 and n == 0),
                                        stop=(k == KD - 1 and n == 2))
                return mm

            def row_transposes(g, par, u):
                eng.wait_ge(s["normed"], g * 2 + u + 1)
                for k in range(KD):
                    last = eng.transpose(misc[:, k * P:(k + 1) * P], xin[:, u, k * P:(k + 1) * P], ident[:, :])
                last.then_inc(s["rowT"], 1)

            def dt_proj(g, par):
                eng.wait_ge(s["hT_done"], g * 2 + 2)
                for u in range(2):
                    last = product(misc[:, u * HEADS:(u + 1) * HEADS], hT_parts(par, slice(u * P, (u + 1) * P)),
                                   w_parts(DT0, DIN))
                last.then_inc(s["dt_ps"], 1)

            def cum_sums(g, par):
                eng.wait_ge(s["dt_done"], g * 3 + 3)
                rhs = da[:, :, :].rearrange("p u h -> p (u h)")
                for i, w in enumerate((tri, suffix, ones)):
                    last = eng.matmul(misc[:, i * 32:(i + 1) * 32], w[:, :], rhs, start=True, stop=True)
                last.then_inc(s["cum_ps"], 1)

            def channel_block(g, par, ch):
                col = CH0 + ch * P
                last = product(proj_ps[ch % 2][:, 0:GR], w_parts(col, col + P), hT_parts(par, slice(0, GR)))
                last.then_inc(s["ch_ps"], 1)

            def z_rows(i, k, j, front):
                c, u, par = i * 4 + k, k % 2, (k // 2) % 2
                if front:
                    eng.wait_ge(s["ch_copied"], NCH + c * (NCH // 2) - 1 + j)
                else:
                    eng.wait_ge(s["z_gate"], c * 2 - 1 + j)
                product(proj_ps[j][:, :], hT_parts(par, slice(u * P, (u + 1) * P)),
                        w_parts(j * 512, (j + 1) * 512)).then_inc(s["z_ps"], 1)

            def xb_rows(i, k):
                g, u, par = i * 2 + k // 2, k % 2, (k // 2) % 2
                eng.wait_ge(s["ch_done"], g * NCH + 4 + 3)
                for n in range(4):
                    last = eng.transpose(misc[:, n * P:(n + 1) * P], cv[par][:, n, u * P:(u + 1) * P], ident[:, :])
                last.then_inc(s["xb_ps"], 1)

            def turn_gated(e, j):
                eng.wait_ge(s["ygate"], e * 2 + j + 3)
                for n in range(4):
                    f = (j * 4 + n) * P
                    last = eng.transpose(misc[:, n * P:(n + 1) * P], yrow[:, f:f + P], ident[:, :])
                last.then_inc(s["yT_ps"], 1)

            def out_proj(e, start, stop):
                if start == 0:
                    eng.wait_ge(s["w_out"], 1)
                    eng.wait_ge(s["yT_done"], e * 2 + 2)
                for n in range(start, stop):
                    last = eng.matmul(misc[:, :], yT[:, n, :], w_out[:, n, :], start=(n == 0), stop=(n == DI // P - 1))
                if stop == DI // P:
                    last.then_inc(s["out_ps"], 1)

            row_transposes(0, 0, 0)
            eng.wait_ge(s["hT_done"], 1)
            row_transposes(0, 0, 1)
            eng.wait_ge(s["folded"], 2)
            dt_proj(0, 0)
            for ch in range(NCH):
                if ch == 4:
                    eng.wait_ge(s["folded"], 4)
                if ch >= 2:
                    eng.wait_ge(s["ch_copied"], ch - 1)
                channel_block(0, 0, ch)
                if ch == 1:
                    cum_sums(0, 0)
                if ch in (2, 4):
                    eng.wait_ge(s["cum_done"], 1)
                    eng.wait_ge(s["hT_done"], 1 + ch // 2)
                    row_transposes(1, 1, ch // 2 - 1)
            eng.wait_ge(s["z_lo"], KD)
            for j in range(2):
                z_rows(0, 0, j, True)
            eng.wait_ge(s["hT_done"], 4)
            xb_rows(0, 0)

            def slot(i, k, front, pre):
                c, gf, u, par = i * 4 + k, i * 2 + k // 2 + 1, k % 2, (k // 2) % 2
                half = u * (NCH // 2)
                tile = slice(u * P, (u + 1) * P)

                def seg(hg):
                    eng.wait_ge(exp_s[hg % 2], c * 2 + hg // 2 + 1)
                    ps = seg_ps[hg % 2]
                    eng.matmul(ps[:, :], ident_r[:, :], mask_r[:, :].unsqueeze(1).broadcast_to([P, HPG, P]),
                               start=True, stop=False, skip_group_check=True)
                    for j in range(HPG):
                        h = hg * HPG + j
                        for part in (da_hi, da_lo):
                            last = eng.matmul(ps[:, j * P:(j + 1) * P],
                                              part[par][:, u, h:h + 1].broadcast_to([P, P]), tri_r[:, :],
                                              start=False, stop=(part is da_lo and j == HPG - 1),
                                              skip_group_check=True)
                    last.then_inc(seg_s[hg % 2], 1)

                def b_dot_c(hg):
                    a, b = hg // 2, hg % 2
                    p = slice(b * HD, (b + 1) * HD)
                    if hg == 0:
                        eng.wait_ge(s["ch_done"], gf * NCH + 3)
                    eng.wait_ge(sc_s[(hg + 1) % 2], c * 2 + (hg + 1) // 2 + 1)
                    eng.matmul(cb_ps[:, :], cv[par][p, 2 + a, tile],
                               cv[par][p, 4 + 4 * a:8 + 4 * a, tile], start=True, stop=True).then_inc(s["cb"], 1)

                def outputs(hg):
                    a, b = hg // 2, hg % 2
                    p = slice(b * HD, (b + 1) * HD)
                    if hg == 0:
                        eng.wait_ge(s["carry_done"], c + 1)
                        eng.wait_ge(s["xdt"], c + 2)
                    eng.wait_ge(yread_s[hg % 2], c * 2 + hg // 2 + 1)
                    n = HPG * HD
                    for j in range(HPG):
                        eng.matmul(y_ps[hg % 2][:, n + j * HD:n + (j + 1) * HD], cv[par][p, 4 + 4 * a + j, tile],
                                   carry[p, a, j, :], start=True, stop=True)
                    eng.wait_ge(sc_s[hg % 2], c * 2 + hg // 2 + 2)
                    for j in range(HPG):
                        h = hg * HPG + j
                        last = eng.matmul(y_ps[hg % 2][:, j * HD:(j + 1) * HD], decay[hg % 2][:, j, :],
                                          xdt[:, h * HD:(h + 1) * HD], start=True, stop=True)
                    last.then_inc(yd_s[hg % 2], 1)

                def front_block(i):
                    if i < 2:
                        eng.wait_ge(s["z_gate"], c * 2 + i + 1)
                    else:
                        eng.wait_ge(s["ch_copied"], gf * NCH + half + i - 1)
                    channel_block(gf, 1 - par, half + i)

                def states():
                    eng.wait_ge(s["xdd"], c + 2)
                    n = HPG * HD
                    for hg in range(NG):
                        a, b = hg // 2, hg % 2
                        last = eng.matmul(misc[b * HD:(b + 1) * HD, a * n:(a + 1) * n],
                                          xb_row[:, 1, hg * HD:(hg + 1) * HD], xdd[:, hg * n:(hg + 1) * n],
                                          start=True, stop=True)
                    last.then_inc(s["state_ps"], 1)

                seg(0)
                b_dot_c(0)
                eng.wait_ge(s["xb_row"], c + 1)
                if front:
                    front_block(0)
                if not first(i, k):
                    turn_gated(c - 1, 0)
                seg(1)
                if not first(i, k):
                    eng.wait_ge(s["yT_done"], c * 2 - 1)
                    turn_gated(c - 1, 1)
                outputs(0)
                if front and u == 1:
                    eng.wait_ge(s["yT_done"], c * 2)
                    cum_sums(gf, 1 - par)
                b_dot_c(1)
                if not first(i, k):
                    if front and u == 1:
                        eng.wait_ge(s["cum_done"], gf + 1)
                    out_proj(c - 1, 0, 3)
                if front:
                    front_block(1)
                seg(2)
                outputs(1)
                b_dot_c(2)
                if not first(i, k):
                    out_proj(c - 1, 3, 6)
                if front:
                    front_block(2)
                seg(3)
                outputs(2)
                b_dot_c(3)
                if not first(i, k):
                    out_proj(c - 1, 6, 8)
                if front:
                    front_block(3)
                    front_block(4)
                eng.wait_ge(s["h_done"], c + 1)
                if front and u == 0:
                    dt_proj(gf, 1 - par)
                if pre:
                    row_transposes(gf + 1, par, 0)
                outputs(3)
                if front:
                    front_block(5)
                if pre:
                    eng.wait_ge(s["hT_done"], gf * 2 + 3)
                    row_transposes(gf + 1, par, 1)
                if front and u == 0:
                    eng.wait_ge(s["dt_v"], gf + 1)
                if u == 0 or last_chunk(i, k):
                    states()
                if not last_chunk(i, k):
                    z_rows(i, k + 1, 0, front)
                    if pre:
                        eng.wait_ge(s["hT_done"], gf * 2 + 4)
                    if u == 1:
                        states()
                    z_rows(i, k + 1, 1, front)
                    eng.wait_ge(s["carry_done"], c + 2)
                    xb_rows(i, k + 1)

            slots(slot, eng)
            eng.wait_ge(s["carry_done"], TILES + 1)
            for j in range(2):
                if j:
                    eng.wait_ge(s["yT_done"], TILES * 2 - 1)
                turn_gated(TILES - 1, j)
            out_proj(TILES - 1, 0, DI // P)


def constants(nc, ident, ones):
    with nc.semaphore("ident_step") as step, nc.Block() as block:
        @block.gpsimd
        def _(eng):
            eng.memset(ones[:, :], 1.0)
            eng.memset(ident[:, :], 0.0).then_inc(step, 1)
            eng.wait_ge(step, 1)
            eng.affine_select(out=ident[:, :], in_=ident[:, :], compare_op=ALU.not_equal, fill=1.0, base=0,
                              pattern=[[-1, P]], channel_multiplier=1)


def feed_forward(nc, ins, dr, ident, acc, mv):
    NB, NI, RG = FF // FB, FB // P, 512
    NR = ROWS // RG
    TPR = RG // P
    with ExitStack() as ctx:
        def sb(name, shape, dt=F32):
            return ctx.enter_context(nc.sbuf_tensor(name, shape, dt))

        blank = sb("blank", [P, SD])
        bn = sb("ff_bn", [P, TPR, 6])
        hT_hi = sb("ff_hT_hi", [P, KD, ROWS], F32R)
        hT_lo = sb("ff_hT_lo", [P, KD, ROWS], F32R)
        stage = [sb(f"ff_stage{i}", [P, KD * FB]) for i in range(3)]
        w_hi = [[sb(f"ff_w_hi{i}{j}", [P, KD * FB], F32R) for j in range(3)] for i in range(2)]
        w_lo = [[sb(f"ff_w_lo{i}{j}", [P, KD * FB], F32R) for j in range(3)] for i in range(2)]
        prod = [sb(f"ff_prod{i}", [P, RG]) for i in range(2)]
        p_hi = [sb(f"ff_p_hi{i}", [P, NI, RG], F32R) for i in range(2)]
        p_lo = [sb(f"ff_p_lo{i}", [P, NI, RG], F32R) for i in range(2)]
        bank = [ctx.enter_context(nc.psum_tensor(f"ff_bank{i}", [P, 512], F32)) for i in range(8)]
        gate_ps, up_ps, down_ps = bank[0:2], bank[2:4], bank[4:8]
        assert NI * D == KD * FB and TPR == 4
        s = {n: ctx.enter_context(nc.semaphore("ff_" + n)) for n in (
            "blanked", "cleared", "acc_dma", "rows_dma0", "rows_dma1", "rows_dma2", "rows_dma3", "rowT", "hT_hi", "hT_lo", "w_dma0", "w_dma1", "w_dma2", "w_hi", "w_lo",
            "gate_ps", "up_ps", "silu", "prod", "p_hi", "p_lo", "down", "add",
            "bn", "stat")}
        CR = 2 * TPR
        rows_dma = [s[f"rows_dma{i}"] for i in range(NR)]
        w_dma = [s["w_dma0"], s["w_dma1"], s["w_dma2"]]
        block = ctx.enter_context(nc.Block())

        def as_in(t):
            return t[:, :].rearrange("p (k n) -> p k n", k=KD)

        def as_down(t):
            return t[:, :].rearrange("p (c n) -> p c n", c=NI)

        @block.sync
        def _(eng):
            def load_piece(b, j):
                if j < 2:
                    src = ins["L0_attn_gate_w" if j == 0 else "L0_attn_up_w"].rearrange("(k p) n -> p k n", p=P)
                    eng.dma_start(as_in(stage[j]), src[:, :, bass.ds(b * FB, FB)]).then_inc(w_dma[j], 16)
                else:
                    src = ins["L0_attn_down_w"][bass.ds(b * FB, FB), :].rearrange("(c p) n -> p c n", p=P)
                    eng.dma_start(as_down(stage[j]), src).then_inc(w_dma[j], 16)

            def load_rows(r):
                eng.dma_start(acc[:, r * TPR:(r + 1) * TPR, :],
                              dr["h2"][r * RG:(r + 1) * RG, :].rearrange("(t p) n -> p t n", p=P))\
                   .then_inc(rows_dma[r], 16)

            load_rows(0)
            for j in range(3):
                load_piece(0, j)
            for r in range(1, NR):
                load_rows(r)
            eng.wait_ge(s["rowT"], TILES)
            eng.dma_start(acc[:, :, :], dr["xh"].rearrange("(t p) n -> p t n", p=P)).then_inc(s["acc_dma"], 16)
            eng.wait_ge(s["blanked"], 2)
            eng.dma_start(dr["sorted"].rearrange("(t p) n -> p t n", p=P),
                          blank[:, :].unsqueeze(1).broadcast_to([P, SORT_TILES, SD])).then_inc(s["cleared"], 16)
            with eng.Fori(1, NB) as b:
                for j in range(3):
                    eng.wait_ge(s["w_lo"], b * 3 + j - 2)
                    load_piece(b, j)
            eng.wait_ge(s["cleared"], 16)

        @block.gpsimd
        def _(eng):
            for name, n in (("silu", 2), ("prod", 2), ("p_lo", 2), ("down", CR), ("add", TPR), ("hT_lo", TPR)):
                eng.sem_inc(s[name], n)
            eng.memset(blank[:, 0:D + 1], 0.0).then_inc(s["blanked"], 1)
            eng.iota(blank[:, D + 1:SD].bitcast(mybir.dt.int32), pattern=[[1, 1]], base=2 * ROWS,
                     channel_multiplier=0).then_inc(s["blanked"], 1)

            def low_parts(b, par):
                for j in range(3):
                    eng.wait_ge(w_dma[j], (b + 1) * 16)
                    eng.wait_ge(s["w_hi"], b * 3 + j + 1)
                    eng.tensor_tensor(w_lo[par][j][:, :], stage[j][:, :], w_hi[par][j][:, :].bitcast(F32),
                                      ALU.subtract).then_inc(s["w_lo"], 1)

            with eng.Fori(0, NB // 2) as i:
                for par in range(2):
                    low_parts(i * 2 + par, par)


        def steps(body, eng):
            with eng.Fori(0, NB // 2 - 1) as i:
                for k in range(2 * NR):
                    body(i * 2 + k // NR, k)
            for k in range(2 * NR):
                body(NB - 2 + k // NR, k)

        def following(width, b, k):
            if not (isinstance(b, int) and b * NR + k % NR == NB * NR - 1):
                width(b + (k + 1) // NR - k // NR, (k + 1) % (2 * NR))

        @block.scalar
        def _(eng):
            for r in range(NR):
                for v in range(TPR):
                    n = r * TPR + v
                    eng.wait_ge(s["rowT"], n + 1)
                    eng.activation(hT_hi[:, :, n * P:(n + 1) * P], bank[v][:, :].rearrange("p (k n) -> p k n", k=KD),
                                   ACT.Copy).then_inc(s["hT_hi"], 1)
                if r < 3:
                    eng.wait_ge(w_dma[r], 16)
                    eng.activation(w_hi[0][r][:, :], stage[r][:, :], ACT.Copy).then_inc(s["w_hi"], 1)

            def width(b, k):
                step = b * NR + k % NR
                for c in range(NI):
                    n = step * NI + c
                    eng.wait_ge(s["gate_ps"], n + 1)
                    eng.wait_ge(s["p_lo"], n + 1)
                    eng.activation(prod[c][:, :], gate_ps[c][:, :], ACT.Silu).then_inc(s["silu"], 1)
                    eng.wait_ge(s["prod"], n + 3)
                    eng.wait_ge(s["down"], step * TPR + TPR)
                    eng.activation(p_hi[k % 2][:, c, :], prod[c][:, :], ACT.Copy).then_inc(s["p_hi"], 1)

            width(0, 0)

            def body(b, k):
                if k % NR and not (isinstance(b, int) and b == NB - 1):
                    j = k % NR - 1
                    eng.wait_ge(w_dma[j], b * 16 + 32)
                    eng.wait_ge(s["down"], b * NR * TPR + CR)
                    eng.activation(w_hi[(k // NR + 1) % 2][j][:, :], stage[j][:, :], ACT.Copy)\
                       .then_inc(s["w_hi"], 1)
                following(width, b, k)

            steps(body, eng)

        @block.vector
        def _(eng):
            with eng.Fori(0, NR) as i:
                for v in range(TPR):
                    eng.wait_ge(s["hT_hi"], i * TPR + v + 1)
                    cols = bass.ds((i * TPR + v) * P, P)
                    eng.tensor_tensor(hT_lo[:, :, cols], bank[v][:, :].rearrange("p (k n) -> p k n", k=KD),
                                      hT_hi[:, :, cols].bitcast(F32), ALU.subtract).then_inc(s["hT_lo"], 1)

            def width(b, k):
                for c in range(NI):
                    n = (b * NR + k % NR) * NI + c
                    eng.wait_ge(s["silu"], n + 3)
                    eng.wait_ge(s["up_ps"], n + 1)
                    eng.tensor_tensor(prod[c][:, :], prod[c][:, :], up_ps[c][:, :], ALU.mult).then_inc(s["prod"], 1)
                    eng.wait_ge(s["prod"], n + 3)
                    eng.wait_ge(s["p_hi"], n + 1)
                    eng.tensor_tensor(p_lo[k % 2][:, c, :], prod[c][:, :], p_hi[k % 2][:, c, :].bitcast(F32),
                                      ALU.subtract).then_inc(s["p_lo"], 1)

            width(0, 0)
            eng.wait_ge(s["acc_dma"], 16)

            def body(b, k):
                following(width, b, k)
                for t in range(TPR):
                    eng.wait_ge(s["down"], (b * NR + k % NR) * TPR + t + 1 + CR)
                    row = acc[:, (k % NR) * TPR + t, :]
                    eng.tensor_tensor(row, down_ps[t][:, :], row, ALU.add).then_inc(s["add"], 1)
                if isinstance(b, int) and b == NB - 1:
                    r = k % NR
                    eng.wait_ge(s["add"], (b * NR + r + 2) * TPR)
                    if r:
                        eng.wait_ge(s["stat"], r * TPR)
                    for t in range(TPR):
                        eng.bn_stats(bn[:, t, :], acc[:, r * TPR + t, :]).then_inc(s["bn"], 1)
                    for t in range(TPR):
                        eng.wait_ge(s["bn"], r * TPR + t + 1)
                        eng.bn_aggr(mv[:, r * TPR + t, :], bn[:, t, :]).then_inc(s["stat"], 1)

            steps(body, eng)

        @block.tensor
        def _(eng):
            for r in range(NR):
                eng.wait_ge(rows_dma[r], 16)
                for v in range(TPR):
                    n = r * TPR + v
                    eng.wait_ge(s["hT_lo"], n + 1)
                    for k in range(KD):
                        last = eng.transpose(bank[v][:, k * P:(k + 1) * P], acc[:, n, k * P:(k + 1) * P], ident[:, :])
                    last.then_inc(s["rowT"], 1)
            eng.wait_ge(s["hT_lo"], TILES + TPR)

            def three(ps, w, x, first, last):
                for i, (a, b) in enumerate(((0, 0), (0, 1), (1, 0))):
                    mm = eng.matmul(ps, w[a], x[b], start=first and i == 0, stop=last and i == 2)
                return mm

            def width(b, k):
                par, r = k // NR % 2, k % NR
                if r == 0:
                    eng.wait_ge(s["w_lo"], b * 3 + 3)
                cols = slice(r * RG, (r + 1) * RG)
                for c in range(NI):
                    n = (b * NR + r) * NI + c
                    for j, ps, free, done in ((0, gate_ps[c], "silu", "gate_ps"), (1, up_ps[c], "prod", "up_ps")):
                        eng.wait_ge(s[free], n + 1)
                        for q in range(KD):
                            w = [as_in(t[par][j])[:, q, c * P:(c + 1) * P] for t in (w_hi, w_lo)]
                            x = [t[:, q, cols] for t in (hT_hi, hT_lo)]
                            mm = three(ps[:, :], w, x, q == 0, q == KD - 1)
                        mm.then_inc(s[done], 1)

            def out(b, k):
                par, step = k // NR % 2, b * NR + k % NR
                eng.wait_ge(s["p_lo"], step * NI + NI + 2)
                for t in range(TPR):
                    eng.wait_ge(s["add"], step * TPR + t + 1)
                    for c in range(NI):
                        x = [v[k % 2][:, c, t * P:(t + 1) * P] for v in (p_hi, p_lo)]
                        w = [as_down(v[par][2])[:, c, :] for v in (w_hi, w_lo)]
                        mm = three(down_ps[t][:, :], x, w, c == 0, c == NI - 1)
                    mm.then_inc(s["down"], 1)

            width(0, 0)

            def body(b, k):
                following(width, b, k)
                out(b, k)

            steps(body, eng)


def experts(nc, ins, dr, out_d, ident, ones, acc, mv):
    with ExitStack() as ctx:
        def sb(name, shape, dt=F32, where=ctx):
            return where.enter_context(nc.sbuf_tensor(name, shape, dt))

        def sem(name):
            return ctx.enter_context(nc.semaphore("moe_" + name))

        w_gu = sb("w_gu", [P, 2, E * KD, EI])
        w_dn = sb("w_dn", [P, E * len(IC), D])
        rstd = sb("moe_rstd", [P, TILES])
        tile_expert = sb("tile_expert", [1, SORT_TILES], mybir.dt.int32)
        s_w = sem("w_dma")
        NW = 2 * E + 2 * E

        with ExitStack() as rctx:
            xm = [sb(f"xm{i}", [P, SD], where=rctx) for i in range(4)]
            xmT = [sb(f"xmT{i}", [P, KD, 4 * P], where=rctx) for i in range(2)]
            logits_T = [sb(f"logits_T{i}", [E, 4 * P], where=rctx) for i in range(2)]
            wr = sb("wr", [P, KD, E], where=rctx)
            half_neg = sb("moe_half_neg", [P, TILES], where=rctx)
            strict = sb("strict", [P, P], where=rctx)
            row_no = sb("row_no", [P, TILES], mybir.dt.int32, where=rctx)
            iota_e = sb("iota_e", [P, E], mybir.dt.int32, where=rctx)
            iota_t = sb("iota_t", [P, SORT_TILES + 1], mybir.dt.int32, where=rctx)
            ef = sb("ef", [P, E], where=rctx)
            tf = sb("tf", [P, SORT_TILES + 1], where=rctx)
            t3 = lambda name: sb(name, [P, TILES, E], where=rctx)
            prob, top, hot0, hot1, hot, run_a, run_b, place = map(
                t3, ("prob", "top", "hot0", "hot1", "hot", "run_a", "run_b", "place"))
            weight = sb("moe_weight", [P, 2, TILES], where=rctx)
            idx = sb("idx", [P, TILES, E], U32, where=rctx)
            idx_f = sb("idx_f", [P, TILES, 2], where=rctx)
            red = sb("red", [P, 4, TILES], where=rctx)
            cmp_n = sb("cmp_n", [P, E, TILES], where=rctx)
            ends = sb("ends", [P, 4, E], where=rctx)
            cmp_t = sb("cmp_t", [P, SORT_TILES, E], where=rctx)
            slot = sb("moe_slot", [P, 2 * TILES], U32, where=rctx)
            slot_f = sb("slot_f", [P, 2 * TILES], where=rctx)
            te_f = sb("te_f", [P, SORT_TILES], where=rctx)
            bank = [rctx.enter_context(nc.psum_tensor(f"rt_bank{i}", [P, 512], F32)) for i in range(6)]
            s = {n: rctx.enter_context(nc.semaphore("rt_" + n)) for n in (
                "wr_dma", "const", "rstd", "xm", "rowT", "xmT", "logits", "logits_sb", "logits_row", "route", "exp", "counts",
                "again", "scat0", "scat1", "scat2", "scat3", "out_dma")}
            scat = [s[f"scat{i}"] for i in range(4)]
            HOT = 5 + 2 * TILES + 8
            block = rctx.enter_context(nc.Block())

            @block.sync
            def _(eng):
                eng.dma_start(wr[:, :, :], ins["L0_ffn_Wr"].rearrange("(k p) e -> p k e", p=P)).then_inc(s["wr_dma"], 16)
                for e in range(E):
                    for j, name in enumerate(("L0_ffn_Wg", "L0_ffn_Wu")):
                        eng.dma_start(w_gu[:, j, e * KD:(e + 1) * KD, :],
                                      ins[name][e].rearrange("(k p) i -> p k i", p=P)).then_inc(s_w, 16)
                    n, full = len(IC), EI // P
                    src = ins["L0_ffn_Wd"][e]
                    eng.dma_start(w_dn[:, e * n:e * n + full, :],
                                  src[0:full * P, :].rearrange("(c p) n -> p c n", p=P)).then_inc(s_w, 16)
                    eng.dma_start(w_dn[0:EI - full * P, e * n + full, :], src[full * P:EI, :]).then_inc(s_w, 16)
                eng.dma_start(out_d.rearrange("(t p) n -> p t n", p=P), acc[:, :, :]).then_inc(s["out_dma"], 16)
                eng.wait_ge(s["wr_dma"], 16)
                eng.wait_ge(s["out_dma"], 16)

            @block.gpsimd
            def _(eng):
                eng.sem_inc(s["xmT"], 2)
                eng.memset(half_neg[:, :], -0.5).then_inc(s["const"], 1)
                eng.memset(strict[:, :], 1.0).then_inc(s["const"], 1)
                eng.iota(iota_e[:, :], pattern=[[1, E]], base=0, channel_multiplier=0).then_inc(s["const"], 1)
                eng.iota(iota_t[:, :], pattern=[[1, SORT_TILES + 1]], base=0, channel_multiplier=0)\
                   .then_inc(s["const"], 1)
                eng.iota(row_no[:, :], pattern=[[P, TILES]], base=0, channel_multiplier=1).then_inc(s["const"], 1)
                eng.wait_ge(s["const"], 5)
                eng.affine_select(out=strict[:, :], in_=strict[:, :], compare_op=ALU.is_gt, fill=0.0, base=0,
                                  pattern=[[1, P]], channel_multiplier=-1).then_inc(s["const"], 1)
                eng.tensor_scalar(rstd[:, :], mv[:, :, 1], EPS, None, ALU.add).then_inc(s["rstd"], 1)
                eng.wait_ge(s["rstd"], 1)
                eng.tensor_tensor(rstd[:, :], rstd[:, :], half_neg[:, :], ALU.pow).then_inc(s["rstd"], 1)
                for n in range(2 * TILES):
                    i, k = n // 2, n % 2
                    eng.wait_ge(s["again"], 3 * n + 3)
                    eng.indirect_dma_start(out=dr["sorted"][:, :],
                                           out_offset=bass.IndirectOffsetOnAxis(
                                               ap=slot[:, k * TILES + i:k * TILES + i + 1], axis=0),
                                           in_=xm[n % 4][:, :], in_offset=None).then_inc(scat[n % 4], 16)
                for i in range(4):
                    eng.wait_ge(scat[i], 16 * (2 * TILES // 4))

            @block.scalar
            def _(eng):
                def logits_out(g):
                    eng.wait_ge(s["logits"], g + 1)
                    if g >= 2:
                        eng.wait_ge(s["logits_row"], g - 1)
                    eng.activation(logits_T[g % 2][:, :], bank[4 + g % 2][0:E, :], ACT.Copy).then_inc(s["logits_sb"], 1)

                for t in range(TILES):
                    g, i = t // 4, t % 4
                    eng.wait_ge(s["rowT"], t + 1)
                    if g >= 2:
                        eng.wait_ge(s["logits"], g - 1)
                    eng.activation(xmT[g % 2][:, :, i * P:(i + 1) * P],
                                   bank[t % 2][:, :].rearrange("p (k n) -> p k n", k=KD), ACT.Copy)\
                       .then_inc(s["xmT"], 1)
                    if t >= 6 and i == 2:
                        logits_out(g - 1)
                logits_out(TILES // 4 - 1)
                eng.wait_ge(s["route"], 2)
                eng.activation(prob[:, :, :], prob[:, :, :], ACT.Exp).then_inc(s["exp"], 1)

            @block.tensor
            def _(eng):
                eng.wait_ge(s["wr_dma"], 16)
                def logits(g):
                    eng.wait_ge(s["xmT"], 4 * g + 6)
                    if g >= 2:
                        eng.wait_ge(s["logits_sb"], g - 1)
                    for k in range(KD):
                        last = eng.matmul(bank[4 + g % 2][0:E, :], wr[:, k, :], xmT[g % 2][:, k, :],
                                          start=(k == 0), stop=(k == KD - 1))
                    last.then_inc(s["logits"], 1)

                def logit_rows(g):
                    eng.wait_ge(s["logits_sb"], g + 1)
                    for i in range(4):
                        t = 4 * g + i
                        last = eng.transpose(bank[2][:, t * E:(t + 1) * E], logits_T[g % 2][:, i * P:(i + 1) * P],
                                             ident[0:E, 0:E])
                    last.then_inc(s["logits_row"], 1)

                for t in range(TILES):
                    eng.wait_ge(s["xm"], t + 1)
                    eng.wait_ge(s["xmT"], t + 1)
                    for k in range(KD):
                        last = eng.transpose(bank[t % 2][:, k * P:(k + 1) * P], xm[t % 4][:, k * P:(k + 1) * P],
                                             ident[:, :])
                    last.then_inc(s["rowT"], 1)
                    if t >= 4 and t % 4 == 1:
                        logits(t // 4 - 1)
                        if t >= 8:
                            logit_rows(t // 4 - 2)
                logits(TILES // 4 - 1)
                for g in (TILES // 4 - 2, TILES // 4 - 1):
                    logit_rows(g)
                eng.wait_ge(s["const"], 6)
                eng.wait_ge(s["route"], HOT)
                flat = hot[:, :, :].rearrange("p t e -> p (t e)")
                eng.matmul(bank[3][:, 0:P], strict[:, :], flat, start=True, stop=True)
                eng.matmul(bank[3][:, P:2 * P], ones[:, :], flat, start=True, stop=True).then_inc(s["counts"], 1)

            @block.vector
            def _(eng):
                done = [0]

                def step(instruction, wait=True):
                    instruction.then_inc(s["route"], 1)
                    done[0] += 1
                    if wait:
                        eng.wait_ge(s["route"], done[0])

                def per_tile(a):
                    return a.unsqueeze(2).broadcast_to([P, TILES, E])

                def normed(t, v):
                    return eng.tensor_scalar(xm[v][:, 0:D], acc[:, t, :], mv[:, t, 0:1], rstd[:, t:t + 1],
                                             ALU.subtract, ALU.mult)

                eng.wait_ge(s["rstd"], 2)
                for t in range(TILES):
                    if t >= 4:
                        eng.wait_ge(s["rowT"], t - 3)
                    normed(t, t % 4).then_inc(s["xm"], 1)
                eng.wait_ge(s["logits_row"], TILES // 4)
                logits = bank[2][:, 0:TILES * E].rearrange("p (t e) -> p t e", e=E)
                step(eng.tensor_reduce(red[:, 0, :], logits, AX_X, ALU.max))
                step(eng.tensor_tensor(prob[:, :, :], logits, per_tile(red[:, 0, :]), ALU.subtract))
                eng.wait_ge(s["exp"], 1)
                step(eng.tensor_reduce(red[:, 1, :], prob[:, :, :], AX_X, ALU.add))
                step(eng.reciprocal(red[:, 2, :], red[:, 1, :]))
                step(eng.tensor_tensor(prob[:, :, :], prob[:, :, :], per_tile(red[:, 2, :]), ALU.mult))
                for t in range(TILES):
                    step(eng.max(top[:, t, :], prob[:, t, :]), wait=t == TILES - 1)
                for t in range(TILES):
                    step(eng.max_index(idx[:, t, :], top[:, t, :], prob[:, t, :]), wait=False)
                eng.wait_ge(s["const"], 6)
                step(eng.tensor_copy(ef[:, :], iota_e[:, :]), wait=False)
                step(eng.tensor_copy(tf[:, :], iota_t[:, :]))
                step(eng.tensor_copy(idx_f[:, :, :], idx[:, :, 0:2]))
                e_of = ef[:, :].unsqueeze(1).broadcast_to([P, TILES, E])
                for k, h in enumerate((hot0, hot1)):
                    step(eng.tensor_tensor(h[:, :, :], e_of, per_tile(idx_f[:, :, k]), ALU.is_equal))
                step(eng.tensor_tensor(hot[:, :, :], hot0[:, :, :], hot1[:, :, :], ALU.add))
                step(eng.tensor_tensor(red[:, 0, :], top[:, :, 0], top[:, :, 1], ALU.add))
                step(eng.reciprocal(red[:, 3, :], red[:, 0, :]))
                assert done[0] == HOT
                for k in range(2):
                    step(eng.tensor_tensor(weight[:, k, :], top[:, :, k], red[:, 3, :], ALU.mult))
                eng.wait_ge(s["counts"], 1)
                before = bank[3][:, 0:P].rearrange("p (t e) -> p t e", e=E)
                total = bank[3][:, P:2 * P].rearrange("p (t e) -> p t e", e=E)
                step(eng.tensor_copy(run_a[:, :, :], total))
                a, b = run_a, run_b
                sh = 1
                while sh < TILES:
                    step(eng.tensor_copy(b[:, 0:sh, :], a[:, 0:sh, :]))
                    step(eng.tensor_tensor(b[:, sh:TILES, :], a[:, sh:TILES, :], a[:, 0:TILES - sh, :], ALU.add))
                    a, b, sh = b, a, 2 * sh
                step(eng.tensor_scalar(tf[:, :], tf[:, :], float(P), None, ALU.mult))
                step(eng.tensor_tensor(cmp_n[:, :, :], a[:, TILES - 1, :].unsqueeze(2).broadcast_to([P, E, TILES]),
                                       tf[:, 0:TILES].unsqueeze(1).broadcast_to([P, E, TILES]), ALU.is_gt))
                step(eng.tensor_reduce(ends[:, 0, :], cmp_n[:, :, :], AX_X, ALU.add))
                step(eng.tensor_scalar(ends[:, 1, :], ends[:, 0, :], float(P), None, ALU.mult))
                step(eng.tensor_copy(ends[:, 3, :], ends[:, 1, :]))
                x, y, sh = 1, 2, 1
                while sh < E:
                    step(eng.tensor_copy(ends[:, y, 0:sh], ends[:, x, 0:sh]))
                    step(eng.tensor_tensor(ends[:, y, sh:E], ends[:, x, sh:E], ends[:, x, 0:E - sh], ALU.add))
                    x, y, sh = y, x, 2 * sh
                step(eng.tensor_tensor(ends[:, y, :], ends[:, x, :], ends[:, 3, :], ALU.subtract))
                step(eng.tensor_tensor(place[:, :, :], a[:, :, :], total, ALU.subtract))
                step(eng.tensor_tensor(place[:, :, :], place[:, :, :], before, ALU.add))
                step(eng.tensor_tensor(place[:, :, :], place[:, :, :],
                                       ends[:, y, :].unsqueeze(1).broadcast_to([P, TILES, E]), ALU.add))
                for k, h in enumerate((hot0, hot1)):
                    step(eng.tensor_tensor(h[:, :, :], h[:, :, :], place[:, :, :], ALU.mult))
                    step(eng.tensor_reduce(slot_f[:, k * TILES:(k + 1) * TILES], h[:, :, :], AX_X, ALU.add))
                step(eng.tensor_copy(slot[:, :], slot_f[:, :]))
                for n in range(2 * TILES):
                    i, k = n // 2, n % 2
                    if n >= 4:
                        eng.wait_ge(scat[n % 4], 16 * (n // 4))
                    normed(i, n % 4).then_inc(s["again"], 1)
                    eng.tensor_copy(xm[n % 4][:, D:D + 1], weight[:, k, i:i + 1]).then_inc(s["again"], 1)
                    eng.tensor_copy(xm[n % 4][:, D + 1:SD].bitcast(mybir.dt.int32), row_no[:, i:i + 1])\
                       .then_inc(s["again"], 1)
                step(eng.tensor_tensor(cmp_t[:, :, :], ends[:, x, :].unsqueeze(1).broadcast_to([P, SORT_TILES, E]),
                                       tf[:, 0:SORT_TILES].unsqueeze(2).broadcast_to([P, SORT_TILES, E]), ALU.is_le))
                step(eng.tensor_reduce(te_f[:, :], cmp_t[:, :, :], AX_X, ALU.add))
                step(eng.tensor_scalar(te_f[:, :], te_f[:, :], float(E - 1), None, ALU.min))
                step(eng.tensor_copy(tile_expert[:, :], te_f[0:1, :]))

        with ExitStack() as ectx:
            NI, UN = len(IC), 4
            xs = [sb(f"xs{i}", [P, SD], where=ectx) for i in range(UN)]
            xT = [sb(f"xT{i}", [P, KD, P], where=ectx) for i in range(2)]
            act_g = [sb(f"act_g{i}", [P, EI], where=ectx) for i in range(2)]
            hT = [sb(f"moe_hT{i}", [P, NI, P], where=ectx) for i in range(2)]
            rows = sb("result_rows", [P, D], where=ectx)
            bank = [ectx.enter_context(nc.psum_tensor(f"ex_bank{i}", [P, 512], F32)) for i in range(8)]
            xT_ps, gate_ps, up_ps, hT_ps, y_ps = bank[0], bank[1:3], bank[3:5], bank[5], bank[6:8]
            s = {n: ectx.enter_context(nc.semaphore("ex_" + n)) for n in (
                "xs0", "xs1", "xs2", "xs3", "xT_ps", "xT", "gate_ps", "up_ps", "silu", "h", "hT_ps", "hT", "y_ps",
                "cleared", "got", "sum", "put", "through", "passed")}
            xs_s = [s[f"xs{i}"] for i in range(UN)]
            block = ectx.enter_context(nc.Block())

            def ahead(body, eng):
                n = (SORT_TILES - 3) // UN
                with eng.Fori(0, n) as i:
                    for v in range(UN):
                        body(i * UN + v, v)
                for j in range(UN * n, SORT_TILES):
                    body(j, j % UN)

            def beyond(j, n):
                return isinstance(j, int) and j + n >= SORT_TILES

            @block.sync
            def _(eng):
                def load(j, v):
                    eng.dma_start(xs[v][:, :], dr["sorted"][bass.ds(j * P, P), :]).then_inc(xs_s[v], 16)

                def body(j, v):
                    if not beyond(j, 2):
                        eng.wait_ge(s["through"], j + 1)
                        load(j + 2, (v + 2) % UN)

                load(0, 0)
                load(1, 1)
                ahead(body, eng)

            @block.gpsimd
            def _(eng):
                for name, n in (("xT_ps", 2), ("xT", 1), ("silu", 2), ("h", 2), ("gate_ps", 2), ("hT_ps", 2),
                                ("hT", 1), ("y_ps", 2), ("sum", 2), ("through", 2)):
                    eng.sem_inc(s[name], n)
                eng.memset(rows[:, :], 0.0).then_inc(s["cleared"], 1)
                eng.wait_ge(s["cleared"], 1)

                def body(j, v):
                    number = bass.IndirectOffsetOnAxis(ap=xs[v][:, D + 1:SD].bitcast(U32), axis=0)
                    eng.wait_ge(xs_s[v], (j - v) * 4 + 16)
                    eng.sem_inc(s["passed"], 1)
                    eng.indirect_dma_start(out=rows[:, :], out_offset=None, in_=out_d, in_offset=number,
                                           bounds_check=ROWS - 1, oob_is_err=False).then_inc(s["got"], 16)
                    eng.wait_ge(s["sum"], j + 3)
                    eng.sem_inc(s["passed"], 1)
                    eng.indirect_dma_start(out=out_d, out_offset=number, in_=rows[:, :], in_offset=None,
                                           bounds_check=ROWS - 1, oob_is_err=False).then_inc(s["put"], 16)
                    eng.wait_ge(s["put"], j * 16 + 16)
                    eng.sem_inc(s["through"], 1)

                ahead(body, eng)

            @block.scalar
            def _(eng):
                def turned(j, v):
                    eng.wait_ge(s["xT_ps"], j + 3)
                    eng.wait_ge(s["gate_ps"], j + 1)
                    eng.activation(xT[v % 2][:, :, :].rearrange("p k n -> p (k n)"), xT_ps[:, :], ACT.Copy)\
                       .then_inc(s["xT"], 1)

                def gate(j, v):
                    eng.wait_ge(s["gate_ps"], j + 3)
                    eng.wait_ge(s["hT_ps"], j + 1)
                    eng.activation(act_g[v % 2][:, :], gate_ps[v % 2][:, 0:EI], ACT.Silu).then_inc(s["silu"], 1)

                turned(0, 0)
                gate(0, 0)
                turned(1, 1)

                def body(j, v):
                    if not beyond(j, 1):
                        gate(j + 1, v + 1)
                    if not beyond(j, 2):
                        turned(j + 2, v)

                ahead(body, eng)

            @block.vector
            def _(eng):
                def product(j, v):
                    eng.wait_ge(s["silu"], j + 3)
                    eng.wait_ge(s["up_ps"], j + 1)
                    eng.tensor_tensor(act_g[v % 2][:, :], act_g[v % 2][:, :], up_ps[v % 2][:, 0:EI], ALU.mult)\
                       .then_inc(s["h"], 1)

                def turned(j, v):
                    eng.wait_ge(s["hT_ps"], j + 3)
                    eng.wait_ge(s["y_ps"], j + 1)
                    full = EI // P
                    eng.tensor_copy(hT[v % 2][:, 0:full, :].rearrange("p c n -> p (c n)"), hT_ps[:, 0:full * P])
                    n = EI - full * P
                    eng.tensor_copy(hT[v % 2][0:n, full, :], hT_ps[0:n, full * P:(full + 1) * P]).then_inc(s["hT"], 1)

                def weighted(j, v):
                    eng.wait_ge(s["y_ps"], j + 3)
                    eng.wait_ge(s["got"], j * 16 + 16)
                    eng.scalar_tensor_tensor(rows[:, :], y_ps[v % 2][:, :], xs[v][:, D:D + 1], rows[:, :],
                                             ALU.mult, ALU.add).then_inc(s["sum"], 1)

                product(0, 0)

                def body(j, v):
                    turned(j, v)
                    if not beyond(j, 1):
                        product(j + 1, v + 1)
                    weighted(j, v)

                ahead(body, eng)

            @block.tensor
            def _(eng):
                eng.wait_ge(s_w, 16 * NW)

                def turn_rows(j, v):
                    eng.wait_ge(xs_s[v], (j - v) * 4 + 16)
                    eng.wait_ge(s["xT"], j + 1)
                    for k in range(KD):
                        last = eng.transpose(xT_ps[:, k * P:(k + 1) * P], xs[v][:, k * P:(k + 1) * P], ident[:, :])
                    last.then_inc(s["xT_ps"], 1)

                def width(j, v):
                    e = eng.value_load(tile_expert[0:1, bass.ds(j, 1)], min_val=0, max_val=E - 1)
                    eng.wait_ge(s["xT"], j + 2)
                    for i, (ps, free, done) in enumerate(((gate_ps[v % 2], "silu", "gate_ps"), (up_ps[v % 2], "h", "up_ps"))):
                        eng.wait_ge(s[free], j + 1)
                        for k in range(KD):
                            mm = eng.matmul(ps[:, 0:EI], xT[v % 2][:, k, :],
                                            w_gu[:, i, bass.ds(e * KD + k, 1), :].rearrange("p a n -> p (a n)"),
                                            start=(k == 0), stop=(k == KD - 1))
                        mm.then_inc(s[done], 1)
                    return e

                def turn_width(j, v):
                    eng.wait_ge(s["h"], j + 3)
                    eng.wait_ge(s["hT"], j + 1)
                    for c, (i, n) in enumerate(IC):
                        last = eng.transpose(hT_ps[0:n, c * P:(c + 1) * P], act_g[v % 2][:, i:i + n], ident[:, :])
                    last.then_inc(s["hT_ps"], 1)

                def out(j, v):
                    e = eng.value_load(tile_expert[0:1, bass.ds(j, 1)], min_val=0, max_val=E - 1)
                    eng.wait_ge(s["hT"], j + 2)
                    eng.wait_ge(s["sum"], j + 1)
                    for c, (i, n) in enumerate(IC):
                        mm = eng.matmul(y_ps[v % 2][:, :], hT[v % 2][0:n, c, :],
                                        w_dn[0:n, bass.ds(e * NI + c, 1), :].rearrange("p a n -> p (a n)"),
                                        start=(c == 0), stop=(c == NI - 1))
                    mm.then_inc(s["y_ps"], 1)

                turn_rows(0, 0)
                width(0, 0)
                turn_rows(1, 1)

                def body(j, v):
                    turn_width(j, v)
                    if not beyond(j, 1):
                        width(j + 1, v + 1)
                    if not beyond(j, 2):
                        turn_rows(j + 2, (v + 2) % UN)
                    out(j, v)

                ahead(body, eng)


def mixer_ffn_experts_kernel(nc, ins, out):
    out_d = out.rearrange("b s d -> (b s) d")
    dr = {name: nc.dram_tensor(name + "_rows", shape, F32, kind="Internal").ap()
          for name, shape in (("xh", (ROWS, D)), ("h2", (ROWS, D)), ("sorted", (SORT_TILES * P, SD)))}
    with nc.sbuf_tensor("ident", [P, P], F32) as ident, nc.sbuf_tensor("ones", [P, P], F32) as ones:
        constants(nc, ident, ones)
        mixer(nc, ins, dr, ident, ones)
        with nc.sbuf_tensor("acc_rows", [P, TILES, D], F32) as acc, nc.sbuf_tensor("acc_mv", [P, TILES, 2], F32) as mv:
            feed_forward(nc, ins, dr, ident, acc, mv)
            experts(nc, ins, dr, out_d, ident, ones, acc, mv)


_INS = ["L0_attn_hidden_states", "L0_attn_in_proj_w", "L0_attn_conv_w", "L0_attn_conv_b", "L0_attn_dt_bias",
        "L0_attn_A_log", "L0_attn_D", "L0_attn_norm_w", "L0_attn_out_proj_w", "L0_attn_ln1_w", "L0_attn_ln2_w",
        "L0_attn_gate_w", "L0_attn_up_w", "L0_attn_down_w", "L0_ffn_Wr", "L0_ffn_Wg", "L0_ffn_Wu", "L0_ffn_Wd"]
_OUT = ((1, ROWS, D), "float32")


def kernel(**inputs):
    import numpy as _np
    import concourse.bacc as _bacc
    from concourse import mybir as _mybir
    from concourse.bass_utils import run_bass_kernel_spmd as _run

    nc = _bacc.Bacc("TRN2", target_bir_lowering=False, num_devices=1)
    arrays, ins = {}, {}
    for name in _INS:
        a = _np.ascontiguousarray(inputs[name])
        arrays[f"in_{name}_dram"] = a
        ins[name] = nc.dram_tensor(f"in_{name}_dram", a.shape, _mybir.dt.from_np(a.dtype), kind="ExternalInput").ap()
    out = nc.dram_tensor("out_0_dram", _OUT[0], _mybir.dt.from_np(_np.dtype(_OUT[1])), kind="ExternalOutput").ap()
    mixer_ffn_experts_kernel(nc, ins, out)
    r = _run(nc, [arrays], core_ids=[0])
    return r.results[0]["out_0_dram"]
```
